# Optimizing a Trainium2 kernel written in Bass

```python
import numpy as np
import jax
import jax.numpy as jnp

def _softmax(x, axis=-1):
    return jax.nn.softmax(x, axis=axis)

def _gelu(x):
    return jax.nn.gelu(x, approximate=True)

def _silu(x):
    return jax.nn.silu(x)

def _sigmoid(x):
    return jax.nn.sigmoid(x)

def _layernorm(x, axis=-1, eps=1e-05):
    m = jnp.mean(x, axis=axis, keepdims=True)
    v = jnp.var(x, axis=axis, keepdims=True)
    return (x - m) / jnp.sqrt(v + eps)

def _scatter_add(tgt, idx, src, axis=0):
    return tgt.at[idx].add(src)

def _segment_sum(src, seg, n):
    return jax.ops.segment_sum(src, seg, n)
kernel_name = 'mk_seq_preln_d1_jaxref_r4_5a07e1'

def setup_inputs(seed: int=0):
    np.random.seed(seed)
    _w = jnp.asarray

    def _L0_attn_setup():
        import jax, jax.numpy as jnp
        import numpy as np
        EPS = 1e-05

        def exp_map_at_origin(v, c):
            sqrt_c = jnp.sqrt(c)
            v_norm = jnp.maximum(jnp.linalg.norm(v, axis=-1, keepdims=True), EPS)
            return 1.0 / sqrt_c * jnp.tanh(sqrt_c * v_norm) * (v / v_norm)

        def log_map_at_origin(y, c):
            sqrt_c = jnp.sqrt(c)
            y_norm = jnp.maximum(jnp.linalg.norm(y, axis=-1, keepdims=True), EPS)
            y_norm_clamped = jnp.minimum(y_norm, 1.0 / sqrt_c - EPS)
            return 1.0 / sqrt_c * jnp.arctanh(sqrt_c * y_norm_clamped) * (y / y_norm)

        def poincare_distance(x, y, c):
            sqrt_c = jnp.sqrt(c)
            xns = jnp.sum(x * x, axis=-1, keepdims=True)
            yns = jnp.sum(y * y, axis=-1, keepdims=True)
            xy = jnp.einsum('bhsd,bhtd->bhst', x, y)
            xnsb = xns
            ynsb = jnp.swapaxes(yns, -2, -1)
            diff_norm_sq = xnsb - 2.0 * xy + ynsb
            denom = jnp.maximum((1.0 - c * xnsb) * (1.0 - c * ynsb), EPS)
            arg = jnp.maximum(1.0 + 2.0 * c * diff_norm_sq / denom, 1.0 + EPS)
            return 1.0 / sqrt_c * jnp.arccosh(arg)
        key = jax.random.key(seed)
        ks = jax.random.split(key, 5)
        B, S, D = (2, 256, 256)
        x = jax.random.normal(ks[0], (B, S, D), dtype=jnp.float32)
        scale = 0.02
        W_q = scale * jax.random.normal(ks[1], (D, D), dtype=jnp.float32)
        W_k = scale * jax.random.normal(ks[2], (D, D), dtype=jnp.float32)
        W_v = scale * jax.random.normal(ks[3], (D, D), dtype=jnp.float32)
        W_o = scale * jax.random.normal(ks[4], (D, D), dtype=jnp.float32)
        return {'x': x, 'W_q': W_q, 'W_k': W_k, 'W_v': W_v, 'W_o': W_o, 'log_c': jnp.zeros((), jnp.float32), 'beta': jnp.zeros((), jnp.float32), 'attention_bias': jnp.zeros((), jnp.float32)}
    _L0_attn_in = _L0_attn_setup()

    def _L0_ffn_setup():
        import jax, jax.numpy as jnp
        import numpy as np
        FEATURES = 256
        D_IN = 256

        def fp8_gemm_optimized(x, input_scale, kernel, kernel_scale):
            s_in = input_scale[0]
            s_k = kernel_scale[0]
            x_q = (x.astype(jnp.float32) / s_in).astype(jnp.float8_e4m3fn)
            k_q = (kernel.astype(jnp.float32) / s_k).astype(jnp.float8_e4m3fn)
            y = jnp.dot(x_q.astype(jnp.float32), k_q.astype(jnp.float32), preferred_element_type=jnp.float32)
            return y * (s_in * s_k)
        key = jax.random.key(seed)
        kx, kk, kb = jax.random.split(key, 3)
        x = jax.random.normal(kx, (4, 2048, D_IN), dtype=jnp.float32)
        limit = np.sqrt(6.0 / (D_IN + FEATURES)).astype(np.float32)
        kernel = jax.random.uniform(kk, (D_IN, FEATURES), dtype=jnp.float32, minval=-limit, maxval=limit).astype(jnp.bfloat16)
        input_scale = jnp.ones((1,), dtype=jnp.float32)
        kernel_scale = jnp.ones((1,), dtype=jnp.float32)
        bias = jnp.zeros((FEATURES,), dtype=jnp.bfloat16)
        return {'x': x, 'kernel': kernel, 'input_scale': input_scale, 'kernel_scale': kernel_scale, 'bias': bias}
    _L0_ffn_in = _L0_ffn_setup()
    _d = {'L0_attn_x': _L0_attn_in['x'], 'L0_attn_W_q': _L0_attn_in['W_q'], 'L0_attn_W_k': _L0_attn_in['W_k'], 'L0_attn_W_v': _L0_attn_in['W_v'], 'L0_attn_W_o': _L0_attn_in['W_o'], 'L0_attn_log_c': _L0_attn_in['log_c'], 'L0_attn_beta': _L0_attn_in['beta'], 'L0_attn_attention_bias': _L0_attn_in['attention_bias'], 'L0_ffn_kernel': _L0_ffn_in['kernel'], 'L0_ffn_input_scale': _L0_ffn_in['input_scale'], 'L0_ffn_kernel_scale': _L0_ffn_in['kernel_scale'], 'L0_ffn_bias': _L0_ffn_in['bias']}
    _x0 = _d['L0_attn_x']
    _d['L0_attn_x'] = jax.random.normal(jax.random.fold_in(jax.random.key(seed), 1), (8, 1024, 256), dtype=_x0.dtype)
    del _x0
    return _d

def reference(L0_attn_x, L0_attn_W_q, L0_attn_W_k, L0_attn_W_v, L0_attn_W_o, L0_attn_log_c, L0_attn_beta, L0_attn_attention_bias, L0_ffn_kernel, L0_ffn_input_scale, L0_ffn_kernel_scale, L0_ffn_bias):

    def _L0_attn_ref(x, W_q, W_k, W_v, W_o, log_c, beta, attention_bias):
        import jax, jax.numpy as jnp
        import numpy as np
        EPS = 1e-05

        def exp_map_at_origin(v, c):
            sqrt_c = jnp.sqrt(c)
            v_norm = jnp.maximum(jnp.linalg.norm(v, axis=-1, keepdims=True), EPS)
            return 1.0 / sqrt_c * jnp.tanh(sqrt_c * v_norm) * (v / v_norm)

        def log_map_at_origin(y, c):
            sqrt_c = jnp.sqrt(c)
            y_norm = jnp.maximum(jnp.linalg.norm(y, axis=-1, keepdims=True), EPS)
            y_norm_clamped = jnp.minimum(y_norm, 1.0 / sqrt_c - EPS)
            return 1.0 / sqrt_c * jnp.arctanh(sqrt_c * y_norm_clamped) * (y / y_norm)

        def poincare_distance(x, y, c):
            sqrt_c = jnp.sqrt(c)
            xns = jnp.sum(x * x, axis=-1, keepdims=True)
            yns = jnp.sum(y * y, axis=-1, keepdims=True)
            xy = jnp.einsum('bhsd,bhtd->bhst', x, y)
            xnsb = xns
            ynsb = jnp.swapaxes(yns, -2, -1)
            diff_norm_sq = xnsb - 2.0 * xy + ynsb
            denom = jnp.maximum((1.0 - c * xnsb) * (1.0 - c * ynsb), EPS)
            arg = jnp.maximum(1.0 + 2.0 * c * diff_norm_sq / denom, 1.0 + EPS)
            return 1.0 / sqrt_c * jnp.arccosh(arg)
        B, S, D = x.shape
        H = 16
        dh = D // H
        c = jax.nn.softplus(log_c)
        beta_pos = jax.nn.softplus(beta)

        def split_heads(t):
            return jnp.transpose(t.reshape(B, S, H, dh), (0, 2, 1, 3))
        q_t = split_heads(x @ W_q.T)
        k_t = split_heads(x @ W_k.T)
        v_t = split_heads(x @ W_v.T)
        q_h = exp_map_at_origin(q_t, c)
        k_h = exp_map_at_origin(k_t, c)
        v_h = exp_map_at_origin(v_t, c)
        dist = poincare_distance(q_h, k_h, c)
        scores = -beta_pos * dist - attention_bias
        weights = jax.nn.softmax(scores, axis=-1)
        v_tan = log_map_at_origin(v_h, c)
        out_tan = jnp.einsum('bhst,bhtd->bhsd', weights, v_tan)
        out_hyp = exp_map_at_origin(out_tan, c)
        out_heads_tan = log_map_at_origin(out_hyp, c)
        concat = jnp.transpose(out_heads_tan, (0, 2, 1, 3)).reshape(B, S, D)
        return concat @ W_o.T

    def _L0_ffn_ref(x, kernel, input_scale, kernel_scale, bias):
        import jax, jax.numpy as jnp
        import numpy as np
        FEATURES = 256
        D_IN = 256

        def fp8_gemm_optimized(x, input_scale, kernel, kernel_scale):
            s_in = input_scale[0]
            s_k = kernel_scale[0]
            x_q = (x.astype(jnp.float32) / s_in).astype(jnp.float8_e4m3fn)
            k_q = (kernel.astype(jnp.float32) / s_k).astype(jnp.float8_e4m3fn)
            y = jnp.dot(x_q.astype(jnp.float32), k_q.astype(jnp.float32), preferred_element_type=jnp.float32)
            return y * (s_in * s_k)
        dtype = jnp.bfloat16
        x = x.astype(dtype)
        orig_shape = x.shape
        x2 = x.reshape(-1, x.shape[-1])
        y = fp8_gemm_optimized(x2, input_scale, kernel, kernel_scale)
        y = y.astype(dtype) + bias
        return y.reshape(orig_shape[:-1] + (FEATURES,))
    x = L0_attn_x
    x = x + _L0_attn_ref(_layernorm(x, axis=-1), L0_attn_W_q, L0_attn_W_k, L0_attn_W_v, L0_attn_W_o, L0_attn_log_c, L0_attn_beta, L0_attn_attention_bias)
    x = x + _L0_ffn_ref(_layernorm(x, axis=-1), L0_ffn_kernel, L0_ffn_input_scale, L0_ffn_kernel_scale, L0_ffn_bias)
    return x

_drawn_inputs = setup_inputs


def setup_inputs(seed=0):
    import zlib

    import numpy as np

    out = dict(_drawn_inputs(seed))
    spreads = {'L0_ffn_bias': (0.0, 0.1)}
    factors = {'L0_attn_W_q': 8.0, 'L0_attn_W_k': 8.0, 'L0_attn_W_v': 6.168, 'L0_attn_W_o': 6.331}
    for name, (base, spread) in spreads.items():
        noise = np.random.default_rng([zlib.crc32(name.encode()), seed]).standard_normal(out[name].shape)
        drawn = base * np.exp(spread * noise) if base else spread * noise
        out[name] = jnp.asarray(drawn.astype(out[name].dtype))
    for name, factor in factors.items():
        out[name] = (out[name] * factor).astype(out[name].dtype)
    return out
```

```python
from contextlib import ExitStack

import concourse.bass as bass
from concourse import mybir

ALU = mybir.AluOpType
ACT = mybir.ActivationFunctionType
AX = mybir.AxisListType
F32 = mybir.dt.float32
BF16 = mybir.dt.bfloat16
I32 = mybir.dt.int32

P = 128
EPS = 1e-5
U_EXACT = 1100.0
A_FLOOR = 1e-8
THETA_MAX = 14.4
EXPONENT_MAX = 60.0

B, S, D = 8, 1024, 256
H, DH = 16, 16
HG, HPG = 4, 4
GT = 4
GTOK = GT * P
NG = B * S // GTOK
NJ = B * HG
KT = S // P
QH = S // GTOK
VW = DH + 2
OW = DH + 1
RU = 19
RD = 18
QPJ = QH * KT
FLT_MAX = 3.4028234e38


class Shared:
    pass


class Steps:

    def __init__(self, eng, sem, start):
        self.eng, self.sem, self.start, self.n = eng, sem, start, 0

    def __call__(self, ins):
        ins.then_inc(self.sem, 1)
        self.n += 1
        self.eng.wait_ge(self.sem, self.start + self.n)

    def mark(self, ins):
        ins.then_inc(self.sem, 1)
        self.n += 1

    def settle(self):
        self.eng.wait_ge(self.sem, self.start + self.n)


def quantise_e4m3fn(v, steps, values, spare, spare2, out):
    steps(v.tensor_scalar(spare.bitcast(I32), values.bitcast(I32), 0x7F800000, None, ALU.bitwise_and))
    steps(v.tensor_scalar(spare, spare, 2.0 ** -6, 1.5 * 2.0 ** 20, ALU.max, ALU.mult))
    steps(v.tensor_tensor(spare2, values, spare, ALU.add))
    steps(v.tensor_tensor(out, spare2, spare, ALU.subtract))


def hold(eng, passed):
    eng.sem_inc(passed, 1)

def _sb(nc, ctx, name, shape, dt=F32):
    return ctx.enter_context(nc.sbuf_tensor(name, shape, dt))


def _sem(nc, ctx, name):
    return ctx.enter_context(nc.semaphore(name))


def emit_setup(nc, g):
    with ExitStack() as ctx:
        def sb(name, shape, dt=F32):
            return _sb(nc, ctx, name, shape, dt)
        wraw = sb("wraw", [P, 4, 2, D])
        kraw = sb("kraw", [P, 2, D], BF16)
        kval, ktmp, ktmp2 = sb("kval", [P, 2 * D]), sb("ktmp", [P, 2 * D]), sb("ktmp2", [P, 2 * D])
        srow = sb("srow", [1, 8])
        brow = sb("brow", [1, D], BF16)
        ones_r = sb("ones_r", [1, P])
        ones_rb = sb("ones_rb", [1, P], BF16)
        t = sb("t", [P, 32])
        w_in, s_in, k_in = (_sem(nc, ctx, n) for n in ("w_in", "s_in", "k_in"))
        consts, wt_ps, sc_ps, wt_done = (_sem(nc, ctx, n) for n in ("consts", "wt_ps", "sc_ps", "wt_done"))
        v_steps, a_steps, to_act, to_dve, g_steps = (
            _sem(nc, ctx, n) for n in ("v_steps", "a_steps", "to_act", "to_dve", "g_steps"))

        with nc.Block() as block:
            @block.sync
            def _(sp):
                for k, a in enumerate((g.log_c, g.beta, g.attention_bias, g.input_scale, g.kernel_scale)):
                    sp.dma_start(srow[0:1, k:k + 1], a.rearrange("(a n) -> a n", a=1)).then_inc(s_in, 16)
                sp.dma_start(brow[:, :], g.ffn_bias.rearrange("(a n) -> a n", a=1)).then_inc(s_in, 16)
                for k, w in enumerate((g.W_q, g.W_k, g.W_v, g.W_o)):
                    sp.dma_start(wraw[:, k], w.rearrange("(c p) d -> p c d", p=P)).then_inc(w_in, 16)
                sp.dma_start(kraw[:, :, :], g.ffn_w.rearrange("(c p) d -> p c d", p=P)).then_inc(k_in, 16)

            @block.gpsimd
            def _(pool):
                step = Steps(pool, g_steps, 0)
                step.mark(pool.memset(g.ident[:, :], 0.0))
                step.mark(pool.memset(g.ident_b[:, :], 0.0))
                step.mark(pool.memset(g.sel[:, :], 0.0))
                pool.memset(ones_r[:, :], 1.0).then_inc(consts, 1)
                pool.memset(ones_rb[:, :], 1.0).then_inc(consts, 1)
                step.settle()
                for m in (g.ident, g.ident_b):
                    pool.affine_select(out=m[:, :], in_=m[:, :], compare_op=ALU.not_equal, fill=1.0, base=0,
                                       pattern=[[-1, P]], channel_multiplier=1).then_inc(consts, 1)
                for a in range(HPG):
                    ins = pool.affine_select(out=g.sel[:, :], in_=g.sel[:, :], compare_op=ALU.not_equal, fill=1.0,
                                             base=-(32 * a + RU - 1), pattern=[[0, P]], channel_multiplier=1)
                    if a < HPG - 1:
                        step(ins)
                    else:
                        ins.then_inc(consts, 1)

            @block.tensor
            def _(pe):
                pe.wait_ge(consts, 5)
                pe.wait_ge(s_in, 16 * 6)
                pe.matmul(g.ps[:, 0, 0:5], ones_r[:, :], srow[:, 0:5], start=True, stop=True).then_inc(sc_ps, 1)
                pe.matmul(g.ps[:, 1, 0:D], ones_rb[:, :], brow[:, :], start=True, stop=True).then_inc(sc_ps, 1)
                pe.wait_ge(w_in, 16 * 4)
                for k in range(4):
                    for oc in range(2):
                        for dc in range(2):
                            ins = pe.transpose(g.ps[:, 2 + k, dc * D + oc * P:dc * D + oc * P + P],
                                               wraw[:, k, oc, dc * P:(dc + 1) * P], g.ident[:, :])
                    ins.then_inc(wt_ps, 1)

            @block.scalar
            def _(act):
                def do(n, *a, **k):
                    act.wait_ge(to_act, n)
                    act.activation(*a, **k).then_inc(to_dve, 1)
                do(1, t[:, 8:10], t[:, 6:8], ACT.Exp)
                act.wait_ge(to_dve, 1)
                act.activation(t[:, 10:12], t[:, 8:10], ACT.Ln, bias=1.0).then_inc(to_dve, 1)
                do(2, t[:, 12:13], g.C_SP, ACT.Ln)
                act.wait_ge(to_dve, 3)
                act.activation(t[:, 13:14], t[:, 12:13], ACT.Exp, scale=0.5).then_inc(to_dve, 1)
                do(3, t[:, 16:17], t[:, 15:16], ACT.Ln, bias=1.0)
                act.activation(t[:, 17:18], t[:, 15:16], ACT.Ln, scale=-1.0, bias=1.0).then_inc(to_dve, 1)
                act.activation(g.EAB, t[:, 18:19], ACT.Exp).then_inc(to_dve, 1)
                for k in range(4):
                    act.wait_ge(wt_ps, k + 1)
                    dst = g.wT[:, :, k * D:(k + 1) * D] if k < 3 else g.woT[:, :, :]
                    act.activation(dst, g.ps[:, 2 + k, :].rearrange("p (c o) -> p c o", c=2),
                                   ACT.Copy).then_inc(wt_done, 1)

            @block.vector
            def _(v):
                step = Steps(v, v_steps, 0)
                v.wait_ge(sc_ps, 2)
                step(v.tensor_copy(t[:, 0:5], g.ps[:, 0, 0:5]))
                v.tensor_copy(g.bias_b[:, :], g.ps[:, 1, 0:D])
                step(v.tensor_scalar(t[:, 20:22], t[:, 0:2], -1.0, None, ALU.mult))
                v.tensor_tensor(t[:, 6:8], t[:, 0:2], t[:, 20:22], ALU.min).then_inc(to_act, 1)
                step(v.tensor_scalar(t[:, 22:24], t[:, 0:2], 0.0, None, ALU.max))
                v.wait_ge(to_dve, 2)
                v.tensor_tensor(g.sc[:, 0:2], t[:, 22:24], t[:, 10:12], ALU.add).then_inc(to_act, 1)
                v.wait_ge(to_act, 2)
                v.wait_ge(to_dve, 4)
                step(v.reciprocal(t[:, 24:25], t[:, 13:14]))
                step(v.tensor_scalar(t[:, 25:26], t[:, 24:25], g.C_SP, t[:, 13:14], ALU.mult, ALU.add))
                step(v.tensor_scalar(g.SQC, t[:, 25:26], 0.5, None, ALU.mult))
                step(v.reciprocal(g.ISQC, g.SQC))
                step(v.tensor_scalar(g.NEGB, g.C_BP, g.ISQC, -1.0, ALU.mult, ALU.mult))
                step(v.tensor_scalar(g.M2SC, g.SQC, -2.0, None, ALU.mult))
                step(v.tensor_scalar(t[:, 19:20], t[:, 2:3], -1.0, None, ALU.mult))
                step(v.tensor_tensor(t[:, 18:19], t[:, 19:20], t[:, 19:20], ALU.subtract))
                step(v.tensor_scalar(t[:, 14:15], g.ISQC, -EPS, None, ALU.add))
                v.tensor_scalar(t[:, 15:16], t[:, 14:15], g.SQC, None, ALU.mult).then_inc(to_act, 1)
                v.wait_ge(to_dve, 7)
                step(v.tensor_tensor(t[:, 26:27], t[:, 16:17], t[:, 17:18], ALU.subtract))
                step(v.tensor_scalar(g.ZS, t[:, 26:27], g.ISQC, 0.5, ALU.mult, ALU.mult))
                step(v.reciprocal(g.INV_SIN, t[:, 3:4]))
                step(v.reciprocal(g.INV_SK, t[:, 4:5]))
                step(v.tensor_scalar(g.S_OUT, t[:, 3:4], t[:, 4:5], None, ALU.mult))
                v.wait_ge(k_in, 16)
                step(v.tensor_scalar(kval[:, :], kraw[:, :, :].rearrange("p c d -> p (c d)"), g.INV_SK, None,
                                     ALU.mult))
                quantise_e4m3fn(v, step, kval[:, :], ktmp[:, :], ktmp2[:, :], kval[:, :])
                step(v.tensor_scalar(ktmp[:, :], kval[:, :], 3.4028234e38 / 460.0, 0.0, ALU.mult, ALU.mult))
                step(v.tensor_tensor(g.kq[:, :, :].rearrange("p c d -> p (c d)"), kval[:, :], ktmp[:, :], ALU.add))
                step(v.memset(g.run_max[:, :], -3.0e38))


def emit_project(nc, g):
    with ExitStack() as ctx:
        def sb(name, shape, dt=F32):
            return _sb(nc, ctx, name, shape, dt)
        STEPS_PROJECT = 37
        xt = sb("xt", [P, 2, GT, D])
        xn = sb("xn", [P, GT, D])
        stats, mv = sb("stats", [P, GT, 6]), sb("mv", [P, GT, 2])
        veps, lnv, rstd, rtmp = (sb(n, [P, GT]) for n in ("veps", "lnv", "rstd", "rtmp"))
        xnT = sb("xnT", [P, 2, GTOK])
        qkv = sb("qkv", [P, GT, 3 * H, DH])
        sq = sb("sq", [P, GT, 3 * H, DH])
        ss, lnss, y, y2 = (sb(n, [P, GT, 3 * H]) for n in ("ss", "lnss", "y", "y2"))
        nrm, e, rp, tn, tt, f, a, kf = (sb(n, [P, GT, 2 * H]) for n in ("nrm", "e", "rp", "tn", "tt", "f", "a", "kf"))
        vg = sb("vg", [P, GT, H])
        qk_rows = sb("qk_rows", [P, 2, GT, H, 32])
        v_rows = sb("v_rows", [P, HG, GT, HPG, VW])
        qk_T = sb("qk_T", [P, 2, HG, GTOK])
        (var_rdy, rs0_rdy, xn_rdy, xT_ps, xT_rdy, qkv_ps, qkv_free, sq_rdy, ss_rdy, y0_rdy,
         n_rdy, e_rdy, rows_rdy, t_ps, t_free, v_out, T_out, d_steps, a1, vrow_rdy) = (
            _sem(nc, ctx, n) for n in (
                "var_rdy", "rs0_rdy", "xn_rdy", "xT_ps", "xT_rdy", "qkv_ps", "qkv_free",
                "sq_rdy", "ss_rdy", "y0_rdy", "n_rdy", "e_rdy", "rows_rdy", "t_ps", "t_free",
                "v_out", "T_out", "pd_steps", "pa_steps", "vrow_rdy"))

        x_in = [_sem(nc, ctx, f"x_in{u}") for u in range(2)]
        passed_v, passed_sp = (_sem(nc, ctx, "pr_passed_" + n) for n in ("v", "sp"))

        with nc.Block() as block:
            @block.sync
            def _(sp):
                sp.dma_start(xt[:, 0], g.x_g[0]).then_inc(x_in[0], 16)

                def group(i, u, last=False):
                    j = 2 * i + u
                    if not last:
                        sp.wait_ge(xn_rdy, j + 1)
                        hold(sp, passed_sp)
                        sp.dma_start(xt[:, 1 - u],
                                     g.x_g[bass.ds(j + 1, 1)].rearrange("a p t d -> (a p) t d")).then_inc(x_in[1 - u], 16)
                    sp.wait_ge(t_free, 8 * (j + 1) + 2)
                    hold(sp, passed_sp)
                    for n, dst in ((0, g.qT_d), (1, g.kT_d)):
                        sp.dma_start(dst[bass.ds(i, 1), :, :, u * GTOK:(u + 1) * GTOK].rearrange(
                            "b g p t -> p (b g) t"), qk_T[:, n]).then_inc(T_out, 16)
                    sp.wait_ge(vrow_rdy, j + 1)
                    hold(sp, passed_sp)
                    for hg in range(HG):
                        sp.dma_start(g.v_d[bass.ds(4 * i + hg, 1), u * GTOK:(u + 1) * GTOK, :].rearrange(
                            "b (t p) f -> p (b t) f", p=P),
                            v_rows[:, hg].rearrange("p t h w -> p t (h w)")).then_inc(v_out, 16)
                with sp.Fori(0, NG // 2 - 1) as i:
                    group(i, 0)
                    group(i, 1)
                group(NG // 2 - 1, 0)
                group(NG // 2 - 1, 1, last=True)
                sp.wait_ge(T_out, 32 * (NG + 1))
                sp.wait_ge(v_out, 64 * (NG + 1))

            @block.tensor
            def _(pe):
                pe.sem_inc(xT_ps, 1)
                pe.sem_inc(t_ps, 1)

                def group(i, u):
                    j = 2 * i + u
                    pe.wait_ge(xn_rdy, j + 2)
                    for dc in range(2):
                        for t in range(GT):
                            ins = pe.transpose(g.ps[:, dc, t * P:(t + 1) * P], xn[:, t, dc * P:(dc + 1) * P],
                                               g.ident[:, :])
                        ins.then_inc(xT_ps, 1)
                    pe.wait_ge(xT_rdy, 2 * (j + 1))
                    for t in range(GT):
                        pe.wait_ge(qkv_free, 2 * (4 * j + t) + 2)
                        for dc in range(2):
                            for half in range(2):
                                ins = pe.matmul(g.ps[:, 2 + 2 * (t % 2) + half, 0:384],
                                                xnT[:, dc, t * P:(t + 1) * P],
                                                g.wT[:, dc, half * 384:(half + 1) * 384],
                                                start=dc == 0, stop=dc == 1)
                        ins.then_inc(qkv_ps, 1)
                    pe.wait_ge(rows_rdy, j + 1)
                    for n in range(2):
                        for hg in range(HG):
                            m = 4 * n + hg
                            pe.wait_ge(t_free, 8 * j + m + 1)
                            for t in range(GT):
                                ins = pe.transpose(
                                    g.ps[:, 6 + m % 2, t * P:(t + 1) * P],
                                    qk_rows[:, n, t, hg * HPG:(hg + 1) * HPG, :].rearrange("p h r -> p (h r)"),
                                    g.ident[:, :])
                            ins.then_inc(t_ps, 1)
                with pe.Fori(0, NG // 2) as i:
                    group(i, 0)
                    group(i, 1)

            @block.scalar
            def _(act):
                act.sem_inc(qkv_free, 4)
                act.sem_inc(t_free, 2)
                act.sem_inc(T_out, 32)

                def group(i, u):
                    j = 2 * i + u
                    step = Steps(act, a1, 2 * j)
                    act.wait_ge(var_rdy, j + 1)
                    step(act.activation(lnv[:, :], veps[:, :], ACT.Ln))
                    act.activation(rstd[:, :], lnv[:, :], ACT.Exp, scale=-0.5).then_inc(rs0_rdy, 1)
                    for dc in range(2):
                        act.wait_ge(xT_ps, 2 * j + dc + 2)
                        act.activation(xnT[:, dc, :], g.ps[:, dc, :], ACT.Copy).then_inc(xT_rdy, 1)
                    for t in range(GT):
                        act.wait_ge(qkv_ps, 4 * j + t + 1)
                        src = g.ps[:, 2 + 2 * (t % 2):4 + 2 * (t % 2), 0:384]
                        act.activation(sq[:, t].rearrange("p (a h) d -> p a (h d)", a=2), src,
                                       ACT.Square).then_inc(qkv_free, 1)
                        act.activation(qkv[:, t].rearrange("p (a h) d -> p a (h d)", a=2), src,
                                       ACT.Copy).then_inc(qkv_free, 1)
                    act.wait_ge(ss_rdy, j + 1)
                    step(act.activation(lnss[:, :, :], ss[:, :, :], ACT.Ln))
                    act.activation(y[:, :, :], lnss[:, :, :], ACT.Exp, scale=-0.5).then_inc(y0_rdy, 1)
                    act.wait_ge(n_rdy, j + 1)
                    act.activation(e[:, :, :], nrm[:, :, :], ACT.Exp, scale=g.M2SC).then_inc(e_rdy, 1)
                    for m in range(8):
                        act.wait_ge(t_ps, 8 * j + m + 2)
                        if m == 0:
                            act.wait_ge(T_out, 32 * (j + 1))
                        act.activation(qk_T[:, m // 4, m % 4, :], g.ps[:, 6 + m % 2, :], ACT.Copy).then_inc(t_free, 1)
                with act.Fori(0, NG // 2) as i:
                    group(i, 0)
                    group(i, 1)

            @block.vector
            def _(v):
                v.sem_inc(xn_rdy, 1)
                v.sem_inc(v_out, 64)
                v.memset(qk_rows[:, :, :, :, :], 0.0).then_inc(d_steps, 1)
                v.wait_ge(d_steps, 1)
                v.memset(qk_rows[:, 0, :, :, 16:17], 1.0).then_inc(d_steps, 1)
                for hg in range(HG):
                    v.tensor_scalar(v_rows[:, hg, :, :, DH:DH + 1], qk_rows[:, 0, :, 0:HPG, 17:18], g.EAB, None,
                                    ALU.add).then_inc(d_steps, 1)
                v.wait_ge(d_steps, 2 + HG)

                def group(i, u):
                    j = 2 * i + u
                    step = Steps(v, d_steps, 2 + HG + j * STEPS_PROJECT)
                    v.wait_ge(x_in[u], 16 * (i + 1))
                    for t in range(GT):
                        step.mark(v.bn_stats(stats[:, t, :], xt[:, u, t, :]))
                    step.settle()
                    hold(v, passed_v)
                    for t in range(GT):
                        step.mark(v.bn_aggr(mv[:, t, :], stats[:, t, :]))
                    step.settle()
                    v.tensor_scalar(veps[:, :], mv[:, :, 1], EPS, None, ALU.add).then_inc(var_rdy, 1)
                    v.wait_ge(rs0_rdy, j + 1)
                    v.wait_ge(var_rdy, j + 1)
                    step(v.tensor_tensor(rtmp[:, :], rstd[:, :], rstd[:, :], ALU.mult))
                    step(v.tensor_tensor(rtmp[:, :], rtmp[:, :], veps[:, :], ALU.mult))
                    step(v.tensor_scalar(rtmp[:, :], rtmp[:, :], -0.5, 1.5, ALU.mult, ALU.add))
                    step(v.tensor_tensor(rstd[:, :], rstd[:, :], rtmp[:, :], ALU.mult))
                    v.wait_ge(xT_ps, 2 * j + 1)
                    for t in range(GT):
                        ins = v.tensor_scalar(xn[:, t, :], xt[:, u, t, :], mv[:, t, 0:1], rstd[:, t:t + 1],
                                              ALU.subtract, ALU.mult)
                    ins.then_inc(xn_rdy, 1)
                    for t in range(GT):
                        v.wait_ge(qkv_free, 4 + 2 * (4 * j + t) + 2)
                        step.mark(v.tensor_reduce(ss[:, t, :], sq[:, t, :, :], AX.X, ALU.add))
                    step.settle()
                    v.tensor_scalar(ss[:, :, :], ss[:, :, :], EPS * EPS, None, ALU.max).then_inc(ss_rdy, 1)
                    v.wait_ge(y0_rdy, j + 1)
                    v.wait_ge(ss_rdy, j + 1)
                    step(v.tensor_tensor(y2[:, :, :], y[:, :, :], y[:, :, :], ALU.mult))
                    step(v.tensor_tensor(y2[:, :, :], y2[:, :, :], ss[:, :, :], ALU.mult))
                    step(v.tensor_scalar(y2[:, :, :], y2[:, :, :], -0.5, 1.5, ALU.mult, ALU.add))
                    step(v.tensor_tensor(y[:, :, :], y[:, :, :], y2[:, :, :], ALU.mult))
                    yqk, ssqk = y[:, :, 0:2 * H], ss[:, :, 0:2 * H]
                    v.tensor_tensor(nrm[:, :, :], ssqk, yqk, ALU.mult).then_inc(n_rdy, 1)
                    step(v.tensor_scalar(vg[:, :, :], y[:, :, 2 * H:], g.ZS, 1.0, ALU.mult, ALU.min))
                    step(v.tensor_scalar(vg[:, :, :], vg[:, :, :], g.EAB, None, ALU.mult))
                    v.wait_ge(v_out, 64 * (j + 1))
                    for hg in range(HG):
                        step.mark(v.tensor_tensor(
                            v_rows[:, hg, :, :, 0:DH], qkv[:, :, 2 * H + hg * HPG:2 * H + (hg + 1) * HPG, :],
                            vg[:, :, hg * HPG:(hg + 1) * HPG].unsqueeze(3).broadcast_to([P, GT, HPG, DH]), ALU.mult))
                    v.wait_ge(e_rdy, j + 1)
                    step(v.tensor_scalar(rp[:, :, :], e[:, :, :], 1.0, None, ALU.add))
                    step(v.reciprocal(rp[:, :, :], rp[:, :, :]))
                    step.mark(v.tensor_scalar(tn[:, :, :], e[:, :, :], -1.0, 1.0, ALU.mult, ALU.add))
                    step(v.tensor_tensor(a[:, :, :], e[:, :, :], rp[:, :, :], ALU.mult))
                    step.mark(v.tensor_tensor(tn[:, :, :], tn[:, :, :], rp[:, :, :], ALU.mult))
                    step(v.tensor_tensor(a[:, :, :], a[:, :, :], rp[:, :, :], ALU.mult))
                    step.mark(v.tensor_tensor(tt[:, :, :], tn[:, :, :], tn[:, :, :], ALU.mult))
                    step.mark(v.tensor_tensor(f[:, :, :], tn[:, :, :], yqk, ALU.mult))
                    step(v.tensor_scalar(a[:, :, :], a[:, :, :], 4.0, A_FLOOR, ALU.mult, ALU.max))
                    step(v.reciprocal(rp[:, :, :], a[:, :, :]))
                    step(v.scalar_tensor_tensor(kf[:, :, H:], f[:, :, H:], 2.0, rp[:, :, H:], ALU.mult, ALU.mult))
                    rq, rk = qk_rows[:, 0], qk_rows[:, 1]
                    v.wait_ge(t_ps, 8 * j + 1)
                    v.tensor_tensor(rq[:, :, :, 0:DH], qkv[:, :, 0:H, :],
                                    f[:, :, 0:H].unsqueeze(3).broadcast_to([P, GT, H, DH]), ALU.mult)
                    v.tensor_tensor(rk[:, :, :, 0:DH], qkv[:, :, H:2 * H, :],
                                    kf[:, :, H:].unsqueeze(3).broadcast_to([P, GT, H, DH]), ALU.mult)
                    v.tensor_copy(rq[:, :, :, 17], tt[:, :, 0:H])
                    v.tensor_copy(rq[:, :, :, 18], rp[:, :, 0:H])
                    v.scalar_tensor_tensor(rk[:, :, :, 16], tt[:, :, H:], -1.0, rp[:, :, H:], ALU.mult, ALU.mult)
                    v.tensor_scalar(rk[:, :, :, 17], rp[:, :, H:], -1.0, None, ALU.mult)
                    v.tensor_scalar(rk[:, :, :, 18], a[:, :, H:], 1.0 / EPS, None, ALU.mult).then_inc(rows_rdy, 1)
                    for hg in range(HG):
                        ins = v.tensor_scalar(v_rows[:, hg, :, :, DH + 1], a[:, :, H + hg * HPG:H + (hg + 1) * HPG],
                                              1.0 / EPS, None, ALU.mult)
                    ins.then_inc(vrow_rdy, 1)
                    assert step.n == STEPS_PROJECT, step.n
                with v.Fori(0, NG // 2) as i:
                    group(i, 0)
                    group(i, 1)


def emit_attend(nc, g):
    with ExitStack() as ctx:
        def sb(name, shape, dt=F32):
            return _sb(nc, ctx, name, shape, dt)
        qT, kT = sb("qT", [P, 2, S]), sb("kT", [P, 2, S])
        vt = sb("vt", [P, 2, KT, HPG, VW])
        rqb = sb("rqb", [P, 2, HPG, S])
        M = sb("M", [P, 2, HPG, GTOK])
        U = sb("U", [P, 4, HPG, GTOK])
        W = sb("W", [P, 2, HPG, GTOK])
        OTs = sb("OTs", [P, 2, GTOK])
        Os = sb("Os", [P, 2, GT, HPG, OW])
        cm = sb("cm", [P, 4 * QPJ])
        red = sb("red", [P, 2])
        two, sel_ones = sb("two", [P, 1]), sb("sel_ones", [P, 1])
        names = ("m_rdy", "d_rdy", "ttr_done", "ln_done", "exp_done", "pv_done", "bc_rdy", "rqb_rdy",
                 "ot_free", "tb_rdy", "os_rdy", "max_steps", "zeroed")
        (m_rdy, d_rdy, ttr_done, ln_done, exp_done, pv_done, bc_rdy, rqb_rdy, ot_free, tb_rdy, os_rdy,
         max_steps, zeroed) = (_sem(nc, ctx, "at_" + n) for n in names)
        passed_pool, passed_v, passed_sp = (_sem(nc, ctx, "at_passed_" + n) for n in ("pool", "v", "sp"))
        in_rdy = [_sem(nc, ctx, f"at_in{u}") for u in range(2)]
        o_out = [_sem(nc, ctx, f"at_o_out{h}") for h in range(2)]
        NB = NJ // 2
        SLOTS = 2 * QPJ

        def split(q):
            return (q // QPJ) % 2, (q % QPJ) // KT, q % KT

        def run(body, eng):
            body(0, first=True)
            with eng.Fori(1, NB - 1) as i:
                body(i)
            body(NB - 1, last=True)

        with nc.Block() as block:
            @block.sync
            def _(sp):
                def load(j, u, ij):
                    src = (g.qT_d.rearrange("b g p s -> (b g) p s"), g.kT_d.rearrange("b g p s -> (b g) p s"))
                    for buf, d in ((qT, src[0]), (kT, src[1])):
                        sp.dma_start(buf[:, u, :], d[bass.ds(ij, 1)].rearrange("a p s -> (a p) s")).then_inc(in_rdy[u], 16)
                    sp.dma_start(vt[:, u].rearrange("p k h w -> p k (h w)"),
                                 g.v_d[bass.ds(ij, 1)].rearrange("a (k p) f -> p (a k) f", p=P)).then_inc(in_rdy[u], 16)

                def store(j, qh):
                    sp.wait_ge(os_rdy, 2 * j + qh + 2)
                    hold(sp, passed_sp)
                    sp.dma_start(g.o_d[bass.ds(j, 1), qh * GTOK:(qh + 1) * GTOK, :].rearrange(
                        "a (t p) f -> p (a t) f", p=P), Os[:, qh].rearrange("p t h w -> p t (h w)")).then_inc(o_out[qh], 16)

                def body(i, first=False, last=False):
                    for u in range(2):
                        j = 2 * i + u
                        if not (last and u == 1):
                            sp.wait_ge(pv_done, QPJ * j + 2)
                            hold(sp, passed_sp)
                            sp.wait_ge(m_rdy, 2 * QPJ * j)
                            hold(sp, passed_sp)
                            load(j + 1, 1 - u, j + 1)
                        if not (first and u == 0):
                            store(j - 1, 1)
                        store(j, 0)
                load(0, 0, 0)
                run(body, sp)
                store(NJ - 1, 1)
                for qh in range(QH):
                    sp.wait_ge(o_out[qh], 16 * NJ)

            @block.gpsimd
            def _(pool):
                def body(i, first=False, last=False):
                    for s in range(SLOTS):
                        u, qh, kt = split(s)
                        j, n = 2 * i + u, SLOTS * i + s
                        if s % QPJ == 0:
                            pool.wait_ge(in_rdy[u], 48 * (i + 1))
                            pool.wait_ge(rqb_rdy, 2 * HPG * (j + 1) + 1)
                        pool.wait_ge(ttr_done, 2 * n)
                        hold(pool, passed_pool)
                        for h in range(HPG):
                            ins = pool.tensor_scalar(M[:, s % 2, h, :], rqb[:, u, h, qh * GTOK:(qh + 1) * GTOK],
                                                     vt[:, u, kt, h, DH + 1:DH + 2], 0.0, ALU.min, ALU.max)
                            if h % 2:
                                ins.then_inc(m_rdy, 1)
                run(body, pool)

            @block.tensor
            def _(pe):
                pe.sem_inc(pv_done, 2)

                def distances(i, s):
                    u, qh, kt = split(s)
                    for pair in range(2):
                        pe.wait_ge(ttr_done, 2 * (SLOTS * i + s) + pair + 1)
                        for h in (2 * pair, 2 * pair + 1):
                            r = slice(32 * h, 32 * h + RD)
                            ins = pe.matmul(g.ps[:, h, :], kT[r, u, kt * P:(kt + 1) * P],
                                            qT[r, u, qh * GTOK:(qh + 1) * GTOK], start=True, stop=True)
                        ins.then_inc(d_rdy, 1)

                def values(i, q):
                    u, qh, kt = split(q)
                    n = SLOTS * i + q
                    pe.wait_ge(exp_done, n + 5)
                    if kt == 0:
                        pe.wait_ge(ot_free, (SLOTS // KT) * i + q // KT + 1)
                    for h in range(HPG):
                        ins = pe.matmul(g.ps[32 * h:32 * h + OW, 4 + qh, :], vt[:, u, kt, h, 0:OW], W[:, q % 2, h, :],
                                        start=kt == 0, stop=kt == KT - 1)
                    ins.then_inc(pv_done, 1)

                def to_token_rows(x, qh):
                    pe.wait_ge(ot_free, x + 3)
                    pe.wait_ge(os_rdy, x + 1)
                    for t in range(GT):
                        ins = pe.transpose(g.ps[:, 6, t * P:(t + 1) * P], OTs[:, qh, t * P:(t + 1) * P], g.ident[:, :])
                    ins.then_inc(tb_rdy, 1)

                def spread_rq(i, u, c):
                    j = 2 * i + u
                    h, qh = c // 2, c % 2
                    if c == 0:
                        pe.wait_ge(in_rdy[u], 48 * (i + 1))
                    pe.wait_ge(rqb_rdy, 2 * HPG * j + c + 1)
                    r = slice(32 * h, 32 * h + RU)
                    pe.matmul(g.ps[:, 7, :], g.sel[r, :], qT[r, u, qh * GTOK:(qh + 1) * GTOK],
                              start=True, stop=True).then_inc(bc_rdy, 1)

                def body(i, first=False, last=False):
                    for s in range(SLOTS + (3 if last else 0)):
                        k, u = s % QPJ, (s // QPJ) % 2
                        if s < SLOTS:
                            if k == 0:
                                pe.wait_ge(in_rdy[u], 48 * (i + 1))
                            distances(i, s)
                        if s >= 3 or not first:
                            values(i, s - 3)
                        if s < SLOTS:
                            if k == 13:
                                to_token_rows(4 * i + 2 * u, 0)
                            if k == 5 and (s >= QPJ or not first):
                                to_token_rows(4 * i + 2 * u - 1, 1)
                            if 6 <= k < 14 and not (last and u == 1):
                                spread_rq(i + u, 1 - u, k - 6)
                for c in range(2 * HPG):
                    spread_rq(0, 0, c)
                run(body, pe)
                to_token_rows(2 * NJ - 1, 1)
                pe.wait_ge(max_steps, 2 * NB + 3)
                pe.matmul(g.ps[0:1, 7, 0:1], red[:, 0:1], sel_ones[:, :], start=True, stop=True).then_inc(bc_rdy, 1)

            @block.scalar
            def _(act):
                act.sem_inc(exp_done, 4)

                def log(i, s):
                    act.wait_ge(ttr_done, 2 * (SLOTS * i + s) + 4)
                    act.activation(U[:, s % 4], U[:, s % 4], ACT.Ln, scale=-4.0, bias=two[:, :]).then_inc(ln_done, 1)

                def power(i, q):
                    n = SLOTS * i + q
                    act.wait_ge(ln_done, n + 1)
                    act.wait_ge(pv_done, n + 1)
                    act.activation(W[:, q % 2], U[:, q % 4], ACT.Exp, scale=g.NEGB).then_inc(exp_done, 1)

                def body(i, first=False, last=False):
                    for s in range(SLOTS + (1 if last else 0)):
                        if s < SLOTS:
                            log(i, s)
                        if s >= 1 or not first:
                            power(i, s - 1)
                act.wait_ge(zeroed, 2)
                run(body, act)

            @block.vector
            def _(v):
                v.sem_inc(ttr_done, 2)
                v.sem_inc(ot_free, 2)
                v.sem_inc(rqb_rdy, 1)
                v.sem_inc(os_rdy, 1)
                v.memset(two[:, :], 2.0).then_inc(zeroed, 1)
                v.memset(sel_ones[:, :], 1.0)
                v.memset(g.ps[:, 4:6, :], 0.0).then_inc(zeroed, 1)
                v.wait_ge(zeroed, 2)

                def clamp(i, s):
                    n = SLOTS * i + s
                    v.wait_ge(exp_done, n + 1)
                    for pair in range(2):
                        v.wait_ge(d_rdy, 2 * n + pair + 1)
                        v.wait_ge(m_rdy, 2 * n + pair + 1)
                        hold(v, passed_v)
                        hs = slice(2 * pair, 2 * pair + 2)
                        v.tensor_tensor_reduce(U[:, s % 4, hs, :], M[:, s % 2, hs, :], g.ps[:, hs, :], 1.0, -3.0e38,
                                               ALU.mult, ALU.max, cm[:, 2 * s + pair:2 * s + pair + 1]).then_inc(ttr_done, 1)

                def copy_rq(j, u, c):
                    v.wait_ge(bc_rdy, 2 * HPG * j + c + 1)
                    if c == 0:
                        v.wait_ge(m_rdy, 2 * QPJ * (j - 1)) if not isinstance(j, int) or j > 0 else None
                    h, qh = c // 2, c % 2
                    v.tensor_copy(rqb[:, u, h, qh * GTOK:(qh + 1) * GTOK], g.ps[:, 7, :]).then_inc(rqb_rdy, 1)

                def copy_sums(x, qh):
                    v.wait_ge(pv_done, KT * x + KT + 2)
                    v.tensor_copy(OTs[:, qh, :], g.ps[:, 4 + qh, :]).then_inc(ot_free, 1)

                def copy_rows(j, qh):
                    x = 2 * j + qh
                    v.wait_ge(tb_rdy, x + 1)
                    v.wait_ge(o_out[qh], 16 * j)
                    v.tensor_copy(Os[:, qh], g.ps[:, 6, :].rearrange("p (t h r) -> p t h r", t=GT, h=HPG)[:, :, :, 0:OW])\
                     .then_inc(os_rdy, 1)

                def body(i, first=False, last=False):
                    for s in range(SLOTS):
                        k, u = s % QPJ, s // QPJ
                        clamp(i, s)
                        if k == 12:
                            copy_sums(4 * i + 2 * u, 0)
                        if k == 15:
                            copy_rows(2 * i + u, 0)
                        if s >= QPJ or not first:
                            if k == 4:
                                copy_sums(4 * i + 2 * u - 1, 1)
                            if k == 7:
                                copy_rows(2 * i + u - 1, 1)
                        if 7 <= k < 15 and not (last and u == 1):
                            copy_rq(2 * i + u + 1, 1 - u, k - 7)
                    v.wait_ge(ttr_done, 2 * SLOTS * (i + 1) + 2)
                    v.tensor_reduce(red[:, 0:1], cm[:, :], AX.X, ALU.max).then_inc(max_steps, 1)
                    v.wait_ge(max_steps, 2 * i + 1)
                    v.tensor_tensor(g.run_max[:, :], g.run_max[:, :], red[:, 0:1], ALU.max).then_inc(max_steps, 1)
                    v.wait_ge(max_steps, 2 * i + 2)
                for c in range(2 * HPG):
                    copy_rq(0, 0, c)
                run(body, v)
                copy_sums(2 * NJ - 1, 1)
                copy_rows(NJ - 1, 1)
                v.tensor_scalar(red[:, 0:1], g.run_max[:, :], -U_EXACT, None, ALU.is_gt).then_inc(max_steps, 1)
                v.tensor_scalar(red[:, 1:2], g.NEGB, -EXPONENT_MAX / THETA_MAX, None, ALU.is_lt).then_inc(max_steps, 1)
                v.wait_ge(max_steps, 2 * NB + 2)
                v.tensor_tensor(red[:, 0:1], red[:, 0:1], red[:, 1:2], ALU.add).then_inc(max_steps, 1)
                v.wait_ge(bc_rdy, 2 * HPG * NJ + 1)
                v.tensor_copy(g.flag[:, :], g.ps[0:1, 7, 0:1]).then_inc(max_steps, 1)


def emit_general(nc, g):
    with ExitStack() as ctx:
        def sb(name, shape, dt=F32):
            return _sb(nc, ctx, name, shape, dt)
        Qs, Ks = sb("Qs", [RU, P]), sb("Ks", [RU, S])
        Vs = sb("Vs", [P, KT, VW])
        rqc, low, shift = sb("rqc", [P, 1]), sb("low", [P, 1]), sb("shift", [P, 1])
        X, Z, T = sb("X", [P, S]), sb("Z", [P, S]), sb("T", [P, S])
        WT = sb("WT", [P, KT, P])
        Og = sb("Og", [P, OW])
        gin, p_rdy, v_rdy, a_rdy, gout = (_sem(nc, ctx, "ge_" + n) for n in ("in", "p_rdy", "v_rdy", "a_rdy", "out"))
        run_known = _sem(nc, ctx, "ge_flag_read")
        gv, ga = _sem(nc, ctx, "ge_v_steps"), _sem(nc, ctx, "ge_a_steps")
        qrows, krows = (d.rearrange("b g (h r) s -> (b g h) r s", h=HPG) for d in (g.qT_d, g.kT_d))

        def steps(eng, body, stored=None):
            needed = eng.value_load(g.flag[0:1, 0:1], min_val=0, max_val=2 * P)
            with eng.If(needed > 0):
                with eng.Fori(0, NJ) as j:
                    with eng.Fori(0, HPG) as h:
                        with eng.Fori(0, KT) as t:
                            body(j, h, t, (j * HPG + h) * KT + t)
                if stored is not None:
                    eng.wait_ge(stored, 16 * (NJ * HPG * KT + 1))

        with nc.Block() as block:
            @block.sync
            def _(sp):
                def body(j, h, t, n):
                    sp.wait_ge(gout, 16 * (n + 1))
                    hold(sp, run_known)
                    sp.dma_start(Qs[:, :], qrows[bass.ds(j * HPG + h, 1), 0:RU, bass.ds(t * P, P)].rearrange(
                        "a r s -> (a r) s")).then_inc(gin, 16)
                    sp.dma_start(Ks[:, :], krows[bass.ds(j * HPG + h, 1), 0:RU, :].rearrange(
                        "a r s -> (a r) s")).then_inc(gin, 16)
                    sp.dma_start(Vs[:, :, :], g.v_d[bass.ds(j, 1), :, bass.ds(h * VW, VW)].rearrange(
                        "a (k p) w -> p (a k) w", p=P)).then_inc(gin, 16)
                    sp.wait_ge(v_rdy, 7 * n + 7)
                    hold(sp, run_known)
                    sp.dma_start(g.o_d[bass.ds(j, 1), bass.ds(t * P, P), bass.ds(h * OW, OW)].rearrange(
                        "a p w -> (a p) w"), Og[:, :]).then_inc(gout, 16)
                sp.sem_inc(gout, 16)
                steps(sp, body, gout)

            @block.tensor
            def _(pe):
                def body(j, h, t, n):
                    pe.wait_ge(gin, 48 * (n + 1))
                    for half in range(2):
                        ks = slice(half * 512, (half + 1) * 512)
                        pe.matmul(g.ps[:, half, :], Qs[0:RD, :], Ks[0:RD, ks], start=True, stop=True)
                        pe.matmul(g.ps[:, 2 + half, :], g.sel[0:RU, :], Ks[:, ks], start=True, stop=True)
                    pe.matmul(g.ps[:, 4, 0:1], Qs[:, :], g.sel[0:RU, 0:1], start=True, stop=True).then_inc(p_rdy, 1)
                    pe.wait_ge(a_rdy, 3 * n + 3)
                    for k in range(KT):
                        ins = pe.transpose(g.ps[:, 5 + k // 4, (k % 4) * P:(k % 4 + 1) * P], Z[:, k * P:(k + 1) * P],
                                           g.ident[:, :])
                    ins.then_inc(p_rdy, 1)
                    pe.wait_ge(v_rdy, 7 * n + 6)
                    for k in range(KT):
                        ins = pe.matmul(g.ps[:, 7, 0:OW], WT[:, k, :], Vs[:, k, 0:OW], start=k == 0, stop=k == KT - 1)
                    ins.then_inc(p_rdy, 1)
                steps(pe, body)

            @block.scalar
            def _(act):
                def body(j, h, t, n):
                    act.wait_ge(v_rdy, 7 * n + 3)
                    act.activation(T[:, :], Z[:, :], ACT.Ln).then_inc(ga, 1)
                    act.wait_ge(ga, n + 1)
                    act.activation(Z[:, :], T[:, :], ACT.Exp, scale=0.5).then_inc(a_rdy, 1)
                    act.wait_ge(v_rdy, 7 * n + 4)
                    act.activation(X[:, :], T[:, :], ACT.Ln).then_inc(a_rdy, 1)
                    act.wait_ge(v_rdy, 7 * n + 5)
                    act.wait_ge(a_rdy, 3 * n + 2)
                    act.activation(Z[:, :], X[:, :], ACT.Exp, scale=g.NEGB, bias=shift[:, :]).then_inc(a_rdy, 1)
                steps(act, body)

            @block.vector
            def _(v):
                def body(j, h, t, n):
                    step = Steps(v, gv, 6 * n)
                    v.wait_ge(p_rdy, 3 * n + 1)
                    v.tensor_copy(rqc[:, :], g.ps[:, 4, 0:1]).then_inc(v_rdy, 1)
                    v.wait_ge(v_rdy, 7 * n + 1)
                    step(v.tensor_scalar(T[:, :], g.ps[:, 2:4, :].rearrange("p a k -> p (a k)"), rqc[:, :], None, ALU.min))
                    step(v.tensor_tensor(T[:, :], T[:, :], g.ps[:, 0:2, :].rearrange("p a k -> p (a k)"), ALU.mult))
                    step(v.tensor_scalar(X[:, :], T[:, :], -2.0, 1.0, ALU.mult, ALU.add))
                    v.tensor_scalar(X[:, :], X[:, :], 1.0 + EPS, None, ALU.max).then_inc(v_rdy, 1)
                    v.wait_ge(v_rdy, 7 * n + 2)
                    step(v.tensor_scalar(T[:, :], X[:, :], -1.0, None, ALU.add))
                    v.scalar_tensor_tensor(Z[:, :], X[:, :], 1.0, T[:, :], ALU.add, ALU.mult).then_inc(v_rdy, 1)
                    v.wait_ge(a_rdy, 3 * n + 1)
                    v.tensor_tensor(T[:, :], X[:, :], Z[:, :], ALU.add).then_inc(v_rdy, 1)
                    v.wait_ge(a_rdy, 3 * n + 2)
                    step(v.tensor_reduce(low[:, :], X[:, :], AX.X, ALU.min))
                    step(v.tensor_scalar(shift[:, :], low[:, :], g.NEGB, -1.0, ALU.mult, ALU.mult))
                    v.sem_inc(v_rdy, 1)
                    v.wait_ge(p_rdy, 3 * n + 2)
                    v.tensor_copy(WT[:, :, :].rearrange("p k q -> p (k q)"),
                                  g.ps[:, 5:7, :].rearrange("p a k -> p (a k)")).then_inc(v_rdy, 1)
                    v.wait_ge(p_rdy, 3 * n + 3)
                    v.tensor_copy(Og[:, :], g.ps[:, 7, 0:OW]).then_inc(v_rdy, 1)
                steps(v, body)


def emit_finish(nc, g):
    with ExitStack() as ctx:
        def sb(name, shape, dt=F32):
            return _sb(nc, ctx, name, shape, dt)
        o_in = sb("o_in", [P, 2, HG, GT, HPG, OW])
        xt = sb("xt2", [P, 2, GT, D])
        rs = sb("rs", [P, HG, GT, HPG])
        on, sq = sb("on", [P, GT, H, DH]), sb("osq", [P, GT, H, DH])
        ss, lnss, y, y2 = (sb("o" + n, [P, GT, H]) for n in ("ss", "lnss", "y", "y2"))
        ocT = sb("ocT", [P, 2, GTOK])
        x1 = sb("x1", [P, GT, D])
        stats, mv = sb("stats2", [P, GT, 6]), sb("mv2", [P, GT, 2])
        veps, lnv, rstd, rtmp, rmax = (sb("f" + n, [P, GT]) for n in ("veps", "lnv", "rstd", "rtmp", "rmax"))
        xb, xq = sb("xb", [P, GT, D], BF16), sb("xq", [P, GT, D], BF16)
        vf, sp1, sp2 = (sb(n, [P, GT, D]) for n in ("vf", "spare1", "spare2"))
        xqT = sb("xqT", [P, 2, GTOK], BF16)
        yb, yb2 = sb("yb", [P, GT, D], BF16), sb("yb2", [P, GT, D], BF16)
        res = sb("res", [P, 2, GT, D])
        (on_rdy, osq_rdy, oss_rdy, oy_rdy, oc_rdy, oT_ps, oT_rdy, wo_ps, var_rdy, rs0_rdy, xq_rdy, xqT_ps,
         xqT_rdy, y_ps, yb_rdy, res_rdy, steps_v, steps_a) = (
            _sem(nc, ctx, "fi_" + n) for n in (
                "on", "osq", "oss", "oy", "oc", "oT_ps", "oT_rdy", "wo_ps", "var", "rs0", "xq", "xqT_ps",
                "xqT_rdy", "y_ps", "yb", "res", "steps_v", "steps_a"))
        psb = g.ps[:, 4, :].bitcast(BF16)
        STEPS_FINISH = 29

        in2, res_out = ([_sem(nc, ctx, f"fi_{n}{u}") for u in range(2)] for n in ("in", "out"))
        passed_v, passed_sp = (_sem(nc, ctx, "fi_passed_" + n) for n in ("v", "sp"))

        with nc.Block() as block:
            @block.sync
            def _(sp):
                def load(i, j, u):
                    sp.dma_start(xt[:, u], g.x_g[bass.ds(j, 1)].rearrange("a p t d -> (a p) t d")).then_inc(in2[u], 16)
                    for hg in range(HG):
                        sp.dma_start(o_in[:, u, hg].rearrange("p t h w -> p t (h w)"),
                                     g.o_d[bass.ds(4 * i + hg, 1), u * GTOK:(u + 1) * GTOK, :].rearrange(
                                         "a (t p) f -> p (a t) f", p=P)).then_inc(in2[u], 16)

                def group(i, u, last=False):
                    j = 2 * i + u
                    if not last:
                        sp.wait_ge(res_rdy, j + 1)
                        hold(sp, passed_sp)
                        load(i + u, j + 1, 1 - u)
                    sp.wait_ge(res_rdy, j + 2)
                    hold(sp, passed_sp)
                    sp.dma_start(g.out_g[bass.ds(j, 1)].rearrange("a p t d -> (a p) t d"), res[:, u]).then_inc(res_out[u], 16)
                load(0, 0, 0)
                with sp.Fori(0, NG // 2 - 1) as i:
                    group(i, 0)
                    group(i, 1)
                group(NG // 2 - 1, 0)
                group(NG // 2 - 1, 1, last=True)
                for u in range(2):
                    sp.wait_ge(res_out[u], 8 * NG + 16)

            @block.tensor
            def _(pe):
                pe.sem_inc(xqT_ps, 1)

                def group(i, u):
                    j = 2 * i + u
                    pe.wait_ge(oc_rdy, j + 1)
                    for dc in range(2):
                        for t in range(GT):
                            ins = pe.transpose(g.ps[:, dc, t * P:(t + 1) * P],
                                               on[:, t, dc * 8:(dc + 1) * 8, :].rearrange("p h d -> p (h d)"), g.ident[:, :])
                        ins.then_inc(oT_ps, 1)
                    pe.wait_ge(oT_rdy, 2 * (j + 1))
                    for t in range(GT):
                        for dc in range(2):
                            ins = pe.matmul(g.ps[:, 2 + t // 2, (t % 2) * D:(t % 2 + 1) * D], ocT[:, dc, t * P:(t + 1) * P],
                                            g.woT[:, dc, :], start=dc == 0, stop=dc == 1)
                    ins.then_inc(wo_ps, 1)
                    pe.wait_ge(xq_rdy, j + 1)
                    for dc in range(2):
                        for t in range(GT):
                            ins = pe.transpose(psb[:, dc * GTOK + t * P:dc * GTOK + (t + 1) * P],
                                               xq[:, t, dc * P:(dc + 1) * P], g.ident_b[:, :])
                    ins.then_inc(xqT_ps, 1)
                    pe.wait_ge(xqT_rdy, j + 1)
                    for t in range(GT):
                        for dc in range(2):
                            ins = pe.matmul(g.ps[:, 6 + t // 2, (t % 2) * D:(t % 2 + 1) * D], xqT[:, dc, t * P:(t + 1) * P],
                                            g.kq[:, dc, :], start=dc == 0, stop=dc == 1)
                    ins.then_inc(y_ps, 1)
                with pe.Fori(0, NG // 2) as i:
                    group(i, 0)
                    group(i, 1)

            @block.scalar
            def _(act):
                def group(i, u):
                    j = 2 * i + u
                    step = Steps(act, steps_a, 2 * j)
                    act.wait_ge(on_rdy, j + 1)
                    act.activation(sq[:, :, :, :], on[:, :, :, :], ACT.Square).then_inc(osq_rdy, 1)
                    act.wait_ge(oss_rdy, j + 1)
                    step(act.activation(lnss[:, :, :], ss[:, :, :], ACT.Ln))
                    act.activation(y[:, :, :], lnss[:, :, :], ACT.Exp, scale=-0.5).then_inc(oy_rdy, 1)
                    for dc in range(2):
                        act.wait_ge(oT_ps, 2 * j + dc + 1)
                        act.activation(ocT[:, dc, :], g.ps[:, dc, :], ACT.Copy).then_inc(oT_rdy, 1)
                    act.wait_ge(var_rdy, j + 1)
                    step(act.activation(lnv[:, :], veps[:, :], ACT.Ln))
                    act.activation(rstd[:, :], lnv[:, :], ACT.Exp, scale=-0.5).then_inc(rs0_rdy, 1)
                    act.wait_ge(xqT_ps, j + 2)
                    act.activation(xqT[:, :, :], psb.rearrange("p (c n) -> p c n", c=2), ACT.Copy).then_inc(xqT_rdy, 1)
                    act.wait_ge(y_ps, j + 1)
                    act.activation(yb[:, :, :].rearrange("p (a t) d -> p a (t d)", a=2), g.ps[:, 6:8, :], ACT.Identity,
                                   scale=g.S_OUT).then_inc(yb_rdy, 1)
                with act.Fori(0, NG // 2) as i:
                    group(i, 0)
                    group(i, 1)

            @block.vector
            def _(v):
                v.sem_inc(res_rdy, 1)
                for u in range(2):
                    v.sem_inc(res_out[u], 16)
                def group(i, u):
                    j = 2 * i + u
                    step = Steps(v, steps_v, STEPS_FINISH * j)
                    v.wait_ge(in2[u], 80 * (i + 1))
                    step(v.reciprocal(rs[:, :, :, :], o_in[:, u, :, :, :, DH]))
                    for hg in range(HG):
                        ins = v.tensor_tensor(on[:, :, hg * HPG:(hg + 1) * HPG, :], o_in[:, u, hg, :, :, 0:DH],
                                              rs[:, hg].unsqueeze(3).broadcast_to([P, GT, HPG, DH]), ALU.mult)
                    ins.then_inc(on_rdy, 1)
                    v.wait_ge(osq_rdy, j + 1)
                    step(v.tensor_reduce(ss[:, :, :], sq[:, :, :, :], AX.X, ALU.add))
                    v.tensor_scalar(ss[:, :, :], ss[:, :, :], EPS * EPS, None, ALU.max).then_inc(oss_rdy, 1)
                    v.wait_ge(oss_rdy, j + 1)
                    v.wait_ge(oy_rdy, j + 1)
                    step(v.tensor_tensor(y2[:, :, :], y[:, :, :], y[:, :, :], ALU.mult))
                    step(v.tensor_tensor(y2[:, :, :], y2[:, :, :], ss[:, :, :], ALU.mult))
                    step(v.tensor_scalar(y2[:, :, :], y2[:, :, :], -0.5, 1.5, ALU.mult, ALU.add))
                    step(v.tensor_tensor(y[:, :, :], y[:, :, :], y2[:, :, :], ALU.mult))
                    step(v.tensor_scalar(y[:, :, :], y[:, :, :], g.ZS, 1.0, ALU.mult, ALU.min))
                    v.tensor_tensor(on[:, :, :, :].rearrange("p t h d -> p (t h) d"),
                                    on[:, :, :, :].rearrange("p t h d -> p (t h) d"),
                                    y[:, :, :].rearrange("p t h -> p (t h)").unsqueeze(2).broadcast_to([P, GT * H, DH]),
                                    ALU.mult).then_inc(oc_rdy, 1)
                    v.wait_ge(wo_ps, j + 1)
                    x1f = x1[:, :, :].rearrange("p (a t) d -> p a (t d)", a=2)
                    step(v.tensor_tensor(x1f, xt[:, u].rearrange("p (a t) d -> p a (t d)", a=2), g.ps[:, 2:4, :], ALU.add))
                    for t in range(GT):
                        step.mark(v.bn_stats(stats[:, t, :], x1[:, t, :]))
                    step.settle()
                    hold(v, passed_v)
                    for t in range(GT):
                        step.mark(v.bn_aggr(mv[:, t, :], stats[:, t, :]))
                    step.settle()
                    v.tensor_scalar(veps[:, :], mv[:, :, 1], EPS, None, ALU.add).then_inc(var_rdy, 1)
                    v.wait_ge(var_rdy, j + 1)
                    v.wait_ge(rs0_rdy, j + 1)
                    step(v.tensor_tensor(rtmp[:, :], rstd[:, :], rstd[:, :], ALU.mult))
                    step(v.tensor_tensor(rtmp[:, :], rtmp[:, :], veps[:, :], ALU.mult))
                    step(v.tensor_scalar(rtmp[:, :], rtmp[:, :], -0.5, 1.5, ALU.mult, ALU.add))
                    step(v.tensor_tensor(rstd[:, :], rstd[:, :], rtmp[:, :], ALU.mult))
                    for t in range(GT):
                        ins = v.tensor_scalar(xb[:, t, :], x1[:, t, :], mv[:, t, 0:1], rstd[:, t:t + 1],
                                              ALU.subtract, ALU.mult)
                    step(ins)
                    step(v.tensor_scalar(vf[:, :, :], xb[:, :, :], g.INV_SIN, None, ALU.mult))
                    step(v.tensor_reduce(rmax[:, :], vf[:, :, :], AX.X, ALU.max, apply_absolute_value=True))
                    step(v.tensor_scalar(rmax[:, :], rmax[:, :], FLT_MAX / 464.001, 0.0, ALU.mult, ALU.mult))
                    flat = [a[:, :, :].rearrange("p t d -> p (t d)") for a in (vf, sp1, sp2, xq)]
                    v.wait_ge(xqT_ps, j + 1)
                    quantise_e4m3fn(v, step, *flat)
                    v.sem_inc(xq_rdy, 1)
                    v.wait_ge(yb_rdy, j + 1)
                    step(v.tensor_tensor(yb2[:, :, :], yb[:, :, :],
                                         g.bias_b[:, :].unsqueeze(1).broadcast_to([P, GT, D]), ALU.add))
                    v.wait_ge(res_out[u], 16 * i + 16)
                    for t in range(GT):
                        ins = v.scalar_tensor_tensor(res[:, u, t, :], yb2[:, t, :], rmax[:, t:t + 1], x1[:, t, :],
                                                     ALU.add, ALU.add)
                    ins.then_inc(res_rdy, 1)
                    assert step.n == STEPS_FINISH, step.n
                with v.Fori(0, NG // 2) as i:
                    group(i, 0)
                    group(i, 1)


def layer_kernel(nc, x, W_q, W_k, W_v, W_o, log_c, beta, attention_bias, ffn_w, input_scale, kernel_scale,
                 ffn_bias, out):
    assert tuple(x.shape) == (B, S, D) and (QH, GT) == (2, 4)
    g = Shared()
    g.W_q, g.W_k, g.W_v, g.W_o, g.log_c, g.beta, g.attention_bias = W_q, W_k, W_v, W_o, log_c, beta, attention_bias
    g.ffn_w, g.input_scale, g.kernel_scale, g.ffn_bias = ffn_w, input_scale, kernel_scale, ffn_bias
    g.x_g = x.rearrange("b (u t p) d -> (b u) p t d", t=GT, p=P)
    g.out_g = out.rearrange("b (u t p) d -> (b u) p t d", t=GT, p=P)
    g.qT_d = nc.dram_tensor("qT_scratch", [B, HG, P, S], F32, kind="Internal").ap()
    g.kT_d = nc.dram_tensor("kT_scratch", [B, HG, P, S], F32, kind="Internal").ap()
    g.v_d = nc.dram_tensor("v_scratch", [NJ, S, HPG * VW], F32, kind="Internal").ap()
    g.o_d = nc.dram_tensor("o_scratch", [NJ, S, HPG * OW], F32, kind="Internal").ap()

    with ExitStack() as root:
        def sb(name, shape, dt=F32):
            return root.enter_context(nc.sbuf_tensor(name, shape, dt))

        g.ident = sb("ident", [P, P])
        g.ident_b = sb("ident_b", [P, P], BF16)
        g.sel = sb("sel", [P, P])
        g.wT = sb("wT", [P, 2, 3 * D])
        g.woT = sb("woT", [P, 2, D])
        g.kq = sb("kq", [P, 2, D], BF16)
        g.bias_b = sb("bias_b", [P, D], BF16)
        g.flag = sb("flag", [1, 1], I32)
        g.run_max = sb("run_max", [P, 1])
        g.ps = root.enter_context(nc.psum_tensor("ps", [P, 8, 512], F32))
        g.sc = sb("sc", [P, 16])
        (g.C_SP, g.C_BP, g.SQC, g.ISQC, g.NEGB, g.ZS, g.M2SC, g.EAB, g.INV_SIN, g.INV_SK, g.S_OUT) = (
            g.sc[:, k:k + 1] for k in range(11))
        emit_setup(nc, g)
        emit_project(nc, g)
        emit_attend(nc, g)
        emit_general(nc, g)
        emit_finish(nc, g)


_INS = ["L0_attn_x", "L0_attn_W_q", "L0_attn_W_k", "L0_attn_W_v", "L0_attn_W_o", "L0_attn_log_c", "L0_attn_beta",
        "L0_attn_attention_bias", "L0_ffn_kernel", "L0_ffn_input_scale", "L0_ffn_kernel_scale", "L0_ffn_bias"]


def kernel(**inputs):
    import numpy as _np
    import concourse.bacc as _bacc
    from concourse.bass_utils import run_bass_kernel_spmd as _run

    nc = _bacc.Bacc("TRN2", target_bir_lowering=False, num_devices=1)
    arrays, args = {}, []
    for name in _INS:
        a = _np.ascontiguousarray(inputs[name])
        if a.ndim == 0:
            a = a.reshape(1)
        arrays[f"in_{name}_dram"] = a
        args.append(nc.dram_tensor(f"in_{name}_dram", a.shape, mybir.dt.from_np(a.dtype), kind="ExternalInput").ap())
    shape = inputs["L0_attn_x"].shape
    args.append(nc.dram_tensor("out_0_dram", shape, F32, kind="ExternalOutput").ap())
    layer_kernel(nc, *args)
    r = _run(nc, [arrays], core_ids=[0])
    return r.results[0]["out_0_dram"]
```

```python
from contextlib import ExitStack

import concourse.bass as bass
from concourse import mybir

ALU = mybir.AluOpType
ACT = mybir.ActivationFunctionType
AX = mybir.AxisListType
F32 = mybir.dt.float32
BF16 = mybir.dt.bfloat16
I32 = mybir.dt.int32

P = 128
ACT_SET = "natural_log_exp_and_others"
EPS = 1e-5
U_EXACT = 1100.0
A_FLOOR = 1e-8
THETA_MAX = 14.4
EXPONENT_MAX = 60.0

B, S, D = 8, 1024, 256
H, DH = 16, 16
HG, HPG = 4, 4
GT = 4
GTOK = GT * P
NG = B * S // GTOK
NJ = B * HG
KT = S // P
QH = S // GTOK
VW = DH + 2
OW = DH + 1
RU = 19
Q_PARTS = (0, 0, 0, 1, 1, 2)
K_PARTS = (0, 1, 2, 0, 1, 0)
RS = RU * len(Q_PARTS)
QPJ = QH * KT
FLT_MAX = 3.4028234e38


class Shared:
    pass


class Steps:

    def __init__(self, eng, sem, start):
        self.eng, self.sem, self.start, self.n = eng, sem, start, 0

    def __call__(self, ins):
        ins.then_inc(self.sem, 1)
        self.n += 1
        self.eng.wait_ge(self.sem, self.start + self.n)

    def mark(self, ins):
        ins.then_inc(self.sem, 1)
        self.n += 1

    def settle(self):
        self.eng.wait_ge(self.sem, self.start + self.n)


def quantise_e4m3fn(v, steps, values, spare, spare2, out):
    steps(v.tensor_scalar(spare.bitcast(I32), values.bitcast(I32), 0x7F800000, None, ALU.bitwise_and))
    steps(v.tensor_scalar(spare, spare, 2.0 ** -6, 1.5 * 2.0 ** 20, ALU.max, ALU.mult))
    steps(v.tensor_tensor(spare2, values, spare, ALU.add))
    steps(v.tensor_tensor(out, spare2, spare, ALU.subtract))


def hold(eng, passed):
    eng.sem_inc(passed, 1)

def _sb(nc, ctx, name, shape, dt=F32):
    return ctx.enter_context(nc.sbuf_tensor(name, shape, dt))


def _sem(nc, ctx, name):
    return ctx.enter_context(nc.semaphore(name))


def emit_setup(nc, g):
    with ExitStack() as ctx:
        def sb(name, shape, dt=F32):
            return _sb(nc, ctx, name, shape, dt)
        wraw = sb("wraw", [P, 4, 2, D])
        kraw = sb("kraw", [P, 2, D], BF16)
        kval, ktmp, ktmp2 = sb("kval", [P, 2 * D]), sb("ktmp", [P, 2 * D]), sb("ktmp2", [P, 2 * D])
        srow = sb("srow", [1, 8])
        brow = sb("brow", [1, D], BF16)
        ones_r = sb("ones_r", [1, P])
        ones_rb = sb("ones_rb", [1, P], BF16)
        t = sb("t", [P, 32])
        w_in, s_in, k_in = (_sem(nc, ctx, n) for n in ("w_in", "s_in", "k_in"))
        consts, wt_ps, sc_ps, wt_done = (_sem(nc, ctx, n) for n in ("consts", "wt_ps", "sc_ps", "wt_done"))
        v_steps, a_steps, to_act, to_dve, g_steps = (
            _sem(nc, ctx, n) for n in ("v_steps", "a_steps", "to_act", "to_dve", "g_steps"))

        with nc.Block() as block:
            @block.sync
            def _(sp):
                for k, a in enumerate((g.log_c, g.beta, g.attention_bias, g.input_scale, g.kernel_scale)):
                    sp.dma_start(srow[0:1, k:k + 1], a.rearrange("(a n) -> a n", a=1)).then_inc(s_in, 16)
                sp.dma_start(brow[:, :], g.ffn_bias.rearrange("(a n) -> a n", a=1)).then_inc(s_in, 16)
                for k, w in enumerate((g.W_q, g.W_k, g.W_v, g.W_o)):
                    sp.dma_start(wraw[:, k], w.rearrange("(c p) d -> p c d", p=P)).then_inc(w_in, 16)
                sp.dma_start(kraw[:, :, :], g.ffn_w.rearrange("(c p) d -> p c d", p=P)).then_inc(k_in, 16)

            @block.gpsimd
            def _(pool):
                step = Steps(pool, g_steps, 0)
                step.mark(pool.memset(g.ident[:, :], 0.0))
                step.mark(pool.memset(g.ident_b[:, :], 0.0))
                step.mark(pool.memset(g.sel[:, :], 0.0))
                pool.memset(ones_r[:, :], 1.0).then_inc(consts, 1)
                pool.memset(ones_rb[:, :], 1.0).then_inc(consts, 1)
                step.settle()
                for m in (g.ident, g.ident_b):
                    pool.affine_select(out=m[:, :], in_=m[:, :], compare_op=ALU.not_equal, fill=1.0, base=0,
                                       pattern=[[-1, P]], channel_multiplier=1).then_inc(consts, 1)
                for part in range(3):
                    ins = pool.affine_select(out=g.sel[:, :], in_=g.sel[:, :], compare_op=ALU.not_equal, fill=1.0,
                                             base=-(RU * Q_PARTS.index(part) + RU - 1), pattern=[[0, P]],
                                             channel_multiplier=1)
                    if part < 2:
                        step(ins)
                    else:
                        ins.then_inc(consts, 1)

            @block.tensor
            def _(pe):
                pe.wait_ge(consts, 5)
                pe.wait_ge(s_in, 16 * 6)
                pe.matmul(g.ps[:, 0, 0:5], ones_r[:, :], srow[:, 0:5], start=True, stop=True).then_inc(sc_ps, 1)
                pe.matmul(g.ps[:, 1, 0:D], ones_rb[:, :], brow[:, :], start=True, stop=True).then_inc(sc_ps, 1)
                pe.wait_ge(w_in, 16 * 4)
                for k in range(4):
                    for oc in range(2):
                        for dc in range(2):
                            ins = pe.transpose(g.ps[:, 2 + k, dc * D + oc * P:dc * D + oc * P + P],
                                               wraw[:, k, oc, dc * P:(dc + 1) * P], g.ident[:, :])
                    ins.then_inc(wt_ps, 1)

            @block.scalar
            def _(act):
                def do(n, *a, **k):
                    act.wait_ge(to_act, n)
                    act.activation(*a, **k).then_inc(to_dve, 1)
                act.preload_act_table_set(ACT_SET)
                do(1, t[:, 8:10], t[:, 6:8], ACT.Exp)
                act.wait_ge(to_dve, 1)
                act.activation(t[:, 10:12], t[:, 8:10], ACT.Ln, bias=1.0).then_inc(to_dve, 1)
                do(2, t[:, 12:13], g.C_SP, ACT.Ln)
                act.wait_ge(to_dve, 3)
                act.activation(t[:, 13:14], t[:, 12:13], ACT.Exp, scale=0.5).then_inc(to_dve, 1)
                do(3, t[:, 16:17], t[:, 15:16], ACT.Ln, bias=1.0)
                act.activation(t[:, 17:18], t[:, 15:16], ACT.Ln, scale=-1.0, bias=1.0).then_inc(to_dve, 1)
                act.activation(g.EAB, t[:, 18:19], ACT.Exp).then_inc(to_dve, 1)
                for k in range(4):
                    act.wait_ge(wt_ps, k + 1)
                    dst = g.wT[:, :, k * D:(k + 1) * D] if k < 3 else g.woT[:, :, :]
                    act.activation(dst, g.ps[:, 2 + k, :].rearrange("p (c o) -> p c o", c=2),
                                   ACT.Copy).then_inc(wt_done, 1)

            @block.vector
            def _(v):
                step = Steps(v, v_steps, 0)
                v.wait_ge(sc_ps, 2)
                step(v.tensor_copy(t[:, 0:5], g.ps[:, 0, 0:5]))
                v.tensor_copy(g.bias_b[:, :], g.ps[:, 1, 0:D])
                step(v.tensor_scalar(t[:, 20:22], t[:, 0:2], -1.0, None, ALU.mult))
                v.tensor_tensor(t[:, 6:8], t[:, 0:2], t[:, 20:22], ALU.min).then_inc(to_act, 1)
                step(v.tensor_scalar(t[:, 22:24], t[:, 0:2], 0.0, None, ALU.max))
                v.wait_ge(to_dve, 2)
                v.tensor_tensor(g.sc[:, 0:2], t[:, 22:24], t[:, 10:12], ALU.add).then_inc(to_act, 1)
                v.wait_ge(to_act, 2)
                v.wait_ge(to_dve, 4)
                step(v.reciprocal(t[:, 24:25], t[:, 13:14]))
                step(v.tensor_scalar(t[:, 25:26], t[:, 24:25], g.C_SP, t[:, 13:14], ALU.mult, ALU.add))
                step(v.tensor_scalar(g.SQC, t[:, 25:26], 0.5, None, ALU.mult))
                step(v.reciprocal(g.ISQC, g.SQC))
                step(v.tensor_scalar(g.NEGB, g.C_BP, g.ISQC, -1.0, ALU.mult, ALU.mult))
                step(v.tensor_scalar(g.M2SC, g.SQC, -2.0, None, ALU.mult))
                step(v.tensor_scalar(t[:, 19:20], t[:, 2:3], -1.0, None, ALU.mult))
                step(v.tensor_tensor(t[:, 18:19], t[:, 19:20], t[:, 19:20], ALU.subtract))
                step(v.tensor_scalar(t[:, 14:15], g.ISQC, -EPS, None, ALU.add))
                v.tensor_scalar(t[:, 15:16], t[:, 14:15], g.SQC, None, ALU.mult).then_inc(to_act, 1)
                v.wait_ge(to_dve, 7)
                step(v.tensor_tensor(t[:, 26:27], t[:, 16:17], t[:, 17:18], ALU.subtract))
                step(v.tensor_scalar(g.ZS, t[:, 26:27], g.ISQC, 0.5, ALU.mult, ALU.mult))
                step(v.reciprocal(g.INV_SIN, t[:, 3:4]))
                step(v.reciprocal(g.INV_SK, t[:, 4:5]))
                step(v.tensor_scalar(g.S_OUT, t[:, 3:4], t[:, 4:5], None, ALU.mult))
                v.wait_ge(k_in, 16)
                step(v.tensor_scalar(kval[:, :], kraw[:, :, :].rearrange("p c d -> p (c d)"), g.INV_SK, None,
                                     ALU.mult))
                quantise_e4m3fn(v, step, kval[:, :], ktmp[:, :], ktmp2[:, :], kval[:, :])
                step(v.tensor_scalar(ktmp[:, :], kval[:, :], 3.4028234e38 / 460.0, 0.0, ALU.mult, ALU.mult))
                step(v.tensor_tensor(g.kq[:, :, :].rearrange("p c d -> p (c d)"), kval[:, :], ktmp[:, :], ALU.add))
                step(v.memset(g.run_max[:, :], -3.0e38))


def emit_project(nc, g):
    with ExitStack() as ctx:
        def sb(name, shape, dt=F32):
            return _sb(nc, ctx, name, shape, dt)
        STEPS_PROJECT = 38
        xt = sb("xt", [P, 2, GT, D])
        xn = sb("xn", [P, GT, D])
        stats, mv = sb("stats", [P, GT, 6]), sb("mv", [P, GT, 2])
        veps, lnv, rstd, rtmp = (sb(n, [P, GT]) for n in ("veps", "lnv", "rstd", "rtmp"))
        xnT = sb("xnT", [P, 2, GTOK])
        qkv = sb("qkv", [P, GT, 3 * H, DH])
        sq = sb("sq", [P, GT, 3 * H, DH])
        ss, lnss, y, y2 = (sb(n, [P, GT, 3 * H]) for n in ("ss", "lnss", "y", "y2"))
        nrm, e, rp, tn, tt, f, a, kf = (sb(n, [P, GT, 2 * H]) for n in ("nrm", "e", "rp", "tn", "tt", "f", "a", "kf"))
        vg = sb("vg", [P, GT, H])
        qk_rows = sb("qk_rows", [P, 2, GT, H, 32])
        v_rows = sb("v_rows", [P, HG, GT, HPG, VW])
        parts = sb("parts", [P, 3, 2, HG, GTOK], BF16)
        rest = sb("rest", [P, 2, HG, GTOK])
        amax = sb("amax", [P, 3, 2 * H])
        amax_r, prod = sb("amax_r", [2 * H, 1]), sb("prod", [1, 3 * H])
        opens = sb("opens", [1, HG], I32)
        (var_rdy, rs0_rdy, xn_rdy, xT_ps, xT_rdy, qkv_ps, qkv_free, sq_rdy, ss_rdy, y0_rdy,
         n_rdy, e_rdy, rows_rdy, t_ps, v_out, T_out, d_steps, a1, vrow_rdy) = (
            _sem(nc, ctx, n) for n in (
                "var_rdy", "rs0_rdy", "xn_rdy", "xT_ps", "xT_rdy", "qkv_ps", "qkv_free",
                "sq_rdy", "ss_rdy", "y0_rdy", "n_rdy", "e_rdy", "rows_rdy", "t_ps", 
                "v_out", "T_out", "pd_steps", "pa_steps", "vrow_rdy"))

        (hi_rdy, rest_rdy, mid_rdy, low_rdy, amax_rdy, am_ps, open_rdy, open_out) = (
            _sem(nc, ctx, "pr_" + n) for n in ("hi", "rest", "mid", "low", "amax", "am_ps", "open", "open_out"))
        x_in = [_sem(nc, ctx, f"x_in{u}") for u in range(2)]
        passed_v, passed_sp, passed_pe = (_sem(nc, ctx, "pr_passed_" + n) for n in ("v", "sp", "pe"))

        with nc.Block() as block:
            @block.sync
            def _(sp):
                sp.dma_start(xt[:, 0], g.x_g[0]).then_inc(x_in[0], 16)

                def group(i, u, last=False):
                    j = 2 * i + u
                    if not last:
                        sp.wait_ge(xn_rdy, j + 1)
                        hold(sp, passed_sp)
                        sp.dma_start(xt[:, 1 - u],
                                     g.x_g[bass.ds(j + 1, 1)].rearrange("a p t d -> (a p) t d")).then_inc(x_in[1 - u], 16)
                    sp.wait_ge(low_rdy, 8 * (j + 1) + 1)
                    hold(sp, passed_sp)
                    for n, dst in ((0, g.qT_d), (1, g.kT_d)):
                        for part in range(3):
                            sp.dma_start(dst[bass.ds(4 * i, HG), part, :, u * GTOK:(u + 1) * GTOK].rearrange(
                                "g p t -> p g t"), parts[:, part, n]).then_inc(T_out, 16)
                    sp.wait_ge(vrow_rdy, j + 1)
                    hold(sp, passed_sp)
                    for hg in range(HG):
                        sp.dma_start(g.v_d[bass.ds(4 * i + hg, 1), u * GTOK:(u + 1) * GTOK, :].rearrange(
                            "b (t p) f -> p (b t) f", p=P),
                            v_rows[:, hg].rearrange("p t h w -> p t (h w)")).then_inc(v_out, 16)
                    if u == 1:
                        sp.wait_ge(open_rdy, i + 1)
                        hold(sp, passed_sp)
                        sp.dma_start(g.open_d[bass.ds(i, 1), :], opens[:, :]).then_inc(open_out, 16)
                with sp.Fori(0, NG // 2 - 1) as i:
                    group(i, 0)
                    group(i, 1)
                group(NG // 2 - 1, 0)
                group(NG // 2 - 1, 1, last=True)
                sp.wait_ge(T_out, 96 * (NG + 1))
                sp.wait_ge(open_out, 16 * (B + 1))
                sp.wait_ge(v_out, 64 * (NG + 1))

            @block.gpsimd
            def _(pool):
                pool.sem_inc(low_rdy, 1)

                def group(i, u):
                    j = 2 * i + u
                    for m in range(8):
                        if m % 4 == 0:
                            pool.wait_ge(mid_rdy, 2 * j + m // 4 + 1)
                        pool.tensor_tensor(parts[:, 2, m // 4, m % 4, :], rest[:, m // 4, m % 4, :],
                                           parts[:, 1, m // 4, m % 4, :], ALU.subtract).then_inc(low_rdy, 1)
                with pool.Fori(0, NG // 2) as i:
                    group(i, 0)
                    group(i, 1)

            @block.tensor
            def _(pe):
                pe.sem_inc(xT_ps, 1)
                pe.sem_inc(t_ps, 1)

                def group(i, u):
                    j = 2 * i + u
                    pe.wait_ge(xn_rdy, j + 2)
                    for dc in range(2):
                        for t in range(GT):
                            ins = pe.transpose(g.ps[:, dc, t * P:(t + 1) * P], xn[:, t, dc * P:(dc + 1) * P],
                                               g.ident[:, :])
                        ins.then_inc(xT_ps, 1)
                    pe.wait_ge(xT_rdy, 2 * (j + 1))
                    for t in range(GT):
                        pe.wait_ge(qkv_free, 2 * (4 * j + t) + 2)
                        for dc in range(2):
                            for half in range(2):
                                ins = pe.matmul(g.ps[:, 2 + 2 * (t % 2) + half, 0:384],
                                                xnT[:, dc, t * P:(t + 1) * P],
                                                g.wT[:, dc, half * 384:(half + 1) * 384],
                                                start=dc == 0, stop=dc == 1)
                        ins.then_inc(qkv_ps, 1)
                    pe.wait_ge(rows_rdy, j + 1)
                    for n in range(2):
                        for hg in range(HG):
                            m = 4 * n + hg
                            pe.wait_ge(rest_rdy, 8 * j + m + 1)
                            for t in range(GT):
                                ins = pe.transpose(
                                    g.ps[:, 6 + m % 2, t * P:(t + 1) * P],
                                    qk_rows[:, n, t, hg * HPG:(hg + 1) * HPG, :].rearrange("p h r -> p (h r)"),
                                    g.ident[:, :])
                            ins.then_inc(t_ps, 1)
                    if u == 1:
                        pe.wait_ge(amax_rdy, 2 * i + 1)
                        pe.transpose(g.ps[0:2 * H, 0, 0:P], amax[:, 2, :], g.ident[:, :]).then_inc(am_ps, 1)
                        pe.wait_ge(amax_rdy, 2 * i + 2)
                        hold(pe, passed_pe)
                        pe.transpose(g.ps[0:1, 1, 0:2 * H], amax_r[:, :], g.ident[0:2 * H, 0:2 * H]).then_inc(am_ps, 1)
                with pe.Fori(0, NG // 2) as i:
                    group(i, 0)
                    group(i, 1)

            @block.scalar
            def _(act):
                act.preload_act_table_set(ACT_SET)
                act.sem_inc(qkv_free, 4)
                act.sem_inc(T_out, 96)

                def group(i, u):
                    j = 2 * i + u
                    step = Steps(act, a1, 2 * j)
                    act.wait_ge(var_rdy, j + 1)
                    step(act.activation(lnv[:, :], veps[:, :], ACT.Ln))
                    act.activation(rstd[:, :], lnv[:, :], ACT.Exp, scale=-0.5).then_inc(rs0_rdy, 1)
                    for dc in range(2):
                        act.wait_ge(xT_ps, 2 * j + dc + 2)
                        act.activation(xnT[:, dc, :], g.ps[:, dc, :], ACT.Copy).then_inc(xT_rdy, 1)
                    for t in range(GT):
                        act.wait_ge(qkv_ps, 4 * j + t + 1)
                        src = g.ps[:, 2 + 2 * (t % 2):4 + 2 * (t % 2), 0:384]
                        act.activation(sq[:, t].rearrange("p (a h) d -> p a (h d)", a=2), src,
                                       ACT.Square).then_inc(qkv_free, 1)
                        act.activation(qkv[:, t].rearrange("p (a h) d -> p a (h d)", a=2), src,
                                       ACT.Copy).then_inc(qkv_free, 1)
                    act.wait_ge(ss_rdy, j + 1)
                    step(act.activation(lnss[:, :, :], ss[:, :, :], ACT.Ln))
                    act.activation(y[:, :, :], lnss[:, :, :], ACT.Exp, scale=-0.5).then_inc(y0_rdy, 1)
                    act.wait_ge(n_rdy, j + 1)
                    act.activation(e[:, :, :], nrm[:, :, :], ACT.Exp, scale=g.M2SC).then_inc(e_rdy, 1)
                    for m in range(8):
                        act.wait_ge(t_ps, 8 * j + m + 2)
                        if m == 0:
                            act.wait_ge(T_out, 96 * (j + 1))
                        act.activation(parts[:, 0, m // 4, m % 4, :], g.ps[:, 6 + m % 2, :], ACT.Copy).then_inc(hi_rdy, 1)
                    for n in range(2):
                        act.wait_ge(rest_rdy, 8 * j + 4 * n + 6)
                        act.activation(parts[:, 1, n], rest[:, n], ACT.Copy).then_inc(mid_rdy, 1)
                with act.Fori(0, NG // 2) as i:
                    group(i, 0)
                    group(i, 1)

            @block.vector
            def _(v):
                v.sem_inc(xn_rdy, 1)
                v.sem_inc(v_out, 64)
                v.sem_inc(rest_rdy, 2)
                v.sem_inc(open_out, 16)
                v.memset(qk_rows[:, :, :, :, :], 0.0).then_inc(d_steps, 1)
                v.wait_ge(d_steps, 1)
                v.memset(qk_rows[:, 0, :, :, 16:17], 1.0).then_inc(d_steps, 1)
                for hg in range(HG):
                    v.tensor_scalar(v_rows[:, hg, :, :, DH:DH + 1], qk_rows[:, 0, :, 0:HPG, 17:18], g.EAB, None,
                                    ALU.add).then_inc(d_steps, 1)
                v.wait_ge(d_steps, 2 + HG)

                def group(i, u):
                    j = 2 * i + u
                    step = Steps(v, d_steps, 2 + HG + i * (2 * STEPS_PROJECT + 3) + u * STEPS_PROJECT)
                    v.wait_ge(x_in[u], 16 * (i + 1))
                    for t in range(GT):
                        step.mark(v.bn_stats(stats[:, t, :], xt[:, u, t, :]))
                    step.settle()
                    hold(v, passed_v)
                    for t in range(GT):
                        step.mark(v.bn_aggr(mv[:, t, :], stats[:, t, :]))
                    step.settle()
                    v.tensor_scalar(veps[:, :], mv[:, :, 1], EPS, None, ALU.add).then_inc(var_rdy, 1)
                    v.wait_ge(rs0_rdy, j + 1)
                    v.wait_ge(var_rdy, j + 1)
                    step(v.tensor_tensor(rtmp[:, :], rstd[:, :], rstd[:, :], ALU.mult))
                    step(v.tensor_tensor(rtmp[:, :], rtmp[:, :], veps[:, :], ALU.mult))
                    step(v.tensor_scalar(rtmp[:, :], rtmp[:, :], -0.5, 1.5, ALU.mult, ALU.add))
                    step(v.tensor_tensor(rstd[:, :], rstd[:, :], rtmp[:, :], ALU.mult))
                    v.wait_ge(xT_ps, 2 * j + 1)
                    for t in range(GT):
                        ins = v.tensor_scalar(xn[:, t, :], xt[:, u, t, :], mv[:, t, 0:1], rstd[:, t:t + 1],
                                              ALU.subtract, ALU.mult)
                    ins.then_inc(xn_rdy, 1)
                    for t in range(GT):
                        v.wait_ge(qkv_free, 4 + 2 * (4 * j + t) + 2)
                        step.mark(v.tensor_reduce(ss[:, t, :], sq[:, t, :, :], AX.X, ALU.add))
                    step.settle()
                    v.tensor_scalar(ss[:, :, :], ss[:, :, :], EPS * EPS, None, ALU.max).then_inc(ss_rdy, 1)
                    v.wait_ge(y0_rdy, j + 1)
                    v.wait_ge(ss_rdy, j + 1)
                    step(v.tensor_tensor(y2[:, :, :], y[:, :, :], y[:, :, :], ALU.mult))
                    step(v.tensor_tensor(y2[:, :, :], y2[:, :, :], ss[:, :, :], ALU.mult))
                    step(v.tensor_scalar(y2[:, :, :], y2[:, :, :], -0.5, 1.5, ALU.mult, ALU.add))
                    step(v.tensor_tensor(y[:, :, :], y[:, :, :], y2[:, :, :], ALU.mult))
                    yqk, ssqk = y[:, :, 0:2 * H], ss[:, :, 0:2 * H]
                    v.tensor_tensor(nrm[:, :, :], ssqk, yqk, ALU.mult).then_inc(n_rdy, 1)
                    step(v.tensor_scalar(vg[:, :, :], y[:, :, 2 * H:], g.ZS, 1.0, ALU.mult, ALU.min))
                    step(v.tensor_scalar(vg[:, :, :], vg[:, :, :], g.EAB, None, ALU.mult))
                    v.wait_ge(v_out, 64 * (j + 1))
                    for hg in range(HG):
                        step.mark(v.tensor_tensor(
                            v_rows[:, hg, :, :, 0:DH], qkv[:, :, 2 * H + hg * HPG:2 * H + (hg + 1) * HPG, :],
                            vg[:, :, hg * HPG:(hg + 1) * HPG].unsqueeze(3).broadcast_to([P, GT, HPG, DH]), ALU.mult))
                    v.wait_ge(e_rdy, j + 1)
                    step(v.tensor_scalar(rp[:, :, :], e[:, :, :], 1.0, None, ALU.add))
                    step(v.reciprocal(rp[:, :, :], rp[:, :, :]))
                    step.mark(v.tensor_scalar(tn[:, :, :], e[:, :, :], -1.0, 1.0, ALU.mult, ALU.add))
                    step(v.tensor_tensor(a[:, :, :], e[:, :, :], rp[:, :, :], ALU.mult))
                    step.mark(v.tensor_tensor(tn[:, :, :], tn[:, :, :], rp[:, :, :], ALU.mult))
                    step(v.tensor_tensor(a[:, :, :], a[:, :, :], rp[:, :, :], ALU.mult))
                    step.mark(v.tensor_tensor(tt[:, :, :], tn[:, :, :], tn[:, :, :], ALU.mult))
                    step.mark(v.tensor_tensor(f[:, :, :], tn[:, :, :], yqk, ALU.mult))
                    step(v.tensor_scalar(a[:, :, :], a[:, :, :], 4.0, A_FLOOR, ALU.mult, ALU.max))
                    step(v.reciprocal(rp[:, :, :], a[:, :, :]))
                    step(v.scalar_tensor_tensor(kf[:, :, H:], f[:, :, H:], 2.0, rp[:, :, H:], ALU.mult, ALU.mult))
                    rq, rk = qk_rows[:, 0], qk_rows[:, 1]
                    v.wait_ge(t_ps, 8 * j + 1)
                    v.tensor_tensor(rq[:, :, :, 0:DH], qkv[:, :, 0:H, :],
                                    f[:, :, 0:H].unsqueeze(3).broadcast_to([P, GT, H, DH]), ALU.mult)
                    v.tensor_tensor(rk[:, :, :, 0:DH], qkv[:, :, H:2 * H, :],
                                    kf[:, :, H:].unsqueeze(3).broadcast_to([P, GT, H, DH]), ALU.mult)
                    v.tensor_copy(rq[:, :, :, 17], tt[:, :, 0:H])
                    v.tensor_copy(rq[:, :, :, 18], rp[:, :, 0:H])
                    v.scalar_tensor_tensor(rk[:, :, :, 16], tt[:, :, H:], -1.0, rp[:, :, H:], ALU.mult, ALU.mult)
                    v.tensor_scalar(rk[:, :, :, 17], rp[:, :, H:], -1.0, None, ALU.mult).then_inc(rows_rdy, 1)
                    for hg in range(HG):
                        ins = v.tensor_scalar(v_rows[:, hg, :, :, DH + 1], a[:, :, H + hg * HPG:H + (hg + 1) * HPG],
                                              1.0 / EPS, None, ALU.mult)
                    ins.then_inc(vrow_rdy, 1)
                    for m in range(8):
                        v.wait_ge(hi_rdy, 8 * j + m + 1)
                        if m == 0:
                            v.wait_ge(low_rdy, 8 * j + 1)
                        v.tensor_tensor(rest[:, m // 4, m % 4, :], g.ps[:, 6 + m % 2, :], parts[:, 0, m // 4, m % 4, :],
                                        ALU.subtract).then_inc(rest_rdy, 1)
                    step(v.tensor_reduce(amax[:, u, :], a[:, :, :].rearrange("p t h -> p h t"), AX.X, ALU.max))
                    if u == 1:
                        v.tensor_tensor(amax[:, 2, :], amax[:, 0, :], amax[:, 1, :], ALU.max).then_inc(amax_rdy, 1)
                        v.wait_ge(am_ps, 2 * i + 1)
                        v.tensor_reduce(amax_r[:, :], g.ps[0:2 * H, 0, 0:P], AX.X, ALU.max).then_inc(amax_rdy, 1)
                        v.wait_ge(am_ps, 2 * i + 2)
                        step(v.tensor_copy(prod[:, 0:2 * H], g.ps[0:1, 1, 0:2 * H]))
                        step(v.tensor_tensor(prod[:, 2 * H:], prod[:, 0:H], prod[:, H:2 * H], ALU.mult))
                        step(v.tensor_reduce(prod[:, 0:HG], prod[:, 2 * H:].rearrange("p (g h) -> p g h", g=HG), AX.X,
                                             ALU.max))
                        v.wait_ge(open_out, 16 * (i + 1))
                        v.tensor_scalar(opens[:, :], prod[:, 0:HG], EPS, None, ALU.is_gt).then_inc(open_rdy, 1)
                    assert step.n == STEPS_PROJECT + 3 * u, step.n
                with v.Fori(0, NG // 2) as i:
                    group(i, 0)
                    group(i, 1)


def emit_attend(nc, g):
    with ExitStack() as ctx:
        def sb(name, shape, dt=F32):
            return _sb(nc, ctx, name, shape, dt)
        qS = sb("qS", [P, 2, HPG, S], BF16)
        kS = sb("kS", [P, 2, HPG, S], BF16)
        vt = sb("vt", [P, 2, KT, HPG, VW])
        opens = sb("opens_all", [1, NJ], I32)
        rqb = sb("rqb", [P, HPG, S])
        M = sb("M", [P, HPG, GTOK])
        U = sb("U", [P, 4, HPG, GTOK])
        W = sb("W", [P, 2, HPG, GTOK])
        OTs = sb("OTs", [P, 2, GTOK])
        Os = sb("Os", [P, 2, GT, HPG, OW])
        cm = sb("cm", [P, 4 * QPJ])
        red, ones_c = sb("red", [P, 2]), sb("ones_c", [P, 1])
        names = ("d_rdy", "ttr_done", "ln_done", "exp_done", "pv_done", "bc_rdy", "rqb_rdy", "m_rdy",
                 "ot_free", "tb_rdy", "os_rdy", "max_steps", "zeroed", "opens_in")
        (d_rdy, ttr_done, ln_done, exp_done, pv_done, bc_rdy, rqb_rdy, m_rdy, ot_free, tb_rdy, os_rdy,
         max_steps, zeroed, opens_in) = (_sem(nc, ctx, "at_" + n) for n in names)
        passed_v, passed_sp = (_sem(nc, ctx, "at_passed_" + n) for n in ("v", "sp"))
        in_rdy = [_sem(nc, ctx, f"at_in{u}") for u in range(2)]
        o_out = [_sem(nc, ctx, f"at_o_out{h}") for h in range(2)]
        NB = NJ // 2
        SLOTS = 2 * QPJ
        IN_UNIT = 16 * (2 * len(Q_PARTS) + 1)

        def split(q):
            return (q // QPJ) % 2, (q % QPJ) // KT, q % KT

        def run(body, eng):
            body(0, first=True)
            with eng.Fori(1, NB - 1) as i:
                body(i)
            body(NB - 1, last=True)

        with nc.Block() as block:
            @block.sync
            def _(sp):
                def load(j, u):
                    for buf, d, order in ((qS, g.qT_d, Q_PARTS), (kS, g.kT_d, K_PARTS)):
                        rows = d.rearrange("j c (h r) s -> j c r h s", h=HPG)
                        for n, part in enumerate(order):
                            sp.dma_start(buf[n * RU:(n + 1) * RU, u], rows[bass.ds(j, 1), part, 0:RU].rearrange(
                                "a r h s -> (a r) h s")).then_inc(in_rdy[u], 16)
                    sp.dma_start(vt[:, u].rearrange("p k h w -> p k (h w)"),
                                 g.v_d[bass.ds(j, 1)].rearrange("a (k p) f -> p (a k) f", p=P)).then_inc(in_rdy[u], 16)

                def store(j, qh):
                    sp.wait_ge(os_rdy, 2 * j + qh + 2)
                    hold(sp, passed_sp)
                    sp.dma_start(g.o_d[bass.ds(j, 1), qh * GTOK:(qh + 1) * GTOK, :].rearrange(
                        "a (t p) f -> p (a t) f", p=P), Os[:, qh].rearrange("p t h w -> p t (h w)")).then_inc(o_out[qh], 16)

                def body(i, first=False, last=False):
                    for u in range(2):
                        j = 2 * i + u
                        if not (last and u == 1):
                            sp.wait_ge(pv_done, QPJ * j + 2)
                            hold(sp, passed_sp)
                            sp.wait_ge(ttr_done, 2 * QPJ * j + 2)
                            hold(sp, passed_sp)
                            load(j + 1, 1 - u)
                        if not (first and u == 0):
                            store(j - 1, 1)
                        store(j, 0)
                sp.dma_start(opens[:, :], g.open_d.rearrange("(a b) g -> a (b g)", a=1)).then_inc(opens_in, 16)
                load(0, 0)
                run(body, sp)
                store(NJ - 1, 1)
                for qh in range(QH):
                    sp.wait_ge(o_out[qh], 16 * NJ)

            @block.tensor
            def _(pe):
                pe.sem_inc(pv_done, 2)
                pe.wait_ge(opens_in, 16)

                def distances(i, s):
                    u, qh, kt = split(s)
                    for pair in range(2):
                        pe.wait_ge(ttr_done, 2 * (SLOTS * i + s) + pair + 1)
                        for h in (2 * pair, 2 * pair + 1):
                            ins = pe.matmul(g.ps[:, h, :], kS[0:RS, u, h, kt * P:(kt + 1) * P],
                                            qS[0:RS, u, h, qh * GTOK:(qh + 1) * GTOK], start=True, stop=True)
                        ins.then_inc(d_rdy, 1)

                def values(i, q):
                    u, qh, kt = split(q)
                    n = SLOTS * i + q
                    pe.wait_ge(exp_done, n + 5)
                    if kt == 0:
                        pe.wait_ge(ot_free, (SLOTS // KT) * i + q // KT + 1)
                    for h in range(HPG):
                        ins = pe.matmul(g.ps[32 * h:32 * h + OW, 4 + qh, :], vt[:, u, kt, h, 0:OW], W[:, q % 2, h, :],
                                        start=kt == 0, stop=kt == KT - 1)
                    ins.then_inc(pv_done, 1)

                def to_token_rows(x, qh):
                    pe.wait_ge(ot_free, x + 3)
                    pe.wait_ge(os_rdy, x + 1)
                    for t in range(GT):
                        ins = pe.transpose(g.ps[:, 6, t * P:(t + 1) * P], OTs[:, qh, t * P:(t + 1) * P], g.ident[:, :])
                    ins.then_inc(tb_rdy, 1)

                def spread_rq(i, u):
                    j = 2 * i + u
                    is_open = pe.value_load(opens[0:1, bass.ds(j, 1)], min_val=0, max_val=1)
                    with pe.If(is_open > 0):
                        for c in range(2 * HPG):
                            pe.wait_ge(rqb_rdy, 2 * HPG * j + c + 1)
                            pe.matmul(g.ps[:, 7, :], g.sel[0:RS, :], qS[0:RS, u, c // 2, (c % 2) * GTOK:(c % 2 + 1) * GTOK],
                                      start=True, stop=True).then_inc(bc_rdy, 1)
                    with pe.Else():
                        pe.sem_inc(bc_rdy, 2 * HPG)

                def body(i, first=False, last=False):
                    for s in range(SLOTS + (3 if last else 0)):
                        k, u = s % QPJ, (s // QPJ) % 2
                        if s < SLOTS:
                            if k == 0:
                                pe.wait_ge(in_rdy[u], IN_UNIT * (i + 1))
                                spread_rq(i, u)
                            distances(i, s)
                        if s >= 3 or not first:
                            values(i, s - 3)
                        if s < SLOTS:
                            if k == 13:
                                to_token_rows(4 * i + 2 * u, 0)
                            if k == 5 and (s >= QPJ or not first):
                                to_token_rows(4 * i + 2 * u - 1, 1)
                run(body, pe)
                to_token_rows(2 * NJ - 1, 1)
                pe.wait_ge(max_steps, 2 * NB + 3)
                pe.matmul(g.ps[0:1, 7, 0:1], red[:, 0:1], ones_c[:, :], start=True, stop=True).then_inc(bc_rdy, 1)

            @block.scalar
            def _(act):
                act.preload_act_table_set(ACT_SET)
                act.sem_inc(exp_done, 4)

                def log(i, s):
                    act.wait_ge(ttr_done, 2 * (SLOTS * i + s) + 4)
                    act.activation(U[:, s % 4], U[:, s % 4], ACT.Ln, scale=-2.0, bias=1.0).then_inc(ln_done, 1)

                def power(i, q):
                    n = SLOTS * i + q
                    act.wait_ge(ln_done, n + 1)
                    act.wait_ge(pv_done, n + 1)
                    act.activation(W[:, q % 2], U[:, q % 4], ACT.Exp, scale=g.NEGB).then_inc(exp_done, 1)

                def body(i, first=False, last=False):
                    for s in range(SLOTS + (1 if last else 0)):
                        if s < SLOTS:
                            log(i, s)
                        if s >= 1 or not first:
                            power(i, s - 1)
                run(body, act)

            @block.vector
            def _(v):
                v.sem_inc(ttr_done, 2)
                v.sem_inc(ot_free, 2)
                v.sem_inc(rqb_rdy, 1)
                v.sem_inc(os_rdy, 1)
                v.memset(ones_c[:, :], 1.0)
                v.memset(g.ps[:, 4:6, :], 0.0).then_inc(zeroed, 1)
                v.wait_ge(zeroed, 1)
                v.wait_ge(opens_in, 16)

                def clamp(i, s, is_open):
                    u, qh, kt = split(s)
                    n = SLOTS * i + s
                    v.wait_ge(exp_done, n + 1)
                    v.wait_ge(in_rdy[u], IN_UNIT * (i + 1))
                    if is_open:
                        v.wait_ge(ttr_done, 2 * n + 2)
                        hold(v, passed_v)
                        for h in range(HPG):
                            ins = v.tensor_scalar(M[:, h, :], rqb[:, h, qh * GTOK:(qh + 1) * GTOK],
                                                  vt[:, u, kt, h, DH + 1:DH + 2], None, ALU.min)
                        ins.then_inc(m_rdy, 1)
                    else:
                        v.sem_inc(m_rdy, 1)
                    for pair in range(2):
                        v.wait_ge(d_rdy, 2 * n + pair + 1)
                        v.wait_ge(m_rdy, n + 1)
                        hold(v, passed_v)
                        hs = slice(2 * pair, 2 * pair + 2)
                        factor = M[:, hs, :] if is_open else \
                            vt[:, u, kt, hs, DH + 1:DH + 2].broadcast_to([P, 2, GTOK])
                        v.tensor_tensor_reduce(U[:, s % 4, hs, :], factor, g.ps[:, hs, :], 1.0, -3.0e38,
                                               ALU.mult, ALU.max, cm[:, 2 * s + pair:2 * s + pair + 1]).then_inc(ttr_done, 1)

                def copy_rq(j):
                    for c in range(2 * HPG):
                        v.wait_ge(bc_rdy, 2 * HPG * j + c + 1)
                        v.tensor_copy(rqb[:, c // 2, (c % 2) * GTOK:(c % 2 + 1) * GTOK], g.ps[:, 7, :]).then_inc(rqb_rdy, 1)
                    v.wait_ge(rqb_rdy, 2 * HPG * (j + 1) + 1)

                def copy_sums(x, qh):
                    v.wait_ge(pv_done, KT * x + KT + 2)
                    v.tensor_copy(OTs[:, qh, :], g.ps[:, 4 + qh, :]).then_inc(ot_free, 1)

                def copy_rows(j, qh):
                    v.wait_ge(tb_rdy, 2 * j + qh + 1)
                    v.wait_ge(o_out[qh], 16 * j)
                    v.tensor_copy(Os[:, qh], g.ps[:, 6, :].rearrange("p (t h r) -> p t h r", t=GT, h=HPG)[:, :, :, 0:OW])\
                     .then_inc(os_rdy, 1)

                def unit(i, u, is_open, first):
                    for k in range(QPJ):
                        clamp(i, QPJ * u + k, is_open)
                        if k == 12:
                            copy_sums(4 * i + 2 * u, 0)
                        if k == 15:
                            copy_rows(2 * i + u, 0)
                        if u == 1 or not first:
                            if k == 4:
                                copy_sums(4 * i + 2 * u - 1, 1)
                            if k == 7:
                                copy_rows(2 * i + u - 1, 1)

                def body(i, first=False, last=False):
                    for u in range(2):
                        j = 2 * i + u
                        is_open = v.value_load(opens[0:1, bass.ds(j, 1)], min_val=0, max_val=1)
                        with v.If(is_open > 0):
                            copy_rq(j)
                            unit(i, u, True, first)
                        with v.Else():
                            v.sem_inc(rqb_rdy, 2 * HPG)
                            unit(i, u, False, first)
                    v.wait_ge(ttr_done, 2 * SLOTS * (i + 1) + 2)
                    v.tensor_reduce(red[:, 0:1], cm[:, :], AX.X, ALU.max).then_inc(max_steps, 1)
                    v.wait_ge(max_steps, 2 * i + 1)
                    v.tensor_tensor(g.run_max[:, :], g.run_max[:, :], red[:, 0:1], ALU.max).then_inc(max_steps, 1)
                    v.wait_ge(max_steps, 2 * i + 2)
                run(body, v)
                copy_sums(2 * NJ - 1, 1)
                copy_rows(NJ - 1, 1)
                v.tensor_scalar(red[:, 0:1], g.run_max[:, :], -U_EXACT, None, ALU.is_gt).then_inc(max_steps, 1)
                v.tensor_scalar(red[:, 1:2], g.NEGB, -EXPONENT_MAX / THETA_MAX, None, ALU.is_lt).then_inc(max_steps, 1)
                v.wait_ge(max_steps, 2 * NB + 2)
                v.tensor_tensor(red[:, 0:1], red[:, 0:1], red[:, 1:2], ALU.add).then_inc(max_steps, 1)
                v.wait_ge(bc_rdy, 2 * HPG * NJ + 1)
                v.tensor_copy(g.flag[:, :], g.ps[0:1, 7, 0:1]).then_inc(max_steps, 1)


def emit_general(nc, g):
    with ExitStack() as ctx:
        def sb(name, shape, dt=F32):
            return _sb(nc, ctx, name, shape, dt)
        Qs, Ks = sb("Qs", [P, P], BF16), sb("Ks", [P, S], BF16)
        Vs = sb("Vs", [P, KT, VW])
        ones_s, diag = sb("ones_s", [P, P]), sb("diag", [P, KT, P])
        rqc, low, shift = sb("rqc", [P, 1]), sb("low", [P, 1]), sb("shift", [P, 1])
        X, Z, T = sb("X", [P, S]), sb("Z", [P, S]), sb("T", [P, S])
        WT = sb("WT", [P, KT, P])
        Og = sb("Og", [P, OW])
        gin, p_rdy, v_rdy, a_rdy, gout = (_sem(nc, ctx, "ge_" + n) for n in ("in", "p_rdy", "v_rdy", "a_rdy", "out"))
        passed_sp = _sem(nc, ctx, "ge_passed_sp")
        gv, ga, ga_ones = (_sem(nc, ctx, "ge_" + n) for n in ("v_steps", "a_steps", "ones"))
        GIN = 16 * (2 * len(Q_PARTS) + 1)

        def steps(eng, body, stored=None):
            needed = eng.value_load(g.flag[0:1, 0:1], min_val=0, max_val=2 * P)
            with eng.If(needed > 0):
                with eng.Fori(0, NJ) as j:
                    with eng.Fori(0, HPG) as h:
                        with eng.Fori(0, KT) as t:
                            body(j, h, t, (j * HPG + h) * KT + t)
                if stored is not None:
                    eng.wait_ge(stored, 16 * (NJ * HPG * KT + 1))

        with nc.Block() as block:
            @block.sync
            def _(sp):
                def body(j, h, t, n):
                    sp.wait_ge(gout, 16 * (n + 1))
                    hold(sp, passed_sp)
                    for c, part in enumerate(Q_PARTS):
                        sp.dma_start(Qs[c * RU:(c + 1) * RU, :], g.qT_d[bass.ds(j, 1), part, bass.ds(h * 32, RU),
                                                                     bass.ds(t * P, P)].rearrange(
                            "a r s -> (a r) s")).then_inc(gin, 16)
                    for c, part in enumerate(K_PARTS):
                        sp.dma_start(Ks[c * RU:(c + 1) * RU, :], g.kT_d[bass.ds(j, 1), part, bass.ds(h * 32, RU),
                                                                     :].rearrange(
                            "a r s -> (a r) s")).then_inc(gin, 16)
                    sp.dma_start(Vs[:, :, :], g.v_d[bass.ds(j, 1), :, bass.ds(h * VW, VW)].rearrange(
                        "a (k p) w -> p (a k) w", p=P)).then_inc(gin, 16)
                    sp.wait_ge(v_rdy, 8 * n + 8)
                    hold(sp, passed_sp)
                    sp.dma_start(g.o_d[bass.ds(j, 1), bass.ds(t * P, P), bass.ds(h * OW, OW)].rearrange(
                        "a p w -> (a p) w"), Og[:, :]).then_inc(gout, 16)
                sp.sem_inc(gout, 16)
                steps(sp, body, gout)

            @block.tensor
            def _(pe):
                def body(j, h, t, n):
                    pe.wait_ge(gin, GIN * (n + 1))
                    pe.wait_ge(v_rdy, 8 * n + 1)
                    for half in range(2):
                        ks = slice(half * 512, (half + 1) * 512)
                        pe.matmul(g.ps[:, half, :], Qs[0:RS, :], Ks[0:RS, ks], start=True, stop=True)
                        pe.matmul(g.ps[:, 2 + half, :], ones_s[:, :],
                                  diag[:, 4 * half:4 * half + 4, :].rearrange("p k q -> p (k q)"),
                                  start=True, stop=True)
                    pe.matmul(g.ps[:, 4, 0:1], Qs[0:RS, :], g.sel[0:RS, 0:1], start=True, stop=True).then_inc(p_rdy, 1)
                    pe.wait_ge(a_rdy, 3 * n + 3)
                    for k in range(KT):
                        ins = pe.transpose(g.ps[:, 5 + k // 4, (k % 4) * P:(k % 4 + 1) * P], Z[:, k * P:(k + 1) * P],
                                           g.ident[:, :])
                    ins.then_inc(p_rdy, 1)
                    pe.wait_ge(v_rdy, 8 * n + 7)
                    for k in range(KT):
                        ins = pe.matmul(g.ps[:, 7, 0:OW], WT[:, k, :], Vs[:, k, 0:OW], start=k == 0, stop=k == KT - 1)
                    ins.then_inc(p_rdy, 1)
                steps(pe, body)

            @block.scalar
            def _(act):
                act.preload_act_table_set(ACT_SET)

                def body(j, h, t, n):
                    act.wait_ge(v_rdy, 8 * n + 4)
                    act.activation(T[:, :], Z[:, :], ACT.Ln).then_inc(ga, 1)
                    act.wait_ge(ga, n + 1)
                    act.activation(Z[:, :], T[:, :], ACT.Exp, scale=0.5).then_inc(a_rdy, 1)
                    act.wait_ge(v_rdy, 8 * n + 5)
                    act.activation(X[:, :], T[:, :], ACT.Ln).then_inc(a_rdy, 1)
                    act.wait_ge(v_rdy, 8 * n + 6)
                    act.wait_ge(a_rdy, 3 * n + 2)
                    act.activation(Z[:, :], X[:, :], ACT.Exp, scale=g.NEGB, bias=shift[:, :]).then_inc(a_rdy, 1)
                steps(act, body)

            @block.vector
            def _(v):
                v.memset(ones_s[:, :], 1.0).then_inc(ga_ones, 1)
                v.wait_ge(ga_ones, 1)

                def body(j, h, t, n):
                    step = Steps(v, gv, 6 * n)
                    v.wait_ge(gin, GIN * (n + 1))
                    for k in range(KT):
                        ins = v.tensor_scalar(diag[:, k, :], g.ident[:, :], Vs[:, k, DH + 1:DH + 2], None, ALU.mult)
                    ins.then_inc(v_rdy, 1)
                    v.wait_ge(p_rdy, 3 * n + 1)
                    v.tensor_copy(rqc[:, :], g.ps[:, 4, 0:1]).then_inc(v_rdy, 1)
                    v.wait_ge(v_rdy, 8 * n + 2)
                    step(v.tensor_scalar(T[:, :], g.ps[:, 2:4, :].rearrange("p a k -> p (a k)"), rqc[:, :], None, ALU.min))
                    step(v.tensor_tensor(T[:, :], T[:, :], g.ps[:, 0:2, :].rearrange("p a k -> p (a k)"), ALU.mult))
                    step(v.tensor_scalar(X[:, :], T[:, :], -2.0, 1.0, ALU.mult, ALU.add))
                    v.tensor_scalar(X[:, :], X[:, :], 1.0 + EPS, None, ALU.max).then_inc(v_rdy, 1)
                    v.wait_ge(v_rdy, 8 * n + 3)
                    step(v.tensor_scalar(T[:, :], X[:, :], -1.0, None, ALU.add))
                    v.scalar_tensor_tensor(Z[:, :], X[:, :], 1.0, T[:, :], ALU.add, ALU.mult).then_inc(v_rdy, 1)
                    v.wait_ge(a_rdy, 3 * n + 1)
                    v.tensor_tensor(T[:, :], X[:, :], Z[:, :], ALU.add).then_inc(v_rdy, 1)
                    v.wait_ge(a_rdy, 3 * n + 2)
                    step(v.tensor_reduce(low[:, :], X[:, :], AX.X, ALU.min))
                    step(v.tensor_scalar(shift[:, :], low[:, :], g.NEGB, -1.0, ALU.mult, ALU.mult))
                    v.sem_inc(v_rdy, 1)
                    v.wait_ge(p_rdy, 3 * n + 2)
                    v.tensor_copy(WT[:, :, :].rearrange("p k q -> p (k q)"),
                                  g.ps[:, 5:7, :].rearrange("p a k -> p (a k)")).then_inc(v_rdy, 1)
                    v.wait_ge(p_rdy, 3 * n + 3)
                    v.tensor_copy(Og[:, :], g.ps[:, 7, 0:OW]).then_inc(v_rdy, 1)
                steps(v, body)


def emit_finish(nc, g):
    with ExitStack() as ctx:
        def sb(name, shape, dt=F32):
            return _sb(nc, ctx, name, shape, dt)
        o_in = sb("o_in", [P, 2, HG, GT, HPG, OW])
        xt = sb("xt2", [P, 2, GT, D])
        rs = sb("rs", [P, HG, GT, HPG])
        on, sq = sb("on", [P, GT, H, DH]), sb("osq", [P, GT, H, DH])
        ss, lnss, y, y2 = (sb("o" + n, [P, GT, H]) for n in ("ss", "lnss", "y", "y2"))
        ocT = sb("ocT", [P, 2, GTOK])
        x1 = sb("x1", [P, GT, D])
        stats, mv = sb("stats2", [P, GT, 6]), sb("mv2", [P, GT, 2])
        veps, lnv, rstd, rtmp, rmax = (sb("f" + n, [P, GT]) for n in ("veps", "lnv", "rstd", "rtmp", "rmax"))
        xb, xq = sb("xb", [P, GT, D], BF16), sb("xq", [P, GT, D], BF16)
        vf, sp1, sp2 = (sb(n, [P, GT, D]) for n in ("vf", "spare1", "spare2"))
        xqT = sb("xqT", [P, 2, GTOK], BF16)
        yb, yb2 = sb("yb", [P, GT, D], BF16), sb("yb2", [P, GT, D], BF16)
        res = sb("res", [P, 2, GT, D])
        (on_rdy, osq_rdy, oss_rdy, oy_rdy, oc_rdy, oT_ps, oT_rdy, wo_ps, var_rdy, rs0_rdy, xq_rdy, xqT_ps,
         xqT_rdy, y_ps, yb_rdy, res_rdy, steps_v, steps_a) = (
            _sem(nc, ctx, "fi_" + n) for n in (
                "on", "osq", "oss", "oy", "oc", "oT_ps", "oT_rdy", "wo_ps", "var", "rs0", "xq", "xqT_ps",
                "xqT_rdy", "y_ps", "yb", "res", "steps_v", "steps_a"))
        psb = g.ps[:, 4, :].bitcast(BF16)
        STEPS_FINISH = 29

        in2, res_out = ([_sem(nc, ctx, f"fi_{n}{u}") for u in range(2)] for n in ("in", "out"))
        passed_v, passed_sp = (_sem(nc, ctx, "fi_passed_" + n) for n in ("v", "sp"))

        with nc.Block() as block:
            @block.sync
            def _(sp):
                def load(i, j, u):
                    sp.dma_start(xt[:, u], g.x_g[bass.ds(j, 1)].rearrange("a p t d -> (a p) t d")).then_inc(in2[u], 16)
                    for hg in range(HG):
                        sp.dma_start(o_in[:, u, hg].rearrange("p t h w -> p t (h w)"),
                                     g.o_d[bass.ds(4 * i + hg, 1), u * GTOK:(u + 1) * GTOK, :].rearrange(
                                         "a (t p) f -> p (a t) f", p=P)).then_inc(in2[u], 16)

                def group(i, u, last=False):
                    j = 2 * i + u
                    if not last:
                        sp.wait_ge(res_rdy, j + 1)
                        hold(sp, passed_sp)
                        load(i + u, j + 1, 1 - u)
                    sp.wait_ge(res_rdy, j + 2)
                    hold(sp, passed_sp)
                    sp.dma_start(g.out_g[bass.ds(j, 1)].rearrange("a p t d -> (a p) t d"), res[:, u]).then_inc(res_out[u], 16)
                load(0, 0, 0)
                with sp.Fori(0, NG // 2 - 1) as i:
                    group(i, 0)
                    group(i, 1)
                group(NG // 2 - 1, 0)
                group(NG // 2 - 1, 1, last=True)
                for u in range(2):
                    sp.wait_ge(res_out[u], 8 * NG + 16)

            @block.tensor
            def _(pe):
                pe.sem_inc(xqT_ps, 1)

                def group(i, u):
                    j = 2 * i + u
                    pe.wait_ge(oc_rdy, j + 1)
                    for dc in range(2):
                        for t in range(GT):
                            ins = pe.transpose(g.ps[:, dc, t * P:(t + 1) * P],
                                               on[:, t, dc * 8:(dc + 1) * 8, :].rearrange("p h d -> p (h d)"), g.ident[:, :])
                        ins.then_inc(oT_ps, 1)
                    pe.wait_ge(oT_rdy, 2 * (j + 1))
                    for t in range(GT):
                        for dc in range(2):
                            ins = pe.matmul(g.ps[:, 2 + t // 2, (t % 2) * D:(t % 2 + 1) * D], ocT[:, dc, t * P:(t + 1) * P],
                                            g.woT[:, dc, :], start=dc == 0, stop=dc == 1)
                    ins.then_inc(wo_ps, 1)
                    pe.wait_ge(xq_rdy, j + 1)
                    for dc in range(2):
                        for t in range(GT):
                            ins = pe.transpose(psb[:, dc * GTOK + t * P:dc * GTOK + (t + 1) * P],
                                               xq[:, t, dc * P:(dc + 1) * P], g.ident_b[:, :])
                    ins.then_inc(xqT_ps, 1)
                    pe.wait_ge(xqT_rdy, j + 1)
                    for t in range(GT):
                        for dc in range(2):
                            ins = pe.matmul(g.ps[:, 6 + t // 2, (t % 2) * D:(t % 2 + 1) * D], xqT[:, dc, t * P:(t + 1) * P],
                                            g.kq[:, dc, :], start=dc == 0, stop=dc == 1)
                    ins.then_inc(y_ps, 1)
                with pe.Fori(0, NG // 2) as i:
                    group(i, 0)
                    group(i, 1)

            @block.scalar
            def _(act):
                act.preload_act_table_set(ACT_SET)

                def group(i, u):
                    j = 2 * i + u
                    step = Steps(act, steps_a, 2 * j)
                    act.wait_ge(on_rdy, j + 1)
                    act.activation(sq[:, :, :, :], on[:, :, :, :], ACT.Square).then_inc(osq_rdy, 1)
                    act.wait_ge(oss_rdy, j + 1)
                    step(act.activation(lnss[:, :, :], ss[:, :, :], ACT.Ln))
                    act.activation(y[:, :, :], lnss[:, :, :], ACT.Exp, scale=-0.5).then_inc(oy_rdy, 1)
                    for dc in range(2):
                        act.wait_ge(oT_ps, 2 * j + dc + 1)
                        act.activation(ocT[:, dc, :], g.ps[:, dc, :], ACT.Copy).then_inc(oT_rdy, 1)
                    act.wait_ge(var_rdy, j + 1)
                    step(act.activation(lnv[:, :], veps[:, :], ACT.Ln))
                    act.activation(rstd[:, :], lnv[:, :], ACT.Exp, scale=-0.5).then_inc(rs0_rdy, 1)
                    act.wait_ge(xqT_ps, j + 2)
                    act.activation(xqT[:, :, :], psb.rearrange("p (c n) -> p c n", c=2), ACT.Copy).then_inc(xqT_rdy, 1)
                    act.wait_ge(y_ps, j + 1)
                    act.activation(yb[:, :, :].rearrange("p (a t) d -> p a (t d)", a=2), g.ps[:, 6:8, :], ACT.Identity,
                                   scale=g.S_OUT).then_inc(yb_rdy, 1)
                with act.Fori(0, NG // 2) as i:
                    group(i, 0)
                    group(i, 1)

            @block.vector
            def _(v):
                v.sem_inc(res_rdy, 1)
                for u in range(2):
                    v.sem_inc(res_out[u], 16)
                def group(i, u):
                    j = 2 * i + u
                    step = Steps(v, steps_v, STEPS_FINISH * j)
                    v.wait_ge(in2[u], 80 * (i + 1))
                    step(v.reciprocal(rs[:, :, :, :], o_in[:, u, :, :, :, DH]))
                    for hg in range(HG):
                        ins = v.tensor_tensor(on[:, :, hg * HPG:(hg + 1) * HPG, :], o_in[:, u, hg, :, :, 0:DH],
                                              rs[:, hg].unsqueeze(3).broadcast_to([P, GT, HPG, DH]), ALU.mult)
                    ins.then_inc(on_rdy, 1)
                    v.wait_ge(osq_rdy, j + 1)
                    step(v.tensor_reduce(ss[:, :, :], sq[:, :, :, :], AX.X, ALU.add))
                    v.tensor_scalar(ss[:, :, :], ss[:, :, :], EPS * EPS, None, ALU.max).then_inc(oss_rdy, 1)
                    v.wait_ge(oss_rdy, j + 1)
                    v.wait_ge(oy_rdy, j + 1)
                    step(v.tensor_tensor(y2[:, :, :], y[:, :, :], y[:, :, :], ALU.mult))
                    step(v.tensor_tensor(y2[:, :, :], y2[:, :, :], ss[:, :, :], ALU.mult))
                    step(v.tensor_scalar(y2[:, :, :], y2[:, :, :], -0.5, 1.5, ALU.mult, ALU.add))
                    step(v.tensor_tensor(y[:, :, :], y[:, :, :], y2[:, :, :], ALU.mult))
                    step(v.tensor_scalar(y[:, :, :], y[:, :, :], g.ZS, 1.0, ALU.mult, ALU.min))
                    v.tensor_tensor(on[:, :, :, :].rearrange("p t h d -> p (t h) d"),
                                    on[:, :, :, :].rearrange("p t h d -> p (t h) d"),
                                    y[:, :, :].rearrange("p t h -> p (t h)").unsqueeze(2).broadcast_to([P, GT * H, DH]),
                                    ALU.mult).then_inc(oc_rdy, 1)
                    v.wait_ge(wo_ps, j + 1)
                    x1f = x1[:, :, :].rearrange("p (a t) d -> p a (t d)", a=2)
                    step(v.tensor_tensor(x1f, xt[:, u].rearrange("p (a t) d -> p a (t d)", a=2), g.ps[:, 2:4, :], ALU.add))
                    for t in range(GT):
                        step.mark(v.bn_stats(stats[:, t, :], x1[:, t, :]))
                    step.settle()
                    hold(v, passed_v)
                    for t in range(GT):
                        step.mark(v.bn_aggr(mv[:, t, :], stats[:, t, :]))
                    step.settle()
                    v.tensor_scalar(veps[:, :], mv[:, :, 1], EPS, None, ALU.add).then_inc(var_rdy, 1)
                    v.wait_ge(var_rdy, j + 1)
                    v.wait_ge(rs0_rdy, j + 1)
                    step(v.tensor_tensor(rtmp[:, :], rstd[:, :], rstd[:, :], ALU.mult))
                    step(v.tensor_tensor(rtmp[:, :], rtmp[:, :], veps[:, :], ALU.mult))
                    step(v.tensor_scalar(rtmp[:, :], rtmp[:, :], -0.5, 1.5, ALU.mult, ALU.add))
                    step(v.tensor_tensor(rstd[:, :], rstd[:, :], rtmp[:, :], ALU.mult))
                    for t in range(GT):
                        ins = v.tensor_scalar(xb[:, t, :], x1[:, t, :], mv[:, t, 0:1], rstd[:, t:t + 1],
                                              ALU.subtract, ALU.mult)
                    step(ins)
                    step(v.tensor_scalar(vf[:, :, :], xb[:, :, :], g.INV_SIN, None, ALU.mult))
                    step(v.tensor_reduce(rmax[:, :], vf[:, :, :], AX.X, ALU.max, apply_absolute_value=True))
                    step(v.tensor_scalar(rmax[:, :], rmax[:, :], FLT_MAX / 464.001, 0.0, ALU.mult, ALU.mult))
                    flat = [a[:, :, :].rearrange("p t d -> p (t d)") for a in (vf, sp1, sp2, xq)]
                    v.wait_ge(xqT_ps, j + 1)
                    quantise_e4m3fn(v, step, *flat)
                    v.sem_inc(xq_rdy, 1)
                    v.wait_ge(yb_rdy, j + 1)
                    step(v.tensor_tensor(yb2[:, :, :], yb[:, :, :],
                                         g.bias_b[:, :].unsqueeze(1).broadcast_to([P, GT, D]), ALU.add))
                    v.wait_ge(res_out[u], 16 * i + 16)
                    for t in range(GT):
                        ins = v.scalar_tensor_tensor(res[:, u, t, :], yb2[:, t, :], rmax[:, t:t + 1], x1[:, t, :],
                                                     ALU.add, ALU.add)
                    ins.then_inc(res_rdy, 1)
                    assert step.n == STEPS_FINISH, step.n
                with v.Fori(0, NG // 2) as i:
                    group(i, 0)
                    group(i, 1)


def layer_kernel(nc, x, W_q, W_k, W_v, W_o, log_c, beta, attention_bias, ffn_w, input_scale, kernel_scale,
                 ffn_bias, out):
    assert tuple(x.shape) == (B, S, D) and (QH, GT) == (2, 4)
    g = Shared()
    g.W_q, g.W_k, g.W_v, g.W_o, g.log_c, g.beta, g.attention_bias = W_q, W_k, W_v, W_o, log_c, beta, attention_bias
    g.ffn_w, g.input_scale, g.kernel_scale, g.ffn_bias = ffn_w, input_scale, kernel_scale, ffn_bias
    g.x_g = x.rearrange("b (u t p) d -> (b u) p t d", t=GT, p=P)
    g.out_g = out.rearrange("b (u t p) d -> (b u) p t d", t=GT, p=P)
    g.qT_d = nc.dram_tensor("qT_scratch", [NJ, 3, P, S], BF16, kind="Internal").ap()
    g.kT_d = nc.dram_tensor("kT_scratch", [NJ, 3, P, S], BF16, kind="Internal").ap()
    g.open_d = nc.dram_tensor("open_scratch", [B, HG], I32, kind="Internal").ap()
    g.v_d = nc.dram_tensor("v_scratch", [NJ, S, HPG * VW], F32, kind="Internal").ap()
    g.o_d = nc.dram_tensor("o_scratch", [NJ, S, HPG * OW], F32, kind="Internal").ap()

    with ExitStack() as root:
        def sb(name, shape, dt=F32):
            return root.enter_context(nc.sbuf_tensor(name, shape, dt))

        g.ident = sb("ident", [P, P])
        g.ident_b = sb("ident_b", [P, P], BF16)
        g.sel = sb("sel", [P, P], BF16)
        g.wT = sb("wT", [P, 2, 3 * D])
        g.woT = sb("woT", [P, 2, D])
        g.kq = sb("kq", [P, 2, D], BF16)
        g.bias_b = sb("bias_b", [P, D], BF16)
        g.flag = sb("flag", [1, 1], I32)
        g.run_max = sb("run_max", [P, 1])
        g.ps = root.enter_context(nc.psum_tensor("ps", [P, 8, 512], F32))
        g.sc = sb("sc", [P, 16])
        (g.C_SP, g.C_BP, g.SQC, g.ISQC, g.NEGB, g.ZS, g.M2SC, g.EAB, g.INV_SIN, g.INV_SK, g.S_OUT) = (
            g.sc[:, k:k + 1] for k in range(11))
        emit_setup(nc, g)
        emit_project(nc, g)
        emit_attend(nc, g)
        emit_general(nc, g)
        emit_finish(nc, g)


_INS = ["L0_attn_x", "L0_attn_W_q", "L0_attn_W_k", "L0_attn_W_v", "L0_attn_W_o", "L0_attn_log_c", "L0_attn_beta",
        "L0_attn_attention_bias", "L0_ffn_kernel", "L0_ffn_input_scale", "L0_ffn_kernel_scale", "L0_ffn_bias"]


def kernel(**inputs):
    import numpy as _np
    import concourse.bacc as _bacc
    from concourse.bass_utils import run_bass_kernel_spmd as _run

    nc = _bacc.Bacc("TRN2", target_bir_lowering=False, num_devices=1)
    arrays, args = {}, []
    for name in _INS:
        a = _np.ascontiguousarray(inputs[name])
        if a.ndim == 0:
            a = a.reshape(1)
        arrays[f"in_{name}_dram"] = a
        args.append(nc.dram_tensor(f"in_{name}_dram", a.shape, mybir.dt.from_np(a.dtype), kind="ExternalInput").ap())
    shape = inputs["L0_attn_x"].shape
    args.append(nc.dram_tensor("out_0_dram", shape, F32, kind="ExternalOutput").ap())
    layer_kernel(nc, *args)
    r = _run(nc, [arrays], core_ids=[0])
    return r.results[0]["out_0_dram"]
```

```python
import math
from contextlib import ExitStack

import concourse.bass as bass
from concourse import mybir

ALU = mybir.AluOpType
ACT = mybir.ActivationFunctionType
AX = mybir.AxisListType
F32 = mybir.dt.float32
BF16 = mybir.dt.bfloat16
I32 = mybir.dt.int32

P = 128
ACT_SET = "natural_log_exp_and_others"
EPS = 1e-5
U_EXACT = 1100.0
A_FLOOR = 1e-8
THETA_MAX = 14.4
EXPONENT_MAX = 60.0

B, S, D = 8, 1024, 256
H, DH = 16, 16
HG, HPG = 4, 4
GT = 4
GTOK = GT * P
NG = B * S // GTOK
NJ = B * HG
KT = S // P
QH = S // GTOK
VW = DH + 3
OW = DH + 2
RU = 19
Q_PARTS = (0, 0, 0, 1, 1, 2)
K_PARTS = (0, 1, 2, 0, 1, 0)
RS = RU * len(Q_PARTS)
QPJ = QH * KT
SLOTS = HG * QPJ
TR = HPG * RU
RING = 4
GROUP_USES = 18
PROJECT_SLOTS, FINISH_SLOTS = 35, 32
PROJECT_AT, FINISH_AT = (0, 25), (4, 32)
FLT_MAX = 3.4028234e38


class Shared:
    pass


class Steps:

    def __init__(self, eng, sem, start):
        self.eng, self.sem, self.start, self.n = eng, sem, start, 0

    def __call__(self, ins):
        ins.then_inc(self.sem, 1)
        self.n += 1
        self.eng.wait_ge(self.sem, self.start + self.n)

    def mark(self, ins):
        ins.then_inc(self.sem, 1)
        self.n += 1

    def settle(self):
        self.eng.wait_ge(self.sem, self.start + self.n)


def quantise_e4m3fn(v, steps, values, spare, spare2, out):
    steps(v.tensor_scalar(spare.bitcast(I32), values.bitcast(I32), 0x7F800000, None, ALU.bitwise_and))
    steps(v.tensor_scalar(spare, spare, 2.0 ** -6, 1.5 * 2.0 ** 20, ALU.max, ALU.mult))
    steps(v.tensor_tensor(spare2, values, spare, ALU.add))
    steps(v.tensor_tensor(out, spare2, spare, ALU.subtract))


def hold(eng, passed):
    eng.sem_inc(passed, 1)

def _sb(nc, ctx, name, shape, dt=F32):
    return ctx.enter_context(nc.sbuf_tensor(name, shape, dt))


def _sem(nc, ctx, name):
    return ctx.enter_context(nc.semaphore(name))


def emit_setup(nc, g):
    with ExitStack() as ctx:
        def sb(name, shape, dt=F32):
            return _sb(nc, ctx, name, shape, dt)
        wraw = sb("wraw", [P, 4, 2, D])
        kraw = sb("kraw", [P, 2, D], BF16)
        kval, ktmp, ktmp2 = sb("kval", [P, 2 * D]), sb("ktmp", [P, 2 * D]), sb("ktmp2", [P, 2 * D])
        srow = sb("srow", [1, 8])
        brow = sb("brow", [1, D], BF16)
        ones_r = sb("ones_r", [1, P])
        ones_rb = sb("ones_rb", [1, P], BF16)
        t = sb("t", [P, 32])
        w_in, s_in, k_in = (_sem(nc, ctx, n) for n in ("w_in", "s_in", "k_in"))
        consts, wt_ps, sc_ps, wt_done = (_sem(nc, ctx, n) for n in ("consts", "wt_ps", "sc_ps", "wt_done"))
        v_steps, a_steps, to_act, to_dve, g_steps = (
            _sem(nc, ctx, n) for n in ("v_steps", "a_steps", "to_act", "to_dve", "g_steps"))

        with nc.Block() as block:
            @block.sync
            def _(sp):
                for k, a in enumerate((g.log_c, g.beta, g.attention_bias, g.input_scale, g.kernel_scale)):
                    sp.dma_start(srow[0:1, k:k + 1], a.rearrange("(a n) -> a n", a=1)).then_inc(s_in, 16)
                sp.dma_start(brow[:, :], g.ffn_bias.rearrange("(a n) -> a n", a=1)).then_inc(s_in, 16)
                for k, w in enumerate((g.W_q, g.W_k, g.W_v, g.W_o)):
                    sp.dma_start(wraw[:, k], w.rearrange("(c p) d -> p c d", p=P)).then_inc(w_in, 16)
                sp.dma_start(kraw[:, :, :], g.ffn_w.rearrange("(c p) d -> p c d", p=P)).then_inc(k_in, 16)

            @block.gpsimd
            def _(pool):
                step = Steps(pool, g_steps, 0)
                step.mark(pool.memset(g.ident[:, :], 0.0))
                step.mark(pool.memset(g.ident_b[:, :], 0.0))
                step.mark(pool.memset(g.sel[:, :], 0.0))
                pool.memset(ones_r[:, :], 1.0).then_inc(consts, 1)
                pool.memset(ones_rb[:, :], 1.0).then_inc(consts, 1)
                step.settle()
                for m in (g.ident, g.ident_b):
                    pool.affine_select(out=m[:, :], in_=m[:, :], compare_op=ALU.not_equal, fill=1.0, base=0,
                                       pattern=[[-1, P]], channel_multiplier=1).then_inc(consts, 1)
                for part in range(3):
                    ins = pool.affine_select(out=g.sel[:, :], in_=g.sel[:, :], compare_op=ALU.not_equal, fill=1.0,
                                             base=-(RU * Q_PARTS.index(part) + RU - 1), pattern=[[0, P]],
                                             channel_multiplier=1)
                    if part < 2:
                        step(ins)
                    else:
                        ins.then_inc(consts, 1)

            @block.tensor
            def _(pe):
                pe.wait_ge(consts, 5)
                pe.wait_ge(s_in, 16 * 6)
                pe.matmul(g.ps[:, 0, 0:5], ones_r[:, :], srow[:, 0:5], start=True, stop=True).then_inc(sc_ps, 1)
                pe.matmul(g.ps[:, 1, 0:D], ones_rb[:, :], brow[:, :], start=True, stop=True).then_inc(sc_ps, 1)
                pe.wait_ge(w_in, 16 * 4)
                for k in range(4):
                    for oc in range(2):
                        for dc in range(2):
                            ins = pe.transpose(g.ps[:, 2 + k, dc * D + oc * P:dc * D + oc * P + P],
                                               wraw[:, k, oc, dc * P:(dc + 1) * P], g.ident[:, :])
                    ins.then_inc(wt_ps, 1)

            @block.scalar
            def _(act):
                def do(n, *a, **k):
                    act.wait_ge(to_act, n)
                    act.activation(*a, **k).then_inc(to_dve, 1)
                act.preload_act_table_set(ACT_SET)
                do(1, t[:, 8:10], t[:, 6:8], ACT.Exp)
                act.wait_ge(to_dve, 1)
                act.activation(t[:, 10:12], t[:, 8:10], ACT.Ln, bias=1.0).then_inc(to_dve, 1)
                do(2, t[:, 12:13], g.C_SP, ACT.Ln)
                act.wait_ge(to_dve, 3)
                act.activation(t[:, 13:14], t[:, 12:13], ACT.Exp, scale=0.5).then_inc(to_dve, 1)
                do(3, t[:, 16:17], t[:, 15:16], ACT.Ln, bias=1.0)
                act.activation(t[:, 17:18], t[:, 15:16], ACT.Ln, scale=-1.0, bias=1.0).then_inc(to_dve, 1)
                act.activation(g.EAB, t[:, 18:19], ACT.Exp).then_inc(to_dve, 1)
                for k in range(4):
                    act.wait_ge(wt_ps, k + 1)
                    dst = g.wT[:, :, k * D:(k + 1) * D] if k < 3 else g.woT[:, :, :]
                    act.activation(dst, g.ps[:, 2 + k, :].rearrange("p (c o) -> p c o", c=2),
                                   ACT.Copy).then_inc(wt_done, 1)

            @block.vector
            def _(v):
                step = Steps(v, v_steps, 0)
                v.wait_ge(sc_ps, 2)
                step(v.tensor_copy(t[:, 0:5], g.ps[:, 0, 0:5]))
                v.tensor_copy(g.bias_b[:, :], g.ps[:, 1, 0:D])
                step(v.tensor_scalar(t[:, 20:22], t[:, 0:2], -1.0, None, ALU.mult))
                v.tensor_tensor(t[:, 6:8], t[:, 0:2], t[:, 20:22], ALU.min).then_inc(to_act, 1)
                step(v.tensor_scalar(t[:, 22:24], t[:, 0:2], 0.0, None, ALU.max))
                v.wait_ge(to_dve, 2)
                v.tensor_tensor(g.sc[:, 0:2], t[:, 22:24], t[:, 10:12], ALU.add).then_inc(to_act, 1)
                v.wait_ge(to_act, 2)
                v.wait_ge(to_dve, 4)
                step(v.reciprocal(t[:, 24:25], t[:, 13:14]))
                step(v.tensor_scalar(t[:, 25:26], t[:, 24:25], g.C_SP, t[:, 13:14], ALU.mult, ALU.add))
                step(v.tensor_scalar(g.SQC, t[:, 25:26], 0.5, None, ALU.mult))
                step(v.reciprocal(g.ISQC, g.SQC))
                step(v.tensor_scalar(g.NEGB, g.C_BP, g.ISQC, -1.0, ALU.mult, ALU.mult))
                step(v.tensor_scalar(g.M2SC, g.SQC, -2.0, None, ALU.mult))
                step(v.tensor_scalar(t[:, 19:20], t[:, 2:3], -1.0, None, ALU.mult))
                step(v.tensor_tensor(t[:, 18:19], t[:, 19:20], t[:, 19:20], ALU.subtract))
                step(v.tensor_scalar(t[:, 14:15], g.ISQC, -EPS, None, ALU.add))
                v.tensor_scalar(t[:, 15:16], t[:, 14:15], g.SQC, None, ALU.mult).then_inc(to_act, 1)
                v.wait_ge(to_dve, 7)
                step(v.tensor_tensor(t[:, 26:27], t[:, 16:17], t[:, 17:18], ALU.subtract))
                step(v.tensor_scalar(g.ZS, t[:, 26:27], g.ISQC, 0.5, ALU.mult, ALU.mult))
                step(v.reciprocal(g.INV_SIN, t[:, 3:4]))
                step(v.reciprocal(g.INV_SK, t[:, 4:5]))
                step(v.tensor_scalar(g.S_OUT, t[:, 3:4], t[:, 4:5], None, ALU.mult))
                v.wait_ge(k_in, 16)
                step(v.tensor_scalar(kval[:, :], kraw[:, :, :].rearrange("p c d -> p (c d)"), g.INV_SK, None,
                                     ALU.mult))
                quantise_e4m3fn(v, step, kval[:, :], ktmp[:, :], ktmp2[:, :], kval[:, :])
                step(v.tensor_scalar(ktmp[:, :], kval[:, :], 3.4028234e38 / 460.0, 0.0, ALU.mult, ALU.mult))
                step(v.tensor_tensor(g.kq[:, :, :].rearrange("p c d -> p (c d)"), kval[:, :], ktmp[:, :], ALU.add))
                step(v.memset(g.run_max[:, :], 0.0))


def project_stage(nc, ctx, g, b7_filled, b7_copied, opens, open_rdy):
    def sb(name, shape, dt=F32):
        return _sb(nc, ctx, name, shape, dt)
    PER = 29
    xt, xn = sb("xt", [P, GT, D]), sb("xn", [P, GT, D])
    stats, mv = sb("stats", [P, GT, 6]), sb("mv", [P, GT, 2])
    veps, lnv, rstd, rtmp = (sb(n, [P, GT]) for n in ("veps", "lnv", "rstd", "rtmp"))
    xnT = sb("xnT", [P, 2, GTOK])
    qkv = sb("qkv", [P, GT, 3 * H, DH])
    ss, lnss, y, y2 = (sb(n, [P, GT, 3 * H]) for n in ("ss", "lnss", "y", "y2"))
    nrm, e, rp, tn, tt, f, a = (sb(n, [P, GT, 2 * H]) for n in ("nrm", "e", "rp", "tn", "tt", "f", "a"))
    vg = sb("vg", [P, GT, H])
    qk_rows = sb("qk_rows", [P, 2, GT, H, RU])
    v_rows = sb("v_rows", [P, HG, GT, HPG, VW])
    parts = sb("parts", [P, 3, HG, GTOK], BF16)
    rest = sb("rest", [P, HG, GTOK])
    amax = sb("amax", [P, 3, 2 * H])
    amax_r, prod = sb("amax_r", [2 * H, 1]), sb("prod", [1, 3 * H])
    (x_in, var_rdy, rs0_rdy, xn_rdy, red_done, sq_rdy, ss_rdy, y0_rdy, n_rdy, vg_rdy, e_rdy, small_rdy,
     vrow_rdy, rows_rdy, hi_rdy, mid_rdy, low_rdy, T_out, v_out, d_steps, a_steps, amax_rdy, amax_steps) = (
        _sem(nc, ctx, "pr_" + n) for n in (
            "x_in", "var", "rs0", "xn", "red_done", "sq", "ss", "y0", "n", "vg", "e", "small",
            "vrow", "rows", "hi", "mid", "low", "T_out", "v_out", "v_steps", "a_steps", "amax", "amax_steps"))
    passed_v, passed_sp, passed_pool, passed_pe = (_sem(nc, ctx, "pr_passed_" + n) for n in ("v", "sp", "pool", "pe"))
    steps_before = {3: 0, 6: 8, 20: 12, 23: 17}

    def squares(t):
        return rest[:, 2 * (t % 2):2 * (t % 2) + 2, :].rearrange("p a n -> p (a n)")[:, 0:3 * D]

    def use(b, u, idx):
        return (2 * GROUP_USES + 2) * b + GROUP_USES * u + idx

    def uses_at(u, k, second):
        if k == 7:
            return second
        if 8 <= k < 16 and not second:
            return 2 + k - 8
        if k in (25, 26):
            return 10 + 2 * (k - 25) + second
        if k in (30, 31):
            return 14 + 2 * (k - 30) + second
        if u == 1 and k in (33, 34) and not second:
            return 18 + k - 33
        return None

    def start_vector(v):
        v.sem_inc(xn_rdy, 1)
        v.sem_inc(v_out, 64)
        v.sem_inc(T_out, 48)
        v.sem_inc(red_done, 2)
        v.sem_inc(rows_rdy, 1)
        v.sem_inc(low_rdy, 1)
        v.sem_inc(vrow_rdy, 1)
        v.sem_inc(b7_copied, 1)
        v.memset(qk_rows[:, :, :, :, :], 0.0).then_inc(d_steps, 1)
        v.wait_ge(d_steps, 1)
        v.memset(qk_rows[:, 0, :, :, 16:17], 1.0).then_inc(d_steps, 1)
        v.memset(qk_rows[:, 1, :, :, 17:18], -1.0).then_inc(d_steps, 1)
        for hg in range(HG):
            v.tensor_scalar(v_rows[:, hg, :, :, DH:DH + 1], qk_rows[:, 0, :, 0:HPG, 17:18], g.EAB, None,
                            ALU.add).then_inc(d_steps, 1)
            v.tensor_copy(v_rows[:, hg, :, :, DH + 1:DH + 2], qk_rows[:, 0, :, 0:HPG, 17:18]).then_inc(d_steps, 1)
        v.wait_ge(d_steps, 3 + 2 * HG)

    def sync(sp, b, u, k):
        n = 2 * b + u
        if k == 0:
            sp.wait_ge(xn_rdy, n + 1)
            hold(sp, passed_sp)
            sp.dma_start(xt[:, :, :], g.x_g[bass.ds(n, 1)].rearrange("a p t d -> (a p) t d")).then_inc(x_in, 16)
        if k == 25:
            sp.wait_ge(vrow_rdy, 2 * n + 3)
            hold(sp, passed_sp)
            for hg in range(HG):
                sp.dma_start(g.v_d[bass.ds(4 * b + hg, 1), u * GTOK:(u + 1) * GTOK, :].rearrange(
                    "b (t p) f -> p (b t) f", p=P),
                    v_rows[:, hg].rearrange("p t h w -> p t (h w)")).then_inc(v_out, 16)
        for at, qk, dst in ((29, 0, g.qT_d), (34, 1, g.kT_d)):
            if k == at:
                sp.wait_ge(low_rdy, 8 * n + 4 * qk + 5)
                hold(sp, passed_sp)
                for part in range(3):
                    sp.dma_start(dst[bass.ds(4 * b, HG), part, :, u * GTOK:(u + 1) * GTOK].rearrange(
                        "g p t -> p g t"), parts[0:TR, part]).then_inc(T_out, 16)

    def gpsimd(pool, b, u, k):
        n = 2 * b + u
        if k in (9, 11, 13, 15):
            t = (k - 9) // 2
            pool.wait_ge(b7_copied, use(b, u, 3 + 2 * t) + 2)
            pool.wait_ge(red_done, 4 * n + t + 1)
            pool.wait_ge(low_rdy, 8 * n + 1)
            src = qkv[:, t].rearrange("p h d -> p (h d)")
            pool.tensor_tensor(squares(t), src, src, ALU.mult).then_inc(sq_rdy, 1)
        if k == 21:
            pool.wait_ge(vg_rdy, n + 1)
            pool.wait_ge(v_out, 64 * (n + 1))
            for hg in range(HG):
                ins = pool.tensor_tensor(
                    v_rows[:, hg, :, :, 0:DH], qkv[:, :, 2 * H + hg * HPG:2 * H + (hg + 1) * HPG, :],
                    vg[:, :, hg * HPG:(hg + 1) * HPG].unsqueeze(3).broadcast_to([P, GT, HPG, DH]), ALU.mult)
            ins.then_inc(vrow_rdy, 1)
        if k == 24:
            pool.wait_ge(small_rdy, n + 1)
            for qk, src in ((0, f[:, :, 0:H]), (1, f[:, :, H:])):
                pool.tensor_tensor(qk_rows[:, qk, :, :, 0:DH], qkv[:, :, qk * H:(qk + 1) * H, :],
                                   src.unsqueeze(3).broadcast_to([P, GT, H, DH]), ALU.mult).then_inc(rows_rdy, 1)
        for at, qk in ((27, 0), (32, 1)):
            if k in (at, at + 1):
                for m in (4 * qk + 2 * (k - at), 4 * qk + 2 * (k - at) + 1):
                    pool.wait_ge(b7_copied, use(b, u, 10 + m) + 2)
                    hold(pool, passed_pool)
                    pool.tensor_copy(parts[0:TR, 1, m % 4, :], rest[0:TR, m % 4, :]).then_inc(mid_rdy, 1)
                    pool.wait_ge(mid_rdy, 8 * n + m + 1)
                    pool.tensor_tensor(parts[0:TR, 2, m % 4, :], rest[0:TR, m % 4, :], parts[0:TR, 1, m % 4, :],
                                       ALU.subtract).then_inc(low_rdy, 1)

    def tensor(pe, b, u, k, second):
        idx = uses_at(u, k, second)
        if idx is None:
            return
        n = 2 * b + u
        bank = g.ps[:, 7, :]
        if idx == 0:
            pe.wait_ge(xn_rdy, n + 2)
        if idx == 2:
            pe.wait_ge(b7_copied, use(b, u, 1) + 2)
        if idx in (10, 14):
            pe.wait_ge(rows_rdy, 2 * n + (idx - 10) // 4 + 2)
            pe.wait_ge(small_rdy, n + 1)
        if idx == 18:
            pe.wait_ge(amax_rdy, 2 * b + 1)
        if idx == 19:
            pe.wait_ge(amax_rdy, 2 * b + 2)
        pe.wait_ge(b7_copied, use(b, u, idx) + 1)
        if idx < 2:
            for t in range(GT):
                ins = pe.transpose(bank[:, t * P:(t + 1) * P], xn[:, t, idx * P:(idx + 1) * P], g.ident[:, :])
        elif idx < 10:
            t, half = (idx - 2) // 2, idx % 2
            for dc in range(2):
                ins = pe.matmul(bank[:, 0:384], xnT[:, dc, t * P:(t + 1) * P],
                                g.wT[:, dc, half * 384:(half + 1) * 384], start=dc == 0, stop=dc == 1)
        elif idx < 18:
            qk, m = (idx - 10) // 4, (idx - 10) % 4
            for t in range(GT):
                ins = pe.transpose(bank[0:TR, t * P:(t + 1) * P],
                                   qk_rows[:, qk, t, m * HPG:(m + 1) * HPG, :].rearrange("p h r -> p (h r)"),
                                   g.ident[:, :])
        elif idx == 18:
            ins = pe.transpose(bank[0:2 * H, 0:P], amax[:, 2, :], g.ident[:, :])
        else:
            hold(pe, passed_pe)
            ins = pe.transpose(bank[0:1, 0:2 * H], amax_r[:, :], g.ident[0:2 * H, 0:2 * H])
        ins.then_inc(b7_filled, 1)

    def copy(v, b, u, k, second):
        idx = uses_at(u, k, second)
        if idx is None:
            return
        n = 2 * b + u
        bank = g.ps[:, 7, :]
        v.wait_ge(b7_filled, use(b, u, idx) + 1)
        if idx < 2:
            v.tensor_copy(xnT[:, idx, :], bank).then_inc(b7_copied, 1)
        elif idx < 10:
            t, half = (idx - 2) // 2, idx % 2
            if idx == 2:
                v.wait_ge(rows_rdy, 2 * n + 1)
                v.wait_ge(vrow_rdy, 2 * n + 1)
            v.tensor_copy(qkv[:, t, 24 * half:24 * (half + 1), :].rearrange("p h d -> p (h d)"),
                          bank[:, 0:384]).then_inc(b7_copied, 1)
        elif idx < 18:
            m = idx - 10
            if m % 4 == 0:
                v.wait_ge(T_out, 48 * (2 * n + m // 4 + 1))
            v.tensor_copy(parts[0:TR, 0, m % 4, :], bank[0:TR, :]).then_inc(hi_rdy, 1)
            v.wait_ge(hi_rdy, 8 * n + m + 1)
            v.tensor_tensor(rest[0:TR, m % 4, :], bank[0:TR, :], parts[0:TR, 0, m % 4, :],
                            ALU.subtract).then_inc(b7_copied, 1)
        elif idx == 18:
            v.tensor_reduce(amax_r[:, :], bank[0:2 * H, 0:P], AX.X, ALU.max).then_inc(amax_steps, 1)
            v.wait_ge(amax_steps, 4 * b + 1)
            v.sem_inc(b7_copied, 1)
            v.sem_inc(amax_rdy, 1)
        else:
            v.tensor_copy(prod[:, 0:2 * H], bank[0:1, 0:2 * H]).then_inc(amax_steps, 1)
            v.wait_ge(amax_steps, 4 * b + 2)
            v.sem_inc(b7_copied, 1)
            v.tensor_tensor(prod[:, 2 * H:], prod[:, 0:H], prod[:, H:2 * H], ALU.mult).then_inc(amax_steps, 1)
            v.wait_ge(amax_steps, 4 * b + 3)
            v.tensor_reduce(prod[:, 0:HG], prod[:, 2 * H:].rearrange("p (g h) -> p g h", g=HG), AX.X,
                            ALU.max).then_inc(amax_steps, 1)
            v.wait_ge(amax_steps, 4 * b + 4)
            v.tensor_scalar(opens[:, :], prod[:, 0:HG], EPS, None, ALU.is_gt).then_inc(open_rdy, 1)

    def scalar(act, b, u, k):
        n = 2 * b + u
        if k == 4:
            act.wait_ge(var_rdy, n + 1)
            act.activation(lnv[:, :], veps[:, :], ACT.Ln).then_inc(a_steps, 1)
            act.wait_ge(a_steps, 2 * n + 1)
            act.activation(rstd[:, :], lnv[:, :], ACT.Exp, scale=-0.5).then_inc(rs0_rdy, 1)
        if k == 18:
            act.wait_ge(ss_rdy, n + 1)
            act.activation(lnss[:, :, :], ss[:, :, :], ACT.Ln).then_inc(a_steps, 1)
            act.wait_ge(a_steps, 2 * n + 2)
            act.activation(y[:, :, :], lnss[:, :, :], ACT.Exp, scale=-0.5).then_inc(y0_rdy, 1)
        if k == 21:
            act.wait_ge(n_rdy, n + 1)
            act.activation(e[:, :, :], nrm[:, :, :], ACT.Exp, scale=g.M2SC).then_inc(e_rdy, 1)

    def vector(v, b, u, k):
        n = 2 * b + u
        step = Steps(v, d_steps, 3 + 2 * HG + PER * n + steps_before.get(k, 0))
        if k == 3:
            v.wait_ge(x_in, 16 * (n + 1))
            for t in range(GT):
                step.mark(v.bn_stats(stats[:, t, :], xt[:, t, :]))
            step.settle()
            hold(v, passed_v)
            for t in range(GT):
                step.mark(v.bn_aggr(mv[:, t, :], stats[:, t, :]))
            step.settle()
            v.tensor_scalar(veps[:, :], mv[:, :, 1], EPS, None, ALU.add).then_inc(var_rdy, 1)
        if k == 6:
            v.wait_ge(rs0_rdy, n + 1)
            v.wait_ge(var_rdy, n + 1)
            step(v.tensor_tensor(rtmp[:, :], rstd[:, :], rstd[:, :], ALU.mult))
            step(v.tensor_tensor(rtmp[:, :], rtmp[:, :], veps[:, :], ALU.mult))
            step(v.tensor_scalar(rtmp[:, :], rtmp[:, :], -0.5, 1.5, ALU.mult, ALU.add))
            step(v.tensor_tensor(rstd[:, :], rstd[:, :], rtmp[:, :], ALU.mult))
            for t in range(GT):
                ins = v.tensor_scalar(xn[:, t, :], xt[:, t, :], mv[:, t, 0:1], rstd[:, t:t + 1],
                                      ALU.subtract, ALU.mult)
            ins.then_inc(xn_rdy, 1)
        if k in (11, 13, 15, 17):
            t = (k - 11) // 2
            v.wait_ge(sq_rdy, 4 * n + t + 1)
            v.tensor_reduce(ss[:, t, :], squares(t).rearrange("p (h d) -> p h d", d=DH), AX.X,
                            ALU.add).then_inc(red_done, 1)
            if t == GT - 1:
                v.wait_ge(red_done, 4 * n + 6)
                v.tensor_scalar(ss[:, :, :], ss[:, :, :], EPS * EPS, None, ALU.max).then_inc(ss_rdy, 1)
        yqk, ssqk = y[:, :, 0:2 * H], ss[:, :, 0:2 * H]
        if k == 20:
            v.wait_ge(y0_rdy, n + 1)
            v.wait_ge(ss_rdy, n + 1)
            step(v.tensor_tensor(y2[:, :, :], y[:, :, :], y[:, :, :], ALU.mult))
            step(v.tensor_tensor(y2[:, :, :], y2[:, :, :], ss[:, :, :], ALU.mult))
            step(v.tensor_scalar(y2[:, :, :], y2[:, :, :], -0.5, 1.5, ALU.mult, ALU.add))
            step(v.tensor_tensor(y[:, :, :], y[:, :, :], y2[:, :, :], ALU.mult))
            v.tensor_tensor(nrm[:, :, :], ssqk, yqk, ALU.mult).then_inc(n_rdy, 1)
            step(v.tensor_scalar(vg[:, :, :], y[:, :, 2 * H:], g.ZS, 1.0, ALU.mult, ALU.min))
            v.tensor_scalar(vg[:, :, :], vg[:, :, :], g.EAB, None, ALU.mult).then_inc(vg_rdy, 1)
        if k == 23:
            v.wait_ge(e_rdy, n + 1)
            step(v.tensor_scalar(rp[:, :, :], e[:, :, :], 1.0, None, ALU.add))
            step(v.reciprocal(rp[:, :, :], rp[:, :, :]))
            step.mark(v.tensor_scalar(tn[:, :, :], e[:, :, :], -1.0, 1.0, ALU.mult, ALU.add))
            step(v.tensor_tensor(a[:, :, :], e[:, :, :], rp[:, :, :], ALU.mult))
            step.mark(v.tensor_tensor(tn[:, :, :], tn[:, :, :], rp[:, :, :], ALU.mult))
            step(v.tensor_tensor(a[:, :, :], a[:, :, :], rp[:, :, :], ALU.mult))
            step.mark(v.tensor_tensor(tt[:, :, :], tn[:, :, :], tn[:, :, :], ALU.mult))
            step.mark(v.tensor_tensor(f[:, :, 0:H], tn[:, :, 0:H], yqk[:, :, 0:H], ALU.mult))
            step.mark(v.scalar_tensor_tensor(f[:, :, H:], tn[:, :, H:], 2.0, yqk[:, :, H:], ALU.mult, ALU.mult))
            step(v.tensor_scalar(a[:, :, :], a[:, :, :], 4.0, A_FLOOR, ALU.mult, ALU.max))
            step(v.reciprocal(rp[:, :, :], a[:, :, :]))
            rq, rk = qk_rows[:, 0], qk_rows[:, 1]
            v.tensor_copy(rq[:, :, :, 17], tt[:, :, 0:H])
            v.tensor_copy(rq[:, :, :, 18], rp[:, :, 0:H])
            v.tensor_scalar(rk[:, :, :, 16], tt[:, :, H:], -1.0, None, ALU.mult).then_inc(small_rdy, 1)
            v.wait_ge(v_out, 64 * (n + 1))
            for hg in range(HG):
                ins = v.tensor_copy(v_rows[:, hg, :, :, DH + 2], rp[:, :, H + hg * HPG:H + (hg + 1) * HPG])
            ins.then_inc(vrow_rdy, 1)
            step(v.tensor_reduce(amax[:, u, :], a[:, :, :].rearrange("p t h -> p h t"), AX.X, ALU.max))
            if u == 1:
                v.tensor_tensor(amax[:, 2, :], amax[:, 0, :], amax[:, 1, :], ALU.max).then_inc(amax_rdy, 1)
        assert step.n == {3: 8, 6: 4, 20: 5, 23: 12}.get(k, 0), (k, step.n)

    p = Shared()
    p.start_vector, p.sync, p.gpsimd, p.tensor, p.copy, p.scalar, p.vector = (
        start_vector, sync, gpsimd, tensor, copy, scalar, vector)
    p.stored = ((T_out, 96 * NG + 48), (v_out, 64 * NG + 64))
    p.T_out, p.v_out = T_out, v_out
    return p


def finish_stage(nc, ctx, g, prefix, b6_filled, b6_copied):
    def sb(name, shape, dt=F32):
        return _sb(nc, ctx, prefix + name, shape, dt)
    PER = 23
    o_in = sb("o_in", [P, HG, GT, HPG, OW])
    xt = sb("xt", [P, GT, D])
    rs = sb("rs", [P, HG, GT, HPG])
    on, sq = sb("on", [P, GT, H, DH]), sb("osq", [P, GT, H, DH])
    ss, lnss, y, y2 = (sb("o" + n, [P, GT, H]) for n in ("ss", "lnss", "y", "y2"))
    ocT = sb("ocT", [P, 2, GTOK])
    x1 = sb("x1", [P, GT, D])
    stats, mv = sb("stats", [P, GT, 6]), sb("mv", [P, GT, 2])
    veps, lnv, rstd, rtmp, rmax = (sb(n, [P, GT]) for n in ("veps", "lnv", "rstd", "rtmp", "rmax"))
    xb, xq = sb("xb", [P, GT, D], BF16), sb("xq", [P, GT, D], BF16)
    vf, sp1, sp2 = xt[:, :, :], on[:, :, :, :].rearrange("p t h d -> p t (h d)"), \
        sq[:, :, :, :].rearrange("p t h d -> p t (h d)")
    xqT = sb("xqT", [P, 2, GTOK], BF16)
    yb, yb2 = sb("yb", [P, GT, D], BF16), sb("yb2", [P, GT, D], BF16)
    res = sb("res", [P, GT, D])
    (f_in, rs_rdy, on_rdy, osq_rdy, oss_rdy, oy_rdy, oy2_rdy, oc_rdy, var_rdy, rs0_rdy, xb_rdy, vf_rdy, sp_rdy,
     sum_rdy, xq_rdy, yb2_rdy, res_rdy, res_out, steps_v, steps_a) = (
        _sem(nc, ctx, prefix + n) for n in (
            "in", "rs", "on", "osq", "oss", "oy", "oy2", "oc", "var", "rs0", "xb", "vf", "sp", "sum", "xq", "yb2",
            "res", "out", "steps_v", "steps_a"))
    passed_v, passed_sp = (_sem(nc, ctx, prefix + "passed_" + n) for n in ("v", "sp"))
    psb = g.ps[:, 6, :].bitcast(BF16)
    steps_before = {5: 0, 8: 1, 11: 2, 17: 6, 20: 14, 23: 21}

    def uses_at(k, second):
        return {(13, 0): 0, (13, 1): 1, (14, 0): 2, (15, 0): 3, (25, 0): 4, (26, 0): 5, (26, 1): 6}.get((k, second))

    def start_vector(v):
        v.sem_inc(res_rdy, 1)
        v.sem_inc(res_out, 16)

    def sync(sp, n, b, u, k, sums_stored):
        if k == 0:
            sp.wait_ge(res_rdy, n + 1)
            if sums_stored is not None:
                sp.wait_ge(sums_stored[u], 16 * (4 * b + 4))
            hold(sp, passed_sp)
            sp.dma_start(xt[:, :, :], g.x_g[bass.ds(n, 1)].rearrange("a p t d -> (a p) t d")).then_inc(f_in, 16)
            for hg in range(HG):
                sp.dma_start(o_in[:, hg].rearrange("p t h w -> p t (h w)"),
                             g.o_d[bass.ds(4 * b + hg, 1), u * GTOK:(u + 1) * GTOK, :].rearrange(
                                 "a (t p) f -> p (a t) f", p=P)).then_inc(f_in, 16)
        if k == 31:
            sp.wait_ge(res_rdy, n + 2)
            hold(sp, passed_sp)
            sp.dma_start(g.out_g[bass.ds(n, 1)].rearrange("a p t d -> (a p) t d"), res[:, :, :]).then_inc(res_out, 16)

    def gpsimd(pool, n, k):
        if k == 5:
            pool.wait_ge(rs_rdy, n + 1)
            for hg in range(HG):
                ins = pool.tensor_tensor(on[:, :, hg * HPG:(hg + 1) * HPG, :], o_in[:, hg, :, :, 0:DH],
                                         rs[:, hg].unsqueeze(3).broadcast_to([P, GT, HPG, DH]), ALU.mult)
            ins.then_inc(on_rdy, 1)
            pool.wait_ge(on_rdy, n + 1)
            pool.tensor_tensor(sq[:, :, :, :], on[:, :, :, :], on[:, :, :, :], ALU.mult).then_inc(osq_rdy, 1)
        if k == 11:
            pool.wait_ge(oy2_rdy, n + 1)
            pool.tensor_tensor(on[:, :, :, :].rearrange("p t h d -> p (t h) d"),
                               on[:, :, :, :].rearrange("p t h d -> p (t h) d"),
                               y[:, :, :].rearrange("p t h -> p (t h)").unsqueeze(2).broadcast_to([P, GT * H, DH]),
                               ALU.mult).then_inc(oc_rdy, 1)
        flat = [a.rearrange("p t d -> p (t d)") for a in (vf, sp1, sp2, xq[:, :, :])]
        if k == 23:
            pool.wait_ge(sp_rdy, n + 1)
            pool.tensor_tensor(flat[2], flat[0], flat[1], ALU.add).then_inc(sum_rdy, 1)
            pool.wait_ge(sum_rdy, n + 1)
            pool.tensor_tensor(flat[3], flat[2], flat[1], ALU.subtract).then_inc(xq_rdy, 1)
        if k == 28:
            pool.wait_ge(yb2_rdy, 3 * n + 2)
            pool.tensor_tensor(yb2[:, :, :], yb[:, :, :], g.bias_b[:, :].unsqueeze(1).broadcast_to([P, GT, D]),
                               ALU.add).then_inc(yb2_rdy, 1)

    def tensor(pe, n, k, second, use):
        idx = uses_at(k, second)
        if idx is None:
            return
        bank = g.ps[:, 6, :]
        if idx == 0:
            pe.wait_ge(oc_rdy, n + 1)
        if idx == 2:
            pe.wait_ge(b6_copied, use(1) + 2)
        if idx == 4:
            pe.wait_ge(xq_rdy, n + 1)
        if idx == 5:
            pe.wait_ge(b6_copied, use(4) + 2)
        pe.wait_ge(b6_copied, use(idx) + 1)
        if idx < 2:
            for t in range(GT):
                ins = pe.transpose(bank[:, t * P:(t + 1) * P],
                                   on[:, t, idx * 8:(idx + 1) * 8, :].rearrange("p h d -> p (h d)"), g.ident[:, :])
        elif idx in (2, 3):
            for a in range(2):
                t = 2 * (idx - 2) + a
                for dc in range(2):
                    ins = pe.matmul(bank[:, a * D:(a + 1) * D], ocT[:, dc, t * P:(t + 1) * P],
                                    g.woT[:, dc, :], start=dc == 0, stop=dc == 1)
        elif idx == 4:
            for dc in range(2):
                for t in range(GT):
                    ins = pe.transpose(psb[:, dc * GTOK + t * P:dc * GTOK + (t + 1) * P],
                                       xq[:, t, dc * P:(dc + 1) * P], g.ident_b[:, :])
        else:
            for a in range(2):
                t = 2 * (idx - 5) + a
                for dc in range(2):
                    ins = pe.matmul(bank[:, a * D:(a + 1) * D], xqT[:, dc, t * P:(t + 1) * P],
                                    g.kq[:, dc, :], start=dc == 0, stop=dc == 1)
        ins.then_inc(b6_filled, 1)

    def copy(v, n, k, second, use):
        idx = uses_at(k, second)
        if idx is None:
            return
        bank = g.ps[:, 6, :]
        v.wait_ge(b6_filled, use(idx) + 1)
        if idx < 2:
            v.tensor_copy(ocT[:, idx, :], bank).then_inc(b6_copied, 1)
        elif idx in (2, 3):
            two = slice(2 * (idx - 2), 2 * (idx - 2) + 2)
            v.tensor_tensor(x1[:, two, :].rearrange("p t d -> p (t d)"),
                            xt[:, two, :].rearrange("p t d -> p (t d)"), bank, ALU.add).then_inc(b6_copied, 1)
            v.wait_ge(b6_copied, use(idx) + 2)
        elif idx == 4:
            v.tensor_copy(xqT[:, :, :], psb.rearrange("p (c n) -> p c n", c=2)).then_inc(b6_copied, 1)
        else:
            two = slice(2 * (idx - 5), 2 * (idx - 5) + 2)
            v.tensor_scalar(yb[:, two, :].rearrange("p t d -> p (t d)"), bank, g.S_OUT, None,
                            ALU.mult).then_inc(b6_copied, 1)
            v.wait_ge(b6_copied, use(idx) + 2)
            v.sem_inc(yb2_rdy, 1)

    def scalar(act, n, k):
        if k == 9:
            act.wait_ge(oss_rdy, n + 1)
            act.activation(lnss[:, :, :], ss[:, :, :], ACT.Ln).then_inc(steps_a, 1)
            act.wait_ge(steps_a, 2 * n + 1)
            act.activation(y[:, :, :], lnss[:, :, :], ACT.Exp, scale=-0.5).then_inc(oy_rdy, 1)
        if k == 18:
            act.wait_ge(var_rdy, n + 1)
            act.activation(lnv[:, :], veps[:, :], ACT.Ln).then_inc(steps_a, 1)
            act.wait_ge(steps_a, 2 * n + 2)
            act.activation(rstd[:, :], lnv[:, :], ACT.Exp, scale=-0.5).then_inc(rs0_rdy, 1)

    def vector(v, n, k):
        step = Steps(v, steps_v, PER * n + steps_before.get(k, 0))
        if k == 5:
            v.wait_ge(f_in, 80 * (n + 1))
            step(v.reciprocal(rs[:, :, :, :], o_in[:, :, :, :, DH]))
            v.sem_inc(rs_rdy, 1)
        if k == 8:
            v.wait_ge(osq_rdy, n + 1)
            step(v.tensor_reduce(ss[:, :, :], sq[:, :, :, :], AX.X, ALU.add))
            v.tensor_scalar(ss[:, :, :], ss[:, :, :], EPS * EPS, None, ALU.max).then_inc(oss_rdy, 1)
        if k == 11:
            v.wait_ge(oss_rdy, n + 1)
            v.wait_ge(oy_rdy, n + 1)
            step(v.tensor_tensor(y2[:, :, :], y[:, :, :], y[:, :, :], ALU.mult))
            step(v.tensor_tensor(y2[:, :, :], y2[:, :, :], ss[:, :, :], ALU.mult))
            step(v.tensor_scalar(y2[:, :, :], y2[:, :, :], -0.5, 1.5, ALU.mult, ALU.add))
            step(v.tensor_tensor(y[:, :, :], y[:, :, :], y2[:, :, :], ALU.mult))
            v.tensor_scalar(y[:, :, :], y[:, :, :], g.ZS, 1.0, ALU.mult, ALU.min).then_inc(oy2_rdy, 1)
        if k == 17:
            for t in range(GT):
                step.mark(v.bn_stats(stats[:, t, :], x1[:, t, :]))
            step.settle()
            hold(v, passed_v)
            for t in range(GT):
                step.mark(v.bn_aggr(mv[:, t, :], stats[:, t, :]))
            step.settle()
            v.tensor_scalar(veps[:, :], mv[:, :, 1], EPS, None, ALU.add).then_inc(var_rdy, 1)
        if k == 20:
            v.wait_ge(var_rdy, n + 1)
            v.wait_ge(rs0_rdy, n + 1)
            step(v.tensor_tensor(rtmp[:, :], rstd[:, :], rstd[:, :], ALU.mult))
            step(v.tensor_tensor(rtmp[:, :], rtmp[:, :], veps[:, :], ALU.mult))
            step(v.tensor_scalar(rtmp[:, :], rtmp[:, :], -0.5, 1.5, ALU.mult, ALU.add))
            step(v.tensor_tensor(rstd[:, :], rstd[:, :], rtmp[:, :], ALU.mult))
            for t in range(GT):
                ins = v.tensor_scalar(xb[:, t, :], x1[:, t, :], mv[:, t, 0:1], rstd[:, t:t + 1],
                                      ALU.subtract, ALU.mult)
            step(ins)
            step(v.tensor_scalar(vf, xb[:, :, :], g.INV_SIN, None, ALU.mult))
            v.wait_ge(oc_rdy, n + 1)
            step(v.tensor_scalar(sp1.bitcast(I32), vf.bitcast(I32), 0x7F800000, None, ALU.bitwise_and))
            v.tensor_scalar(sp1, sp1, 2.0 ** -6, 1.5 * 2.0 ** 20, ALU.max, ALU.mult).then_inc(sp_rdy, 1)
        if k == 23:
            step(v.tensor_reduce(rmax[:, :], vf, AX.X, ALU.max, apply_absolute_value=True))
            step(v.tensor_scalar(rmax[:, :], rmax[:, :], FLT_MAX / 464.001, 0.0, ALU.mult, ALU.mult))
        if k == 30:
            v.wait_ge(yb2_rdy, 3 * n + 3)
            v.wait_ge(res_out, 16 * (n + 1))
            for t in range(GT):
                ins = v.scalar_tensor_tensor(res[:, t, :], yb2[:, t, :], rmax[:, t:t + 1], x1[:, t, :],
                                             ALU.add, ALU.add)
            ins.then_inc(res_rdy, 1)
        assert step.n == {5: 1, 8: 1, 11: 4, 17: 8, 20: 7, 23: 2}.get(k, 0), (k, step.n)

    p = Shared()
    p.start_vector, p.sync, p.gpsimd, p.tensor, p.copy, p.scalar, p.vector, p.uses_at, p.stored = (
        start_vector, sync, gpsimd, tensor, copy, scalar, vector, uses_at, res_out)
    return p


def emit_layer(nc, g):
    with ExitStack() as ctx:
        def sb(name, shape, dt=F32):
            return _sb(nc, ctx, name, shape, dt)
        qS = sb("qS", [P, 2, HPG, S], BF16)
        kS = sb("kS", [P, 2, HPG, S], BF16)
        vt = sb("vt", [P, 2, KT, HPG, VW])
        opens = sb("opens", [1, HG], I32)
        rqb = sb("rqb", [P, HPG, GTOK])
        U = sb("U", [P, RING, HPG, GTOK])
        OTs = sb("OTs", [P, 2, GTOK])
        Os = sb("Os", [P, 2, GT, HPG, OW])
        low = sb("low", [P, 2, HPG, GTOK], BF16)
        count = sb("count", [P, OW], BF16)
        past = sb("past", [P, 1])
        cm = sb("cm", [P, SLOTS // KT])
        red, ones_c = sb("red", [P, 2]), sb("ones_c", [P, 1])
        names = ("d_rdy", "clamped", "past_rdy", "low_rdy", "counted", "ln_done", "exp_done", "pv_done", "bc_rdy", "rqb_rdy", "m_rdy",
                 "ot_free", "max_steps", "zeroed", "opens", "b6_filled", "b6_copied", "b7_filled", "b7_copied")
        (d_rdy, clamped, past_rdy, low_rdy, counted, ln_done, exp_done, pv_done, bc_rdy, rqb_rdy, m_rdy, ot_free,
         max_steps, zeroed, open_rdy, b6_filled, b6_copied, b7_filled, b7_copied) = (
            _sem(nc, ctx, "at_" + n) for n in names)
        passed_v, passed_sp, passed_pe, passed_act = (
            _sem(nc, ctx, "at_passed_" + n) for n in ("v", "sp", "pe", "act"))
        in_rdy = [_sem(nc, ctx, f"at_in{u}") for u in range(2)]
        o_out = [_sem(nc, ctx, f"at_o_out{h}") for h in range(2)]
        IN_UNIT = 16 * (2 * len(Q_PARTS) + 1)
        project = project_stage(nc, ctx, g, b7_filled, b7_copied, opens, open_rdy)
        finish = finish_stage(nc, ctx, g, "fi_", b6_filled, b6_copied)

        order6 = sorted([(5 + KT * x, 0, ("sums", x)) for x in range(SLOTS // KT)] +
                        [(FINISH_AT[u] + k, second, ("finish", u, finish.uses_at(k, second))) for u in range(2)
                         for k in range(FINISH_SLOTS) for second in range(2) if finish.uses_at(k, second) is not None],
                        key=lambda entry: (entry[0], entry[1], entry[2][0] != "sums"))
        place6 = {key: n for n, (_, _, key) in enumerate(order6)}
        first6 = {key: n for n, key in enumerate([key for _, _, key in order6 if key[0] == "sums" and key[1] > 0])}
        MISSING6 = len(order6) - len(first6)

        def use6(i, key, first):
            return first6[key] if first else len(order6) * i - MISSING6 + place6[key]

        def finish_use(i, u):
            return lambda idx: use6(i, ("finish", u, idx), False)

        def last_use(u):
            return lambda idx: use6(B, ("sums", 0), False) + 1 + 7 * u + idx

        def split(q):
            return (q // QPJ) % HG, (q % QPJ) // KT, q % KT

        def run(body, eng):
            body(0, first=True)
            with eng.Fori(1, B - 1) as i:
                body(i)
            body(B - 1, last=True)

        def project_slots(s):
            return [(u, s - PROJECT_AT[u]) for u in range(2) if 0 <= s - PROJECT_AT[u] < PROJECT_SLOTS]

        def finish_slots(s):
            return [(u, s - FINISH_AT[u]) for u in range(2) if 0 <= s - FINISH_AT[u] < FINISH_SLOTS]

        with nc.Block() as block:
            @block.sync
            def _(sp):
                def load(i, u4):
                    j, u = HG * i + u4, u4 % 2
                    for buf, d, order in ((qS, g.qT_d, Q_PARTS), (kS, g.kT_d, K_PARTS)):
                        rows = d.rearrange("j c (h r) s -> j c r h s", h=HPG)
                        for n, part in enumerate(order):
                            sp.dma_start(buf[n * RU:(n + 1) * RU, u], rows[bass.ds(j, 1), part].rearrange(
                                "a r h s -> (a r) h s")).then_inc(in_rdy[u], 16)
                    sp.dma_start(vt[:, u].rearrange("p k h w -> p k (h w)"),
                                 g.v_d[bass.ds(j, 1)].rearrange("a (k p) f -> p (a k) f", p=P)).then_inc(in_rdy[u], 16)

                def load_next(i, u4):
                    j = HG * i + u4
                    sp.wait_ge(pv_done, QPJ * j + RING)
                    hold(sp, passed_sp)
                    sp.wait_ge(ln_done, QPJ * j + 1)
                    hold(sp, passed_sp)
                    if u4 == HG - 1:
                        wait_operands(i + 2)
                        load(i + 1, 0)
                    else:
                        load(i, u4 + 1)

                def wait_operands(batches):
                    sp.wait_ge(project.T_out, 192 * batches + 48)
                    hold(sp, passed_sp)
                    sp.wait_ge(project.v_out, 128 * batches + 64)
                    hold(sp, passed_sp)

                def store(i, x, first=False):
                    qh = (x + 1) % 2
                    j = HG * i + (x + 1) // 2 - 1
                    sp.wait_ge(b6_copied, use6(i, ("sums", x), first) + 2)
                    hold(sp, passed_sp)
                    sp.dma_start(g.o_d[bass.ds(j, 1), qh * GTOK:(qh + 1) * GTOK, :].rearrange(
                        "a (t p) f -> p (a t) f", p=P), Os[:, qh].rearrange("p t h w -> p t (h w)")).then_inc(o_out[qh], 16)

                def body(i, first=False, last=False):
                    for s in range(SLOTS):
                        if s % QPJ == 4 and s < SLOTS - QPJ:
                            load_next(i, s // QPJ)
                        if s % KT == 6 and (s > KT or not first):
                            store(i, s // KT, first)
                        if not first:
                            for u, k in finish_slots(s):
                                finish.sync(sp, 2 * i - 2 + u, i - 1, u, k, o_out)
                        if not last:
                            for u, k in project_slots(s):
                                project.sync(sp, i + 1, u, k)
                        if s == SLOTS - 4 and not last:
                            load_next(i, HG - 1)

                for s in range(PROJECT_AT[1] + PROJECT_SLOTS):
                    for u, k in project_slots(s):
                        project.sync(sp, 0, u, k)
                wait_operands(1)
                load(0, 0)
                run(body, sp)
                store(B, 0)
                for u in range(2):
                    for k in range(FINISH_SLOTS):
                        finish.sync(sp, 2 * B - 2 + u, B - 1, u, k, o_out)
                for qh in range(QH):
                    sp.wait_ge(o_out[qh], 16 * NJ)
                for sem, count in project.stored:
                    sp.wait_ge(sem, count)
                sp.wait_ge(finish.stored, 16 * NG + 16)

            @block.gpsimd
            def _(pool):
                def body(i, first=False, last=False):
                    for s in range(SLOTS):
                        if not first:
                            for u, k in finish_slots(s):
                                finish.gpsimd(pool, 2 * i - 2 + u, k)
                        if not last:
                            for u, k in project_slots(s):
                                project.gpsimd(pool, i + 1, u, k)
                for s in range(PROJECT_AT[1] + PROJECT_SLOTS):
                    for u, k in project_slots(s):
                        project.gpsimd(pool, 0, u, k)
                run(body, pool)
                for u in range(2):
                    for k in range(FINISH_SLOTS):
                        finish.gpsimd(pool, 2 * B - 2 + u, k)

            @block.tensor
            def _(pe):
                pe.sem_inc(pv_done, RING)
                pe.wait_ge(zeroed, 3)

                def distances(i, s, pair, is_open):
                    u, qh, kt = split(s)
                    n = SLOTS * i + s
                    if is_open and s % QPJ > 0:
                        pe.wait_ge(clamped, 2 * n + pair)
                    else:
                        pe.wait_ge(ln_done, n + 1)
                    for h in (2 * pair, 2 * pair + 1):
                        ins = pe.matmul(g.ps[:, h, :], kS[0:RS, u % 2, h, kt * P:(kt + 1) * P],
                                        qS[0:RS, u % 2, h, qh * GTOK:(qh + 1) * GTOK], start=True, stop=True)
                    ins.then_inc(d_rdy, 1)

                def values(i, q):
                    u, qh, kt = split(q)
                    n = SLOTS * i + q
                    pe.wait_ge(exp_done, n + 1)
                    if kt == 0:
                        pe.wait_ge(ot_free, (SLOTS // KT) * i + q // KT + 1)
                    for h in range(HPG):
                        ins = pe.matmul(g.ps[32 * h:32 * h + OW, 4 + qh, :], vt[:, u % 2, kt, h, 0:OW],
                                        U[:, q % RING, h, :], start=kt == 0, stop=False)
                    ins.then_inc(pv_done, 1)

                def count_low(i, q):
                    u, qh, kt = split(q)
                    pe.wait_ge(low_rdy, SLOTS * i + q + RING + 1)
                    for h in range(HPG):
                        ins = pe.matmul(g.ps[32 * h:32 * h + OW, 4 + qh, :], count[:, :], low[:, q % 2, h, :],
                                        start=False, stop=kt == KT - 1)
                    ins.then_inc(counted, 1)

                def to_token_rows(i, x, first=False):
                    pe.wait_ge(ot_free, (SLOTS // KT) * i + x + 2)
                    pe.wait_ge(b6_copied, use6(i, ("sums", x), first) + 1)
                    for t in range(GT):
                        ins = pe.transpose(g.ps[:, 6, t * P:(t + 1) * P], OTs[:, (x + 1) % 2, t * P:(t + 1) * P], g.ident[:, :])
                    ins.then_inc(b6_filled, 1)

                def spread_rq(i, u, qh, free):
                    n = HPG * (QH * (HG * i + u) + qh)
                    pe.wait_ge(b6_copied, free)
                    for h in range(HPG):
                        pe.wait_ge(rqb_rdy, n + h + 1)
                        pe.matmul(g.ps[:, 6, :], g.sel[0:RS, :], qS[0:RS, u % 2, h, qh * GTOK:(qh + 1) * GTOK],
                                  start=True, stop=True).then_inc(bc_rdy, 1)
                    pe.wait_ge(rqb_rdy, n + HPG + 1)

                def uses_before(i, s, first):
                    before = [key for at, _, key in order6 if at < s and (not first or key in first6)]
                    if before:
                        return use6(i, before[-1], first) + 2
                    return 1 if first else use6(i, order6[0][2], False) + 1

                def unit(i, u4, is_open, first, last):
                    if not is_open:
                        pe.sem_inc(bc_rdy, QH * HPG)
                    for s in range(QPJ * u4, QPJ * (u4 + 1)):
                        if is_open and s % KT == 0:
                            spread_rq(i, u4, (s % QPJ) // KT, uses_before(i, s, first))
                        distances(i, s, 0, is_open)
                        distances(i, s, 1, is_open)
                        later_uses(i, s, 0, first, last)
                        if s >= 3 or not first:
                            values(i, s - 3)
                        later_uses(i, s, 1, first, last)
                        if s >= 4 or not first:
                            count_low(i, s - 4)

                def body(i, first=False, last=False):
                    for u4 in range(HG):
                        pe.wait_ge(in_rdy[u4 % 2], IN_UNIT * (2 * i + u4 // 2 + 1))
                        hold(pe, passed_pe)
                        pe.wait_ge(open_rdy, i + 1)
                        hold(pe, passed_pe)
                        is_open = pe.value_load(opens[0:1, u4:u4 + 1], min_val=0, max_val=1)
                        with pe.If(is_open > 0):
                            unit(i, u4, True, first, last)
                        with pe.Else():
                            unit(i, u4, False, first, last)
                    if last:
                        for q in range(SLOTS - 4, SLOTS):
                            if q > SLOTS - 4:
                                values(i, q)
                            count_low(i, q)

                def later_uses(i, s, second, first, last):
                    if s % KT == 5 and not second and (s > KT or not first):
                        to_token_rows(i, s // KT, first)
                    if not first:
                        for u, k in finish_slots(s):
                            finish.tensor(pe, 2 * i - 2 + u, k, second, finish_use(i, u))
                    if not last:
                        for u, k in project_slots(s):
                            project.tensor(pe, i + 1, u, k, second)

                for s in range(PROJECT_AT[1] + PROJECT_SLOTS):
                    for u, k in project_slots(s):
                        for second in range(2):
                            project.tensor(pe, 0, u, k, second)
                run(body, pe)
                to_token_rows(B, 0)
                for u in range(2):
                    for k in range(FINISH_SLOTS):
                        for second in range(2):
                            finish.tensor(pe, 2 * B - 2 + u, k, second, last_use(u))
                pe.wait_ge(max_steps, 2 * B + 5)
                pe.matmul(g.ps[0:1, 7, 0:1], red[:, 0:1], ones_c[:, :], start=True, stop=True).then_inc(bc_rdy, 1)

            @block.scalar
            def _(act):
                act.preload_act_table_set(ACT_SET)

                def log(i, s, is_open):
                    n = SLOTS * i + s
                    if is_open:
                        act.wait_ge(clamped, 2 * n + 3)
                        act.activation(U[:, s % RING], U[:, s % RING], ACT.Ln, scale=-2.0, bias=1.0).then_inc(ln_done, 1)
                    else:
                        act.wait_ge(d_rdy, 2 * n + 2)
                        act.wait_ge(pv_done, n + 1)
                        act.wait_ge(low_rdy, n + 1)
                        act.activation(U[:, s % RING], g.ps[:, 0:HPG, :], ACT.Ln, scale=-2.0 / EPS,
                                       bias=1.0).then_inc(ln_done, 1)

                def power(i, q):
                    n = SLOTS * i + q
                    act.wait_ge(ln_done, n + 2)
                    act.activation(U[:, q % RING], U[:, q % RING], ACT.Exp, scale=g.NEGB).then_inc(exp_done, 1)

                def unit(i, u4, is_open, first, last):
                    for s in range(QPJ * u4, QPJ * (u4 + 1)):
                        log(i, s, is_open)
                        if s >= 1 or not first:
                            power(i, s - 1)
                        if not first:
                            for u, k in finish_slots(s):
                                finish.scalar(act, 2 * i - 2 + u, k)
                        if not last:
                            for u, k in project_slots(s):
                                project.scalar(act, i + 1, u, k)

                def body(i, first=False, last=False):
                    act.wait_ge(open_rdy, i + 1)
                    hold(act, passed_act)
                    for u4 in range(HG):
                        is_open = act.value_load(opens[0:1, u4:u4 + 1], min_val=0, max_val=1)
                        with act.If(is_open > 0):
                            unit(i, u4, True, first, last)
                        with act.Else():
                            unit(i, u4, False, first, last)
                    if last:
                        power(i, SLOTS - 1)
                act.activation(past[:, :], g.NEGB, ACT.Exp, scale=math.log(2.0 * U_EXACT + 1.0)).then_inc(past_rdy, 1)
                for s in range(PROJECT_AT[1] + PROJECT_SLOTS):
                    for u, k in project_slots(s):
                        project.scalar(act, 0, u, k)
                run(body, act)
                for u in range(2):
                    for k in range(FINISH_SLOTS):
                        finish.scalar(act, 2 * B - 2 + u, k)

            @block.vector
            def _(v):
                v.sem_inc(ln_done, 1)
                v.sem_inc(clamped, 1)
                v.sem_inc(low_rdy, RING)
                v.sem_inc(counted, 2)
                v.sem_inc(ot_free, 2)
                v.sem_inc(rqb_rdy, 1)
                v.sem_inc(b6_copied, 1)
                v.memset(ones_c[:, :], 1.0)
                v.memset(count[:, OW - 1:OW], 1.0).then_inc(zeroed, 1)
                v.memset(count[:, 0:OW - 1], 0.0).then_inc(zeroed, 1)
                v.memset(g.ps[:, 4:6, :], 0.0).then_inc(zeroed, 1)
                v.wait_ge(zeroed, 3)
                v.wait_ge(past_rdy, 1)
                project.start_vector(v)
                finish.start_vector(v)

                def clamp(i, s, pair):
                    u, qh, kt = split(s)
                    n = SLOTS * i + s
                    if pair == 0:
                        v.wait_ge(pv_done, n + 1)
                        v.wait_ge(low_rdy, n + 1)
                        v.wait_ge(in_rdy[u % 2], IN_UNIT * (2 * i + u // 2 + 1))
                        hold(v, passed_v)
                        for h in range(HPG):
                            ins = v.tensor_scalar(U[:, s % RING, h, :], rqb[:, h, :], vt[:, u % 2, kt, h, DH + 2:DH + 3],
                                                  1.0 / EPS, ALU.mult, ALU.min)
                        ins.then_inc(m_rdy, 1)
                    v.wait_ge(m_rdy, n + 1)
                    v.wait_ge(d_rdy, 2 * n + pair + 1)
                    hs = slice(2 * pair, 2 * pair + 2)
                    v.tensor_tensor(U[:, s % RING, hs, :], U[:, s % RING, hs, :], g.ps[:, hs, :],
                                    ALU.mult).then_inc(clamped, 1)

                def find_low(i, q):
                    n = SLOTS * i + q
                    v.wait_ge(exp_done, n + 1)
                    v.wait_ge(counted, n + 1)
                    v.tensor_scalar(low[:, q % 2], U[:, q % RING], past[:, :], None, ALU.is_gt).then_inc(low_rdy, 1)

                def copy_rq(i, u, qh):
                    n = HPG * (QH * (HG * i + u) + qh)
                    v.wait_ge(clamped, 2 * QPJ * (HG * i + u) + 2 * KT * qh + 1)
                    hold(v, passed_v)
                    for h in range(HPG):
                        v.wait_ge(bc_rdy, n + h + 1)
                        v.tensor_copy(rqb[:, h, :], g.ps[:, 6, :]).then_inc(rqb_rdy, 1)
                    v.wait_ge(rqb_rdy, n + HPG + 1)

                def copy_sums(i, x):
                    v.wait_ge(counted, SLOTS * i + KT * x + 2)
                    v.tensor_copy(OTs[:, (x + 1) % 2, :], g.ps[:, 4 + (x + 1) % 2, :]).then_inc(ot_free, 1)

                def copy_rows(i, x, first=False):
                    v.wait_ge(b6_filled, use6(i, ("sums", x), first) + 1)
                    qh = (x + 1) % 2
                    if not (first and x < 3):
                        v.wait_ge(o_out[qh], 16 * (HG * i + (x + 1) // 2 - 1))
                    v.tensor_copy(Os[:, qh], g.ps[:, 6, :].rearrange("p (t h r) -> p t h r", t=GT, h=HPG)[:, :, :, 0:OW])\
                     .then_inc(b6_copied, 1)
                    v.wait_ge(b6_copied, use6(i, ("sums", x), first) + 2)
                    v.tensor_reduce(cm[:, x:x + 1], Os[:, qh, :, :, OW - 1], AX.XY, ALU.max)

                def copies(i, s, second, first, last):
                    if s % KT == 5 and not second and (s > KT or not first):
                        copy_rows(i, s // KT, first)
                    if not first:
                        for u, k in finish_slots(s):
                            finish.copy(v, 2 * i - 2 + u, k, second, finish_use(i, u))
                    if not last:
                        for u, k in project_slots(s):
                            project.copy(v, i + 1, u, k, second)

                def unit(i, u4, is_open, first, last):
                    for s in range(QPJ * u4, QPJ * (u4 + 1)):
                        if is_open:
                            if s % KT == 0:
                                copy_rq(i, u4, (s % QPJ) // KT)
                            clamp(i, s, 0)
                            clamp(i, s, 1)
                        copies(i, s, 0, first, last)
                        if s >= 3 or not first:
                            find_low(i, s - 3)
                        copies(i, s, 1, first, last)
                        if s % KT == 4 and (s > KT or not first):
                            copy_sums(i, s // KT)
                        if not first:
                            for u, k in finish_slots(s):
                                finish.vector(v, 2 * i - 2 + u, k)
                        if not last:
                            for u, k in project_slots(s):
                                project.vector(v, i + 1, u, k)

                def body(i, first=False, last=False):
                    v.wait_ge(open_rdy, i + 1)
                    hold(v, passed_v)
                    for u4 in range(HG):
                        is_open = v.value_load(opens[0:1, u4:u4 + 1], min_val=0, max_val=1)
                        with v.If(is_open > 0):
                            unit(i, u4, True, first, last)
                        with v.Else():
                            v.sem_inc(rqb_rdy, QH * HPG)
                            v.sem_inc(m_rdy, QPJ)
                            v.wait_ge(clamped, 2 * QPJ * (HG * i + u4) + 1)
                            hold(v, passed_v)
                            v.sem_inc(clamped, 2 * QPJ)
                            unit(i, u4, False, first, last)
                    v.tensor_reduce(red[:, 0:1], cm[:, :], AX.X, ALU.max).then_inc(max_steps, 1)
                    v.wait_ge(max_steps, 2 * i + 2)
                    v.tensor_tensor(g.run_max[:, :], g.run_max[:, :], red[:, 0:1], ALU.max).then_inc(max_steps, 1)
                    v.wait_ge(max_steps, 2 * i + 3)
                for s in range(PROJECT_AT[1] + PROJECT_SLOTS):
                    for u, k in project_slots(s):
                        for second in range(2):
                            project.copy(v, 0, u, k, second)
                        project.vector(v, 0, u, k)
                v.memset(cm[:, :], 0.0).then_inc(max_steps, 1)
                v.wait_ge(max_steps, 1)
                run(body, v)
                for q in range(SLOTS - 3, SLOTS):
                    find_low(B - 1, q)
                copy_sums(B, 0)
                copy_rows(B, 0)
                for u in range(2):
                    for k in range(FINISH_SLOTS):
                        for second in range(2):
                            finish.copy(v, 2 * B - 2 + u, k, second, last_use(u))
                        finish.vector(v, 2 * B - 2 + u, k)
                v.tensor_tensor(g.run_max[:, :], g.run_max[:, :], cm[:, 0:1], ALU.max).then_inc(max_steps, 1)
                v.tensor_scalar(red[:, 1:2], g.NEGB, -EXPONENT_MAX / THETA_MAX, None, ALU.is_lt).then_inc(max_steps, 1)
                v.wait_ge(max_steps, 2 * B + 3)
                v.tensor_scalar(red[:, 0:1], g.run_max[:, :], 0.5, None, ALU.is_gt).then_inc(max_steps, 1)
                v.wait_ge(max_steps, 2 * B + 4)
                v.tensor_tensor(red[:, 0:1], red[:, 0:1], red[:, 1:2], ALU.add).then_inc(max_steps, 1)
                v.wait_ge(bc_rdy, QH * HPG * NJ + 1)
                v.tensor_copy(g.flag[:, :], g.ps[0:1, 7, 0:1]).then_inc(max_steps, 1)


def emit_general(nc, g):
    with ExitStack() as ctx:
        def sb(name, shape, dt=F32):
            return _sb(nc, ctx, name, shape, dt)
        Qs, Ks = sb("Qs", [P, P], BF16), sb("Ks", [P, S], BF16)
        Vs = sb("Vs", [P, KT, VW])
        ones_s, diag = sb("ones_s", [P, P]), sb("diag", [P, KT, P])
        rqc, least, shift = sb("rqc", [P, 1]), sb("least", [P, 1]), sb("shift", [P, 1])
        X, Z, T = sb("X", [P, S]), sb("Z", [P, S]), sb("T", [P, S])
        WT = sb("WT", [P, KT, P])
        Og = sb("Og", [P, OW])
        gin, p_rdy, v_rdy, a_rdy, gout = (_sem(nc, ctx, "ge_" + n) for n in ("in", "p_rdy", "v_rdy", "a_rdy", "out"))
        passed_sp = _sem(nc, ctx, "ge_passed_sp")
        gv, ga, ga_ones = (_sem(nc, ctx, "ge_" + n) for n in ("v_steps", "a_steps", "ones"))
        GIN = 16 * (2 * len(Q_PARTS) + 1)

        def steps(eng, body, stored=None):
            needed = eng.value_load(g.flag[0:1, 0:1], min_val=0, max_val=2 * P)
            with eng.If(needed > 0):
                with eng.Fori(0, NJ) as j:
                    with eng.Fori(0, HPG) as h:
                        with eng.Fori(0, KT) as t:
                            body(j, h, t, (j * HPG + h) * KT + t)
                if stored is not None:
                    eng.wait_ge(stored, 16 * (NJ * HPG * KT + 1))

        with nc.Block() as block:
            @block.sync
            def _(sp):
                def body(j, h, t, n):
                    sp.wait_ge(gout, 16 * (n + 1))
                    hold(sp, passed_sp)
                    for c, part in enumerate(Q_PARTS):
                        sp.dma_start(Qs[c * RU:(c + 1) * RU, :], g.qT_d[bass.ds(j, 1), part, bass.ds(h * RU, RU),
                                                                     bass.ds(t * P, P)].rearrange(
                            "a r s -> (a r) s")).then_inc(gin, 16)
                    for c, part in enumerate(K_PARTS):
                        sp.dma_start(Ks[c * RU:(c + 1) * RU, :], g.kT_d[bass.ds(j, 1), part, bass.ds(h * RU, RU),
                                                                     :].rearrange(
                            "a r s -> (a r) s")).then_inc(gin, 16)
                    sp.dma_start(Vs[:, :, :], g.v_d[bass.ds(j, 1), :, bass.ds(h * VW, VW)].rearrange(
                        "a (k p) w -> p (a k) w", p=P)).then_inc(gin, 16)
                    sp.wait_ge(v_rdy, 8 * n + 8)
                    hold(sp, passed_sp)
                    sp.dma_start(g.o_d[bass.ds(j, 1), bass.ds(t * P, P), bass.ds(h * OW, OW)].rearrange(
                        "a p w -> (a p) w"), Og[:, :]).then_inc(gout, 16)
                sp.sem_inc(gout, 16)
                steps(sp, body, gout)

            @block.tensor
            def _(pe):
                def body(j, h, t, n):
                    pe.wait_ge(gin, GIN * (n + 1))
                    pe.wait_ge(v_rdy, 8 * n + 1)
                    for half in range(2):
                        ks = slice(half * 512, (half + 1) * 512)
                        pe.matmul(g.ps[:, half, :], Qs[0:RS, :], Ks[0:RS, ks], start=True, stop=True)
                        pe.matmul(g.ps[:, 2 + half, :], ones_s[:, :],
                                  diag[:, 4 * half:4 * half + 4, :].rearrange("p k q -> p (k q)"),
                                  start=True, stop=True)
                    pe.matmul(g.ps[:, 4, 0:1], Qs[0:RS, :], g.sel[0:RS, 0:1], start=True, stop=True).then_inc(p_rdy, 1)
                    pe.wait_ge(a_rdy, 3 * n + 3)
                    for k in range(KT):
                        ins = pe.transpose(g.ps[:, 5 + k // 4, (k % 4) * P:(k % 4 + 1) * P], Z[:, k * P:(k + 1) * P],
                                           g.ident[:, :])
                    ins.then_inc(p_rdy, 1)
                    pe.wait_ge(v_rdy, 8 * n + 7)
                    for k in range(KT):
                        ins = pe.matmul(g.ps[:, 7, 0:OW], WT[:, k, :], Vs[:, k, 0:OW], start=k == 0, stop=k == KT - 1)
                    ins.then_inc(p_rdy, 1)
                steps(pe, body)

            @block.scalar
            def _(act):
                act.preload_act_table_set(ACT_SET)

                def body(j, h, t, n):
                    act.wait_ge(v_rdy, 8 * n + 4)
                    act.activation(T[:, :], Z[:, :], ACT.Ln).then_inc(ga, 1)
                    act.wait_ge(ga, n + 1)
                    act.activation(Z[:, :], T[:, :], ACT.Exp, scale=0.5).then_inc(a_rdy, 1)
                    act.wait_ge(v_rdy, 8 * n + 5)
                    act.activation(X[:, :], T[:, :], ACT.Ln).then_inc(a_rdy, 1)
                    act.wait_ge(v_rdy, 8 * n + 6)
                    act.wait_ge(a_rdy, 3 * n + 2)
                    act.activation(Z[:, :], X[:, :], ACT.Exp, scale=g.NEGB, bias=shift[:, :]).then_inc(a_rdy, 1)
                steps(act, body)

            @block.vector
            def _(v):
                v.memset(ones_s[:, :], 1.0).then_inc(ga_ones, 1)
                v.wait_ge(ga_ones, 1)

                def body(j, h, t, n):
                    step = Steps(v, gv, 6 * n)
                    v.wait_ge(gin, GIN * (n + 1))
                    for k in range(KT):
                        ins = v.tensor_scalar(diag[:, k, :], g.ident[:, :], Vs[:, k, DH + 2:DH + 3], None, ALU.mult)
                    ins.then_inc(v_rdy, 1)
                    v.wait_ge(p_rdy, 3 * n + 1)
                    v.tensor_copy(rqc[:, :], g.ps[:, 4, 0:1]).then_inc(v_rdy, 1)
                    v.wait_ge(v_rdy, 8 * n + 2)
                    step(v.tensor_scalar(T[:, :], g.ps[:, 2:4, :].rearrange("p a k -> p (a k)"), rqc[:, :], 1.0 / EPS,
                                         ALU.mult, ALU.min))
                    step(v.tensor_tensor(T[:, :], T[:, :], g.ps[:, 0:2, :].rearrange("p a k -> p (a k)"), ALU.mult))
                    step(v.tensor_scalar(X[:, :], T[:, :], -2.0, 1.0, ALU.mult, ALU.add))
                    v.tensor_scalar(X[:, :], X[:, :], 1.0 + EPS, None, ALU.max).then_inc(v_rdy, 1)
                    v.wait_ge(v_rdy, 8 * n + 3)
                    step(v.tensor_scalar(T[:, :], X[:, :], -1.0, None, ALU.add))
                    v.scalar_tensor_tensor(Z[:, :], X[:, :], 1.0, T[:, :], ALU.add, ALU.mult).then_inc(v_rdy, 1)
                    v.wait_ge(a_rdy, 3 * n + 1)
                    v.tensor_tensor(T[:, :], X[:, :], Z[:, :], ALU.add).then_inc(v_rdy, 1)
                    v.wait_ge(a_rdy, 3 * n + 2)
                    step(v.tensor_reduce(least[:, :], X[:, :], AX.X, ALU.min))
                    step(v.tensor_scalar(shift[:, :], least[:, :], g.NEGB, -1.0, ALU.mult, ALU.mult))
                    v.sem_inc(v_rdy, 1)
                    v.wait_ge(p_rdy, 3 * n + 2)
                    v.tensor_copy(WT[:, :, :].rearrange("p k q -> p (k q)"),
                                  g.ps[:, 5:7, :].rearrange("p a k -> p (a k)")).then_inc(v_rdy, 1)
                    v.wait_ge(p_rdy, 3 * n + 3)
                    v.tensor_copy(Og[:, :], g.ps[:, 7, 0:OW]).then_inc(v_rdy, 1)
                steps(v, body)


def emit_finish_again(nc, g):
    with ExitStack() as ctx:
        b6_filled, b6_copied = (_sem(nc, ctx, "rf_" + n) for n in ("filled", "copied"))
        finish = finish_stage(nc, ctx, g, "rf_", b6_filled, b6_copied)

        def groups(eng, group):
            needed = eng.value_load(g.flag[0:1, 0:1], min_val=0, max_val=2 * P)
            with eng.If(needed > 0):
                with eng.Fori(0, B) as i:
                    for u in range(2):
                        for k in range(FINISH_SLOTS):
                            group(i, u, k, lambda idx: 14 * i + 7 * u + idx)
                if eng is nc.sync:
                    eng.wait_ge(finish.stored, 16 * NG + 16)

        with nc.Block() as block:
            @block.sync
            def _(sp):
                groups(sp, lambda i, u, k, use: finish.sync(sp, 2 * i + u, i, u, k, None))

            @block.gpsimd
            def _(pool):
                groups(pool, lambda i, u, k, use: finish.gpsimd(pool, 2 * i + u, k))

            @block.tensor
            def _(pe):
                def group(i, u, k, use):
                    for second in range(2):
                        finish.tensor(pe, 2 * i + u, k, second, use)
                groups(pe, group)

            @block.scalar
            def _(act):
                act.preload_act_table_set(ACT_SET)
                groups(act, lambda i, u, k, use: finish.scalar(act, 2 * i + u, k))

            @block.vector
            def _(v):
                v.sem_inc(b6_copied, 1)
                finish.start_vector(v)

                def group(i, u, k, use):
                    for second in range(2):
                        finish.copy(v, 2 * i + u, k, second, use)
                    finish.vector(v, 2 * i + u, k)
                groups(v, group)


def layer_kernel(nc, x, W_q, W_k, W_v, W_o, log_c, beta, attention_bias, ffn_w, input_scale, kernel_scale,
                 ffn_bias, out):
    assert tuple(x.shape) == (B, S, D) and (QH, GT) == (2, 4)
    g = Shared()
    g.W_q, g.W_k, g.W_v, g.W_o, g.log_c, g.beta, g.attention_bias = W_q, W_k, W_v, W_o, log_c, beta, attention_bias
    g.ffn_w, g.input_scale, g.kernel_scale, g.ffn_bias = ffn_w, input_scale, kernel_scale, ffn_bias
    g.x_g = x.rearrange("b (u t p) d -> (b u) p t d", t=GT, p=P)
    g.out_g = out.rearrange("b (u t p) d -> (b u) p t d", t=GT, p=P)
    g.qT_d = nc.dram_tensor("qT_scratch", [NJ, 3, TR, S], BF16, kind="Internal").ap()
    g.kT_d = nc.dram_tensor("kT_scratch", [NJ, 3, TR, S], BF16, kind="Internal").ap()
    g.v_d = nc.dram_tensor("v_scratch", [NJ, S, HPG * VW], F32, kind="Internal").ap()
    g.o_d = nc.dram_tensor("o_scratch", [NJ, S, HPG * OW], F32, kind="Internal").ap()

    with ExitStack() as root:
        def sb(name, shape, dt=F32):
            return root.enter_context(nc.sbuf_tensor(name, shape, dt))

        g.ident = sb("ident", [P, P])
        g.ident_b = sb("ident_b", [P, P], BF16)
        g.sel = sb("sel", [P, P], BF16)
        g.wT = sb("wT", [P, 2, 3 * D])
        g.woT = sb("woT", [P, 2, D])
        g.kq = sb("kq", [P, 2, D], BF16)
        g.bias_b = sb("bias_b", [P, D], BF16)
        g.flag = sb("flag", [1, 1], I32)
        g.run_max = sb("run_max", [P, 1])
        g.ps = root.enter_context(nc.psum_tensor("ps", [P, 8, 512], F32))
        g.sc = sb("sc", [P, 16])
        (g.C_SP, g.C_BP, g.SQC, g.ISQC, g.NEGB, g.ZS, g.M2SC, g.EAB, g.INV_SIN, g.INV_SK, g.S_OUT) = (
            g.sc[:, k:k + 1] for k in range(11))
        emit_setup(nc, g)
        emit_layer(nc, g)
        emit_general(nc, g)
        emit_finish_again(nc, g)


_INS = ["L0_attn_x", "L0_attn_W_q", "L0_attn_W_k", "L0_attn_W_v", "L0_attn_W_o", "L0_attn_log_c", "L0_attn_beta",
        "L0_attn_attention_bias", "L0_ffn_kernel", "L0_ffn_input_scale", "L0_ffn_kernel_scale", "L0_ffn_bias"]


def kernel(**inputs):
    import numpy as _np
    import concourse.bacc as _bacc
    from concourse.bass_utils import run_bass_kernel_spmd as _run

    nc = _bacc.Bacc("TRN2", target_bir_lowering=False, num_devices=1)
    arrays, args = {}, []
    for name in _INS:
        a = _np.ascontiguousarray(inputs[name])
        if a.ndim == 0:
            a = a.reshape(1)
        arrays[f"in_{name}_dram"] = a
        args.append(nc.dram_tensor(f"in_{name}_dram", a.shape, mybir.dt.from_np(a.dtype), kind="ExternalInput").ap())
    shape = inputs["L0_attn_x"].shape
    args.append(nc.dram_tensor("out_0_dram", shape, F32, kind="ExternalOutput").ap())
    layer_kernel(nc, *args)
    r = _run(nc, [arrays], core_ids=[0])
    return r.results[0]["out_0_dram"]
```
